# Optimizing a Trainium2 kernel written in Bass

```python
import numpy as np
import jax
import jax.numpy as jnp

def _softmax(x, axis=-1):
    return jax.nn.softmax(x, axis=axis)

def _gelu(x):
    return jax.nn.gelu(x, approximate=True)

def _silu(x):
    return jax.nn.silu(x)

def _sigmoid(x):
    return jax.nn.sigmoid(x)

def _layernorm(x, axis=-1, eps=1e-05):
    m = jnp.mean(x, axis=axis, keepdims=True)
    v = jnp.var(x, axis=axis, keepdims=True)
    return (x - m) / jnp.sqrt(v + eps)

def _scatter_add(tgt, idx, src, axis=0):
    return tgt.at[idx].add(src)

def _segment_sum(src, seg, n):
    return jax.ops.segment_sum(src, seg, n)
kernel_name = 'mk_decoder_postln_d1_seqx_r8_c7bbd2'

def setup_inputs(seed: int=0):
    np.random.seed(seed)
    _w = jnp.asarray

    def _rec_inputs():
        import jax
        import jax.numpy as jnp
        _rk = jax.random.key(seed)
        x = -0.0003929 + 0.9999 * jax.random.normal(jax.random.fold_in(_rk, 1), (8, 256, 256), jnp.float32)
        _lenS = 256 - jax.random.randint(jax.random.fold_in(_rk, 7), (8,), 0, max(1, 256 // 4) + 1, jnp.int32)
        _lenS2 = 64 - jax.random.randint(jax.random.fold_in(_rk, 8), (8,), 0, max(1, 64 // 4) + 1, jnp.int32)
        _ctx_2048P = jax.random.normal(jax.random.fold_in(_rk, 11), (8, 16, 256), jnp.float32)
        _ctx_2048c = jax.random.dirichlet(jax.random.fold_in(_rk, 511), 0.3 * jnp.ones((16,), jnp.float32), (8, 64))
        _ctx_2048t = jnp.einsum('bsk,bkd->bsd', _ctx_2048c, _ctx_2048P)
        _ctx_2048t = _ctx_2048t * jax.lax.rsqrt(jnp.mean(jnp.square(_ctx_2048t)) + 1e-12) * 0.953939
        ctx_2048 = -1.39393e-06 + 0.999914 * (_ctx_2048t + 0.3 * jax.random.normal(jax.random.fold_in(_rk, 611), (8, 64, 256), jnp.float32))
        itok_BxS_0_1023 = jax.random.randint(jax.random.fold_in(_rk, 12), (8, 256), 0, 128, jnp.int32)
        return (x, ctx_2048, itok_BxS_0_1023)
    x, ctx_2048, itok_BxS_0_1023 = _rec_inputs()

    def _L0_attn_setup():
        import jax, jax.numpy as jnp
        import numpy as np
        import math
        N_HEADS, D_MODEL, D_HEAD = (16, 256, 128)
        BATCH, SEQ = (4, 256)
        ROPE_THETA = 10000.0

        def _rope_cos_sin(seq_len, head_dim, dtype=jnp.float32):
            inv_freq = 1.0 / ROPE_THETA ** (jnp.arange(0, head_dim, 2, dtype=jnp.float32) / head_dim)
            m = jnp.arange(seq_len, dtype=jnp.float32)
            freqs = jnp.outer(m, inv_freq)
            return (jnp.cos(freqs).astype(dtype), jnp.sin(freqs).astype(dtype))

        def _apply_rope(x, cos, sin):
            x1 = x[..., 0::2]
            x2 = x[..., 1::2]
            cos = cos[None, :, None, :]
            sin = sin[None, :, None, :]
            r1 = x1 * cos - x2 * sin
            r2 = x1 * sin + x2 * cos
            out = jnp.stack([r1, r2], axis=-1)
            return out.reshape(x.shape)
        key = jax.random.key(seed)
        ks = jax.random.split(key, 9)
        std = 0.02
        return {'normalized_resid_pre': jax.random.normal(ks[0], (BATCH, SEQ, D_MODEL), jnp.float32), 'W_Q': jax.random.normal(ks[1], (N_HEADS, D_MODEL, D_HEAD), jnp.float32) * std, 'b_Q': jnp.zeros((N_HEADS, D_HEAD), jnp.float32), 'W_K': jax.random.normal(ks[2], (N_HEADS, D_MODEL, D_HEAD), jnp.float32) * std, 'b_K': jnp.zeros((N_HEADS, D_HEAD), jnp.float32), 'W_V': jax.random.normal(ks[3], (N_HEADS, D_MODEL, D_HEAD), jnp.float32) * std, 'b_V': jnp.zeros((N_HEADS, D_HEAD), jnp.float32), 'W_O': jax.random.normal(ks[4], (N_HEADS, D_HEAD, D_MODEL), jnp.float32) * std, 'b_O': jnp.zeros((D_MODEL,), jnp.float32)}
    _L0_attn_all = _L0_attn_setup()
    _L0_attn_in = {k: v for k, v in _L0_attn_all.items() if k in ('W_Q', 'b_Q', 'W_K', 'b_K', 'W_V', 'b_V', 'W_O', 'b_O')}
    del _L0_attn_all

    def _L0_xattn_setup():
        import jax, jax.numpy as jnp
        import numpy as np
        B, Lq, Lk = (2, 512, 128)
        Q_DIM, KV_DIM = (256, 256)
        H, HD = (16, 128)
        KVC, QC, R = (64, 96, 64)
        LOOKBACK = 8
        NEG = -1e+30

        def _rope(x, L):
            half = x.shape[-1] // 2
            inv_freq = 1.0 / 10000.0 ** (jnp.arange(half, dtype=jnp.float32) / half)
            ang = jnp.arange(L, dtype=jnp.float32)[:, None] * inv_freq
            cos, sin = (jnp.cos(ang), jnp.sin(ang))
            x1, x2 = (x[..., :half], x[..., half:])
            return jnp.concatenate([x1 * cos - x2 * sin, x1 * sin + x2 * cos], axis=-1)
        key = jax.random.key(seed)
        ks = jax.random.split(key, 11)

        def w(k, shape, fan_in):
            return jax.random.normal(k, shape, jnp.float32) / np.sqrt(fan_in).astype(np.float32)
        return {'q': jax.random.normal(ks[0], (B, Lq, Q_DIM), jnp.float32), 'kv': jax.random.normal(ks[1], (B, Lk, KV_DIM), jnp.float32), 'seg_id': jnp.sort(jax.random.randint(ks[2], (B, Lq), 0, Lk), axis=-1), 'W_kvc': w(ks[3], (KV_DIM, KVC), KV_DIM), 'W_dq': w(ks[4], (Q_DIM, QC), Q_DIM), 'W_uq': w(ks[5], (QC, H * HD), QC), 'W_qr': w(ks[6], (QC, H * R), QC), 'W_uk': w(ks[7], (KVC, H * HD), KVC), 'W_kr': w(ks[8], (KVC, R), KVC), 'W_uv': w(ks[9], (KVC, H * HD), KVC), 'W_o': w(ks[10], (H * HD, Q_DIM), H * HD)}
    _L0_xattn_all = _L0_xattn_setup()
    _L0_xattn_in = {k: v for k, v in _L0_xattn_all.items() if k in ('W_kvc', 'W_dq', 'W_uq', 'W_qr', 'W_uk', 'W_kr', 'W_uv', 'W_o')}
    del _L0_xattn_all

    def _L0_ffn_setup():
        import jax, jax.numpy as jnp
        import numpy as np
        E = 8
        TOP_K = 2
        H = 256
        I = 176
        SI = 704
        key = jax.random.key(seed)
        ks = jax.random.split(key, 9)
        s = lambda fan_in: 1.0 / np.sqrt(fan_in)
        return {'hidden_states': jax.random.normal(ks[0], (4, 256, H), dtype=jnp.float32), 'router_w': jax.random.normal(ks[1], (E, H), dtype=jnp.float32) * s(H), 'w_gate': jax.random.normal(ks[2], (E, H, I), dtype=jnp.float32) * s(H), 'w_up': jax.random.normal(ks[3], (E, H, I), dtype=jnp.float32) * s(H), 'w_down': jax.random.normal(ks[4], (E, I, H), dtype=jnp.float32) * s(I), 'sw_gate': jax.random.normal(ks[5], (H, SI), dtype=jnp.float32) * s(H), 'sw_up': jax.random.normal(ks[6], (H, SI), dtype=jnp.float32) * s(H), 'sw_down': jax.random.normal(ks[7], (SI, H), dtype=jnp.float32) * s(SI), 'shared_gate_w': jax.random.normal(ks[8], (H,), dtype=jnp.float32) * s(H)}
    _L0_ffn_all = _L0_ffn_setup()
    _L0_ffn_in = {k: v for k, v in _L0_ffn_all.items() if k in ('router_w', 'w_gate', 'w_up', 'w_down', 'sw_gate', 'sw_up', 'sw_down', 'shared_gate_w')}
    del _L0_ffn_all
    return {'x': x, 'ctx_2048': ctx_2048, 'itok_BxS_0_1023': itok_BxS_0_1023, 'L0_attn_W_Q': _L0_attn_in['W_Q'], 'L0_attn_b_Q': _L0_attn_in['b_Q'], 'L0_attn_W_K': _L0_attn_in['W_K'], 'L0_attn_b_K': _L0_attn_in['b_K'], 'L0_attn_W_V': _L0_attn_in['W_V'], 'L0_attn_b_V': _L0_attn_in['b_V'], 'L0_attn_W_O': _L0_attn_in['W_O'], 'L0_attn_b_O': _L0_attn_in['b_O'], 'L0_xattn_W_kvc': _L0_xattn_in['W_kvc'], 'L0_xattn_W_dq': _L0_xattn_in['W_dq'], 'L0_xattn_W_uq': _L0_xattn_in['W_uq'], 'L0_xattn_W_qr': _L0_xattn_in['W_qr'], 'L0_xattn_W_uk': _L0_xattn_in['W_uk'], 'L0_xattn_W_kr': _L0_xattn_in['W_kr'], 'L0_xattn_W_uv': _L0_xattn_in['W_uv'], 'L0_xattn_W_o': _L0_xattn_in['W_o'], 'L0_ffn_router_w': _L0_ffn_in['router_w'], 'L0_ffn_w_gate': _L0_ffn_in['w_gate'], 'L0_ffn_w_up': _L0_ffn_in['w_up'], 'L0_ffn_w_down': _L0_ffn_in['w_down'], 'L0_ffn_sw_gate': _L0_ffn_in['sw_gate'], 'L0_ffn_sw_up': _L0_ffn_in['sw_up'], 'L0_ffn_sw_down': _L0_ffn_in['sw_down'], 'L0_ffn_shared_gate_w': _L0_ffn_in['shared_gate_w']}

def reference(x, ctx_2048, itok_BxS_0_1023, L0_attn_W_Q, L0_attn_b_Q, L0_attn_W_K, L0_attn_b_K, L0_attn_W_V, L0_attn_b_V, L0_attn_W_O, L0_attn_b_O, L0_xattn_W_kvc, L0_xattn_W_dq, L0_xattn_W_uq, L0_xattn_W_qr, L0_xattn_W_uk, L0_xattn_W_kr, L0_xattn_W_uv, L0_xattn_W_o, L0_ffn_router_w, L0_ffn_w_gate, L0_ffn_w_up, L0_ffn_w_down, L0_ffn_sw_gate, L0_ffn_sw_up, L0_ffn_sw_down, L0_ffn_shared_gate_w):
    import jax
    import jax.numpy as jnp

    def _L0_attn_ref(normalized_resid_pre, W_Q, b_Q, W_K, b_K, W_V, b_V, W_O, b_O):
        import jax, jax.numpy as jnp
        import numpy as np
        import math
        N_HEADS, D_MODEL, D_HEAD = (16, 256, 128)
        BATCH, SEQ = (4, 256)
        ROPE_THETA = 10000.0

        def _rope_cos_sin(seq_len, head_dim, dtype=jnp.float32):
            inv_freq = 1.0 / ROPE_THETA ** (jnp.arange(0, head_dim, 2, dtype=jnp.float32) / head_dim)
            m = jnp.arange(seq_len, dtype=jnp.float32)
            freqs = jnp.outer(m, inv_freq)
            return (jnp.cos(freqs).astype(dtype), jnp.sin(freqs).astype(dtype))

        def _apply_rope(x, cos, sin):
            x1 = x[..., 0::2]
            x2 = x[..., 1::2]
            cos = cos[None, :, None, :]
            sin = sin[None, :, None, :]
            r1 = x1 * cos - x2 * sin
            r2 = x1 * sin + x2 * cos
            out = jnp.stack([r1, r2], axis=-1)
            return out.reshape(x.shape)
        x = normalized_resid_pre
        T = x.shape[1]
        d_head = W_Q.shape[-1]
        Q = jnp.einsum('btc,ncd->btnd', x, W_Q) + b_Q
        K = jnp.einsum('btc,ncd->btnd', x, W_K) + b_K
        V = jnp.einsum('btc,ncd->btnd', x, W_V) + b_V
        cos, sin = _rope_cos_sin(T, d_head, x.dtype)
        Q = _apply_rope(Q, cos, sin)
        K = _apply_rope(K, cos, sin)
        scores = jnp.einsum('bqnd,bknd->bnqk', Q, K) / math.sqrt(d_head)
        causal = jnp.tril(jnp.ones((T, T), dtype=bool))
        scores = jnp.where(causal[None, None], scores, -jnp.inf)
        probs = jax.nn.softmax(scores, axis=-1)
        z = jnp.einsum('bnqk,bknd->bqnd', probs, V)
        out = jnp.einsum('bqnd,ndm->bqm', z, W_O) + b_O
        return out

    def _L0_xattn_ref(q, kv, seg_id, W_kvc, W_dq, W_uq, W_qr, W_uk, W_kr, W_uv, W_o):
        import jax, jax.numpy as jnp
        import numpy as np
        B, Lq, Lk = (2, 512, 128)
        Q_DIM, KV_DIM = (256, 256)
        H, HD = (16, 128)
        KVC, QC, R = (64, 96, 64)
        LOOKBACK = 8
        NEG = -1e+30

        def _rope(x, L):
            half = x.shape[-1] // 2
            inv_freq = 1.0 / 10000.0 ** (jnp.arange(half, dtype=jnp.float32) / half)
            ang = jnp.arange(L, dtype=jnp.float32)[:, None] * inv_freq
            cos, sin = (jnp.cos(ang), jnp.sin(ang))
            x1, x2 = (x[..., :half], x[..., half:])
            return jnp.concatenate([x1 * cos - x2 * sin, x1 * sin + x2 * cos], axis=-1)
        b, lq, _ = q.shape
        lk = kv.shape[1]
        kv_c = kv @ W_kvc
        q_c = q @ W_dq
        q_nope = (q_c @ W_uq).reshape(b, lq, H, HD).transpose(0, 2, 1, 3)
        q_rope = (q_c @ W_qr).reshape(b, lq, H, R).transpose(0, 2, 1, 3)
        k_nope = (kv_c @ W_uk).reshape(b, lk, H, HD)
        v = (kv_c @ W_uv).reshape(b, lk, H, HD)
        k_rope = kv_c @ W_kr
        q_rope = _rope(q_rope, lq)
        k_rope = _rope(k_rope, lk)
        scale = 1.0 / np.sqrt(HD + R).astype(np.float32)
        scores = (jnp.einsum('bhqd,bkhd->bhqk', q_nope, k_nope) + jnp.einsum('bhqr,bkr->bhqk', q_rope, k_rope)) * scale
        k_ids = jnp.arange(lk)[None, None, :]
        qs = seg_id[:, :, None]
        good = (k_ids <= qs) & (k_ids >= qs - LOOKBACK)
        scores = jnp.where(good[:, None, :, :], scores, NEG)
        attn = jax.nn.softmax(scores, axis=-1)
        out = jnp.einsum('bhqk,bkhd->bqhd', attn, v).reshape(b, lq, H * HD)
        return out @ W_o

    def _L0_ffn_ref(hidden_states, router_w, w_gate, w_up, w_down, sw_gate, sw_up, sw_down, shared_gate_w):
        import jax, jax.numpy as jnp
        import numpy as np
        E = 8
        TOP_K = 2
        H = 256
        I = 176
        SI = 704
        B, S, Hd = hidden_states.shape
        x = hidden_states.reshape(-1, Hd)
        shared = jnp.einsum('ts,sh->th', jax.nn.silu(x @ sw_gate) * (x @ sw_up), sw_down)
        logits = x @ router_w.T
        probs = jax.nn.softmax(logits.astype(jnp.float32), axis=-1)
        top_w, top_i = jax.lax.top_k(probs, TOP_K)
        top_w = top_w / jnp.sum(top_w, axis=-1, keepdims=True)
        combine = jnp.sum(jax.nn.one_hot(top_i, E, dtype=x.dtype) * top_w[..., None].astype(x.dtype), axis=1)
        h = jax.nn.silu(jnp.einsum('th,ehi->eti', x, w_gate)) * jnp.einsum('th,ehi->eti', x, w_up)
        expert_out = jnp.einsum('eti,eih->eth', h, w_down)
        routed = jnp.einsum('eth,te->th', expert_out, combine)
        shared_out = jax.nn.sigmoid(x @ shared_gate_w)[:, None] * shared
        return (routed + shared_out).reshape(B, S, Hd)
    x = _layernorm(x + _L0_attn_ref(x, L0_attn_W_Q, L0_attn_b_Q, L0_attn_W_K, L0_attn_b_K, L0_attn_W_V, L0_attn_b_V, L0_attn_W_O, L0_attn_b_O), axis=-1)
    x = _layernorm(x + _L0_xattn_ref(x, ctx_2048, itok_BxS_0_1023, L0_xattn_W_kvc, L0_xattn_W_dq, L0_xattn_W_uq, L0_xattn_W_qr, L0_xattn_W_uk, L0_xattn_W_kr, L0_xattn_W_uv, L0_xattn_W_o), axis=-1)
    x = _layernorm(x + _L0_ffn_ref(x, L0_ffn_router_w, L0_ffn_w_gate, L0_ffn_w_up, L0_ffn_w_down, L0_ffn_sw_gate, L0_ffn_sw_up, L0_ffn_sw_down, L0_ffn_shared_gate_w), axis=-1)
    return x

_drawn_inputs = setup_inputs


def setup_inputs(seed=0):
    import zlib

    import numpy as np

    out = dict(_drawn_inputs(seed))
    spreads = {'L0_attn_b_Q': (0.0, 0.73),
     'L0_attn_b_K': (0.0, 0.719),
     'L0_attn_b_V': (0.0, 0.1),
     'L0_attn_b_O': (0.0, 0.1)}
    factors = {'L0_attn_W_Q': 3.735, 'L0_attn_W_K': 3.406}
    for name, (base, spread) in spreads.items():
        noise = np.random.default_rng([zlib.crc32(name.encode()), seed]).standard_normal(out[name].shape)
        drawn = base * np.exp(spread * noise) if base else spread * noise
        out[name] = jnp.asarray(drawn.astype(out[name].dtype))
    for name, factor in factors.items():
        out[name] = (out[name] * factor).astype(out[name].dtype)
    return out
```

```python
from contextlib import ExitStack

import numpy as np

import concourse.bass as bass
from concourse import mybir

ALU = mybir.AluOpType
ACT = mybir.ActivationFunctionType
F32 = mybir.dt.float32
F32R = mybir.dt.float32r
BF16 = mybir.dt.bfloat16
I32 = mybir.dt.int32
AX_X = mybir.AxisListType.X

P = 128
B, T, D = 8, 256, 256
KC = D // P
TT = T // P
NT = B * TT
H, HD = 16, 128
PAIRS = H // 2
UNITS = 2 * B
KT, KVC, QC, R = 64, 64, 96, 64
LOOKBACK = 8
E, I, SI = 8, 176, 704
GATES = E + 1
CH = -(-(E * I + SI) // P)
LAST = E * I + SI - (CH - 1) * P
GT = 512
GROUPS = B * T // GT
GTT = GT // P
RING = 6
BIG = 1e30
XSCALE = float(1.0 / np.sqrt(HD + R).astype(np.float32))
EPS = 1e-5
NEG = -1e30


def build(nc, t, out):
    ctx = ExitStack()
    with ctx:
        def sb(name, shape, dt=F32, where=ctx):
            return where.enter_context(nc.sbuf_tensor(name, shape, dt))

        def sem(name):
            return ctx.enter_context(nc.semaphore(name))

        bank = [ctx.enter_context(nc.psum_tensor(f"bank{i}", [P, 512], F32)) for i in range(8)]

        y = sb("y", [P, NT, D])
        xh = sb("xh", [P, KC, B * T], F32R)
        xl = sb("xl", [P, KC, B * T], F32R)
        ident = sb("ident", [P, P])
        ln_stats = sb("ln_stats", [P, NT, 6])
        ln_mv = sb("ln_mv", [P, NT, 2])
        mv_tile = sb("mv_tile", [P, GTT, 2])
        ln_std = sb("ln_std", [P, NT])
        ln_rstd = sb("ln_rstd", [P, NT])
        eps_t = sb("eps_t", [P, 1])
        identb = sb("identb", [P, P], BF16)

        p0 = ExitStack()
        wukT = sb("wukT", [P, H, KVC], where=p0)
        wuqT = sb("wuqT", [P, H, QC], where=p0)
        wuvT = sb("wuvT", [P, H, KVC], where=p0)
        wox = sb("wox", [P, H, D], where=p0)
        ctxT = sb("ctxT", [P, KC, B * KT], where=p0)
        wkvc = sb("wkvc", [P, KC, 2 * KVC], where=p0)
        wkr = sb("wkr", [KVC, 2, 2 * R], where=p0)
        wdq = sb("wdq", [P, KC, QC], where=p0)
        seg_i = sb("seg_i", [P, NT], I32, where=p0)
        seg = sb("seg", [P, NT], where=p0)
        keys = sb("keys", [P, KT], where=p0)
        xcosK = sb("xcosK", [P, KT], where=p0)
        xsinK = sb("xsinK", [P, KT], where=p0)

        p2 = ExitStack()
        wqrh = sb("wqrh", [QC, PAIRS, 2, 2 * R], F32R, where=p2)
        wqrl = sb("wqrl", [QC, PAIRS, 2, 2 * R], F32R, where=p2)
        kvc = sb("kvc", [P, B * KT], where=p2)
        Mh = sb("Mh", [P, PAIRS, D], F32R, where=p2)
        Ml = sb("Ml", [P, PAIRS, D], F32R, where=p2)
        KP = sb("KP", [QC, B, H, KT], where=p2)
        krT = sb("krT", [P, B, KT], where=p2)
        pen = sb("pen", [P, NT, KT], where=p2)
        RB = sb("RB", [P, 2 * KT], where=p2)
        BDh = sb("BDh", [P, 2 * KT], F32R, where=p2)
        BDl = sb("BDl", [P, 2 * KT], F32R, where=p2)
        qc = sb("qc", [QC, T], where=p2)
        qch = sb("qch", [QC, T], F32R, where=p2)
        qcl = sb("qcl", [QC, T], F32R, where=p2)
        rq = sb("rq", [P, 2, 2, T], where=p2)
        qrT = sb("qrT", [P, PAIRS, T], where=p2)
        xmax = sb("xmax", [P, TT, H], where=p2)
        xsum = sb("xsum", [P, TT, H], where=p2)
        xrec = sb("xrec", [P, TT, H], where=p2)
        wdqh = sb("wdqh", [P, KC, QC], F32R, where=p2)
        wdql = sb("wdql", [P, KC, QC], F32R, where=p2)
        xcosQ = sb("xcosQ", [P, T], where=p2)
        xsinQ = sb("xsinQ", [P, T], where=p2)
        p2pre = ExitStack()
        wqr = sb("wqr", [QC, PAIRS, 2, 2 * R], where=p2pre)
        AT = sb("AT", [KVC, H, QC], where=p2pre)
        krc = sb("krc", [P, B, KT], where=p2pre)
        krs = sb("krs", [P, B, KT], where=p2pre)
        pen2 = sb("pen2", [P, NT, KT], where=p2pre)
        p2pre.close()
        p2loop = ExitStack()
        xs = sb("xs", [P, TT, H, KT], where=p2loop)
        xpT = sb("xpT", [P, TT, PAIRS, P], where=p2loop)
        VO = sb("VO", [P, PAIRS, D], where=p2loop)
        p2loop.close()
        p2.close()

        p1 = ExitStack()
        xraw = sb("xraw", [P, KC, B * T], where=p1)
        bo = sb("bo", [P, D], where=p1)
        bqk = sb("bqk", [P, H * 2], where=p1)
        bv = sb("bv", [P, H], where=p1)
        cosT = sb("cosT", [P, 2, T], where=p1)
        sinT = sb("sinT", [P, 2, T], where=p1)
        maskb = sb("maskb", [P, P], BF16, where=p1)
        maskf = sb("maskf", [P, P], where=p1)
        qkraw = [sb(f"qkraw{i}", [P, KC, 2 * HD], where=p1) for i in range(2)]
        wqkh = [sb(f"wqkh{i}", [P, KC, 2 * HD], F32R, where=p1) for i in range(2)]
        wqkl = [sb(f"wqkl{i}", [P, KC, 2 * HD], F32R, where=p1) for i in range(2)]
        vraw = sb("vraw", [P, KC, 2 * HD], where=p1)
        wvh = sb("wvh", [P, KC, 2 * HD], F32R, where=p1)
        wvl = sb("wvl", [P, KC, 2 * HD], F32R, where=p1)
        oraw = sb("oraw", [P, 2, D], where=p1)
        woh = sb("woh", [P, 2, D], F32R, where=p1)
        wol = sb("wol", [P, 2, D], F32R, where=p1)
        qkb = sb("qkb", [P, 2, 2, T], where=p1)
        rcos = sb("rcos", [P, 2, 2, T], where=p1)
        rsin = sb("rsin", [P, 2, 2, T], where=p1)
        qkr = sb("qkr", [P, 2, 2, T], where=p1)
        V = sb("V", [P, B, TT, 2 * HD], where=p1)
        prob = sb("prob", [P, 4, 3 * P], where=p1)
        probT = sb("probT", [P, 2, 3 * P], where=p1)
        negmax = sb("negmax", [P, 2, 2], where=p1)
        psums = sb("psums", [P, 4, 2], where=p1)
        prec = sb("prec", [P, 4, 2], where=p1)
        zh = sb("zh", [P, 2, B, T], F32R, where=p1)
        zl = sb("zl", [P, 2, B, T], F32R, where=p1)
        p1.close()
        p0.close()

        p3 = ExitStack()
        guraw = sb("guraw", [P, RING, 2, KC, P], where=p3)
        dnraw = sb("dnraw", [P, RING, D], where=p3)
        guh = sb("guh", [P, CH, 2, KC, P], F32R, where=p3)
        gul = sb("gul", [P, CH, 2, KC, P], F32R, where=p3)
        dnh = sb("dnh", [P, CH, D], F32R, where=p3)
        dnl = sb("dnl", [P, CH, D], F32R, where=p3)
        rwh = sb("rwh", [P, KC, P], F32R, where=p3)
        rwl = sb("rwl", [P, KC, P], F32R, where=p3)
        lg = sb("lg", [P, NT, GATES], where=p3)
        ex = sb("ex", [P, NT, GATES], where=p3)
        rt = [sb(f"rt{i}", [P, NT, E], where=p3) for i in range(3)]
        rcol = [sb(f"rcol{i}", [P, NT], where=p3) for i in range(2)]
        comb = sb("comb", [P, NT, GATES], where=p3)
        crest = [sb(f"crest{i}", [P, NT, GATES], where=p3) for i in range(2)]
        cpart = sb("cpart", [P, NT, 3, GATES], BF16, where=p3)
        combT = sb("combT", [3 * GATES, B * T], BF16, where=p3)
        sel = sb("sel", [3 * GATES, CH * P], BF16, where=p3)
        enum = sb("enum", [P, E], where=p3)
        p3pre = ExitStack()
        self_ = sb("self_", [3 * GATES, CH * P], where=p3pre)
        lgT = sb("lgT", [GATES, B * T], where=p3pre)
        rwraw = sb("rwraw", [P, KC, P], where=p3pre)
        p3pre.close()
        p3loop = ExitStack()
        act_g = sb("act_g", [P, 2, GT], where=p3loop)
        gu_t = sb("gu_t", [P, 2, GT], where=p3loop)
        hf = sb("hf", [P, 2, GT], where=p3loop)
        hh_ = sb("hh_", [P, 2, GT], F32R, where=p3loop)
        hl_ = sb("hl_", [P, 2, GT], F32R, where=p3loop)
        p3loop.close()
        p3.close()

        bQK, bS = (bank[0], bank[1]), (bank[2], bank[3])
        bT, bZ, bVO = bank[4], (bank[5], bank[7]), bank[6]
        ln_bank = (bank[5], bank[7])
        A_BANKS, KP_BANKS = (0, 1, 3, 4), (2, 0, 1, 3)

        x_in = [sem(f"x_in{i}") for i in range(4)]
        y_in = sem("y_in")
        cst_in = sem("cst_in")
        bias_in = sem("bias_in")
        qkraw_in = [sem(f"qkraw_in{i}") for i in range(2)]
        vraw_in = sem("vraw_in")
        oraw_in = sem("oraw_in")
        out_done = sem("out_done")
        consts = sem("consts")
        eps_set = sem("eps_set")
        passed_act, passed_pool, passed_pe, passed_dve = (sem("passed_" + e) for e in ("act", "pool", "pe", "dve"))
        xh_ready = sem("xh_ready")
        xl_ready = sem("xl_ready")
        y_init = sem("y_init")
        w_hi = sem("w_hi")
        wqk_ready = sem("wqk_ready")
        wv_ready = sem("wv_ready")
        wo_ready = sem("wo_ready")
        qk_done = sem("qk_done")
        vmm_done = sem("vmm_done")
        s_done = sem("s_done")
        t_done = sem("t_done")
        pv_done = sem("pv_done")
        wo_done = sem("wo_done")
        qkb_done = sem("qkb_done")
        vcopy_done = sem("vcopy_done")
        exp_done = sem("exp_done")
        ptc_done = sem("ptc_done")
        zh_done = sem("zh_done")
        max_done = sem("max_done")
        ropemul_done = sem("ropemul_done")
        rec_done = sem("rec_done")
        zl_done = sem("zl_done")
        yadd_done = sem("yadd_done")
        norm_done = sem("norm_done")
        rope_done = sem("rope_done")
        stat_done = sem("stat_done")
        mv_done = sem("mv_done")
        aggr_done = sem("aggr_done")
        std_done = sem("std_done")
        rstd_done = sem("rstd_done")
        xn_done = sem("xn_done")
        xt_done = sem("xt_done")
        xth_done = sem("xth_done")
        xtl_done = sem("xtl_done")
        xw_in = sem("xw_in")
        wqr_in = sem("wqr_in")
        table_in = sem("table_in")
        wdqh_done = sem("wdqh_done")
        wdql_done = sem("wdql_done")
        wqrh_done = sem("wqrh_done")
        wqrl_done = sem("wqrl_done")
        zero_done = sem("zero_done")
        seg_done = sem("seg_done")
        pen_step = sem("pen_step")
        pre_mm = sem("pre_mm")
        pre_cp = sem("pre_cp")
        ml_done = sem("ml_done")
        kr_mm = sem("kr_mm")
        kr_mul = sem("kr_mul")
        kr_done = sem("kr_done")
        raw_in = [sem(f"raw_in{i}") for i in range(RING)]
        misc_in = sem("misc_in")
        rwh_done = sem("rwh_done")
        rwl_done = sem("rwl_done")
        sel_done = sem("sel_done")
        guh_done = sem("guh_done")
        dnh_done = sem("dnh_done")
        wg_ready = sem("wg_ready")
        lgT_mm = sem("lgT_mm")
        lgT_cp = sem("lgT_cp")
        lg_mm = sem("lg_mm")
        lg_cp = sem("lg_cp")
        r_step = sem("r_step")
        r_exp = sem("r_exp")
        comb_mm = sem("comb_mm")
        comb_cp = sem("comb_cp")
        g_done = sem("g_done")
        u_done = sem("u_done")
        k_done = sem("k_done")
        silu_done = sem("silu_done")
        gut_done = sem("gut_done")
        hf_done = sem("hf_done")
        hh_done = sem("hh_done")
        hl_done = sem("hl_done")
        d_done = sem("d_done")
        y3_done = sem("y3_done")
        c_done = sem("c_done")
        vo_mm = sem("vo_mm")
        vo_cp = sem("vo_cp")
        a_done = sem("a_done")
        qch_done = sem("qch_done")
        qcl_done = sem("qcl_done")
        qr_mm = sem("qr_mm")
        rq_done = sem("rq_done")
        qr_ready = sem("qr_ready")
        bdh_done = sem("bdh_done")
        bd_ready = sem("bd_ready")
        xs_done = sem("xs_done")
        xmax_done = sem("xmax_done")
        xsub_done = sem("xsub_done")
        xexp_done = sem("xexp_done")
        xsum_done = sem("xsum_done")
        xrec_done = sem("xrec_done")
        xp_ready = sem("xp_ready")
        e_done = sem("e_done")
        pt_cp = sem("pt_cp")
        f_done = sem("f_done")
        y2_done = sem("y2_done")


        QK, ROT, SC, NORM, TR, PV, ZLO, WO, ADD = 8, 7, 6, 5, 4, 3, 2, 1, 0

        def attention(eng, step):
            for s in range(-QK, 0):
                step(0, 0, s, 0, UNITS)
            with eng.Fori(0, PAIRS - 1) as pair:
                base = pair * UNITS
                for s in range(UNITS):
                    step(base, pair, s, 0, 2 * UNITS)
            for s in range(UNITS):
                step((PAIRS - 1) * UNITS, PAIRS - 1, s, 0, UNITS)

        def where(k):
            return k // UNITS, k % UNITS // B, k % B

        LN_GROUP = 512 // D

        def phase_one_over(eng):
            eng.wait_ge(wo_done, PAIRS * B + 8)
            eng.wait_ge(yadd_done, PAIRS * B + 1)
            eng.wait_ge(rope_done, PAIRS * UNITS)
            eng.wait_ge(zh_done, PAIRS * UNITS)

        def ln_act_std(act, n):
            act.wait_ge(mv_done, NT * (n + 1))
            act.activation(ln_std[:, :], ln_mv[:, :, 1], ACT.Sqrt, bias=eps_t[:, 0:1]).then_inc(std_done, 1)

        def ln_act_hi(act, n):
            for g in range(B):
                act.wait_ge(xt_done, B * n + g + 1)
                act.activation(xh[:, :, g * T:(g + 1) * T], ln_bank[g % 2][:, :], ACT.Copy).then_inc(xth_done, 1)

        def ln_dve_normalise(dve, n):
            dve.wait_ge(std_done, n + 1)
            dve.reciprocal(ln_rstd[:, :], ln_std[:, :]).then_inc(rstd_done, 1)
            dve.wait_ge(rstd_done, n + 1)
            for i in range(NT):
                dve.tensor_scalar(y[:, i, :], y[:, i, :], ln_mv[:, i, 0:1], ln_rstd[:, i:i + 1], ALU.subtract,
                                  ALU.mult).then_inc(xn_done, 1)

        def ln_dve_lo(dve, n):
            for g in range(B):
                dve.wait_ge(xth_done, B * n + g + 1)
                cols = slice(g * T, (g + 1) * T)
                dve.tensor_tensor(xl[:, :, cols], ln_bank[g % 2][:, :], xh[:, :, cols].bitcast(F32),
                                  ALU.subtract).then_inc(xtl_done, 1)

        def ln_pe_transpose(pe, n):
            for g in range(B):
                if g >= 2:
                    pe.wait_ge(xtl_done, B * n + g - 1)
                for i in range(TT):
                    pe.wait_ge(xn_done, NT * n + g * TT + i + 1)
                    for c in range(KC):
                        ins = pe.transpose(ln_bank[g % 2][:, c * T + i * P:c * T + (i + 1) * P],
                                           y[:, g * TT + i, c * P:(c + 1) * P], ident[:, :])
                ins.then_inc(xt_done, 1)

        XW = [(wukT[:, :, :], "wukT"), (wuqT[:, :, :], "wuqT"), (wuvT[:, :, :], "wuvT"), (wox[:, :, :], "wox"),
              (ctxT[:, :, :], "ctxT"), (wkvc[:, :, :], "wkvc"), (wkr[:, :, :], "wkr"), (wdq[:, :, :], "wdq"),
              (seg_i[:, :], "seg"), (keys[:, :], "keys"), (xcosK[:, :], "xcosK"), (xsinK[:, :], "xsinK")]

        def cross(eng, prologue, body):
            prologue()
            with eng.Fori(0, B - 1) as b:
                body(b, True)
            body(B - 1, False)

        R_STEPS = 24

        def phase_two_over(eng):
            eng.wait_ge(f_done, NT)
            eng.wait_ge(y2_done, NT + 2)
            eng.wait_ge(pt_cp, 2 * NT + 2)

        UP = 2

        def mlp(eng, step, end):
            for s in range(-UP, 0):
                step(0, 0, s, 0, CH)
            for s in range(CH):
                step(0, 0, s, 0, 2 * CH)
            end(0)
            with eng.Fori(1, GROUPS - 1) as g:
                for s in range(CH):
                    step(g * CH, g, s, 0, 2 * CH)
                end(g)
            for s in range(CH):
                step((GROUPS - 1) * CH, GROUPS - 1, s, 0, CH)
            end(GROUPS - 1)

        def rows(c):
            return P if c % CH < CH - 1 else LAST

        def reuse(eng, sem_, base, k):
            if isinstance(base, int) and base + k < 2 and k < CH:
                return
            eng.wait_ge(sem_, base + (k if k % CH == 0 else k - 1))

        block = ctx.enter_context(nc.Block())

        @block.sync
        def _(sp):
            for j in range(4):
                cols = slice(j * 2 * T, (j + 1) * 2 * T)
                sp.dma_start(xraw[:, :, cols], t["xT"][:, :, cols]).then_inc(x_in[j], 16)
                if j == 0:
                    sp.dma_start(qkraw[0][:, :, :], t["wqk"][0]).then_inc(qkraw_in[0], 16)
                    sp.dma_start(cosT[:, :, :], t["cos"]).then_inc(cst_in, 16)
                    sp.dma_start(sinT[:, :, :], t["sin"]).then_inc(cst_in, 16)
                    sp.dma_start(vraw[:, :, :], t["wv"][0]).then_inc(vraw_in, 16)
                    sp.dma_start(qkraw[1][:, :, :], t["wqk"][1]).then_inc(qkraw_in[1], 16)
            sp.dma_start(oraw[:, :, :], t["wo"][0]).then_inc(oraw_in, 16)
            sp.dma_start(y[:, :, :], t["x"]).then_inc(y_in, 16)
            for dst, name in XW:
                sp.dma_start(dst, t[name]).then_inc(xw_in, 16)
            with sp.Fori(0, PAIRS - 1) as pair:
                sp.wait_ge(wqk_ready, pair * 2 + 1)
                sp.dma_start(qkraw[0][:, :, :], t["wqk"][pair * 2 + 2]).then_inc(qkraw_in[0], 16)
                sp.wait_ge(wv_ready, pair + 1)
                sp.dma_start(vraw[:, :, :], t["wv"][pair + 1]).then_inc(vraw_in, 16)
                sp.wait_ge(wqk_ready, pair * 2 + 2)
                sp.dma_start(qkraw[1][:, :, :], t["wqk"][pair * 2 + 3]).then_inc(qkraw_in[1], 16)
                sp.wait_ge(wo_ready, pair + 1)
                sp.dma_start(oraw[:, :, :], t["wo"][pair + 1]).then_inc(oraw_in, 16)
            phase_one_over(sp)
            sp.dma_start(wqr[:, :, :, :], t["wqr"]).then_inc(wqr_in, 16)
            sp.dma_start(xcosQ[:, :], t["xcosQ"]).then_inc(table_in, 16)
            sp.dma_start(xsinQ[:, :], t["xsinQ"]).then_inc(table_in, 16)
            sp.wait_ge(qr_ready, 1)
            sp.wait_ge(a_done, 1)
            for c in range(CH):
                if c >= RING:
                    sp.wait_ge(wg_ready, c - RING + 1)
                sp.dma_start(guraw[:, c % RING, :, :, :], t["wgu"][c]).then_inc(raw_in[c % RING], 16)
                sp.dma_start(dnraw[0:rows(c), c % RING, :], t["wdn"][c, 0:rows(c), :]).then_inc(raw_in[c % RING], 16)
                if c == RING - 1:
                    phase_two_over(sp)
                    sp.dma_start(rwraw[:, :, :], t["rw"]).then_inc(misc_in, 16)
                    sp.dma_start(self_[:, :], t["sel"]).then_inc(misc_in, 16)
                    sp.dma_start(enum[:, :], t["enum"]).then_inc(misc_in, 16)
            for g in range(GROUPS):
                sp.wait_ge(xn_done, 2 * NT + (g + 1) * GTT)
                sp.dma_start(out[:, g * GTT:(g + 1) * GTT, :], y[:, g * GTT:(g + 1) * GTT, :]).then_inc(out_done, 16)
            sp.wait_ge(out_done, 16 * GROUPS)

        @block.gpsimd
        def _(pool):
            splits = [0]

            def split(hi, lo, raw, raw_sem, raw_count, number, ready):
                pool.wait_ge(raw_sem, raw_count)
                pool.sem_inc(passed_pool, 1)
                pool.tensor_copy(hi, raw).then_inc(w_hi, 1)
                pool.wait_ge(w_hi, number + 1)
                pool.tensor_tensor(lo, raw, hi.bitcast(F32), ALU.subtract).then_inc(ready, 1)

            def split_qk(hh, pair, number):
                split(wqkh[hh][:, :, :], wqkl[hh][:, :, :], qkraw[hh][:, :, :], qkraw_in[hh],
                      (pair + 1) * 16, number, wqk_ready)

            def split_v(pair, number):
                split(wvh[:, :, :], wvl[:, :, :], vraw[:, :, :], vraw_in, (pair + 1) * 16, number, wv_ready)

            pool.memset(eps_t[:, :], EPS).then_inc(eps_set, 1)
            split_qk(0, 0, 0)
            split_v(0, 1)

            def step(base, pair, s, lo, hi):
                k = s + ROT
                if lo <= k < hi:
                    pool.wait_ge(ropemul_done, base + (k + 1))
                    if not (isinstance(base, int) and base + k < 2):
                        pool.wait_ge(s_done, base + (k - 1))
                    pool.tensor_tensor(qkr[:, k % 2, :, :], rcos[:, k % 2, :, :], rsin[:, k % 2, :, :],
                                       ALU.add).then_inc(rope_done, 1)
                if s == -4:
                    split_qk(1, 0, 2)
                if s == 0:
                    pool.wait_ge(wo_done, pair * B + 8)
                    split(woh[:, :, :], wol[:, :, :], oraw[:, :, :], oraw_in, (pair + 1) * 16, pair * 4 + 3,
                          wo_ready)
                if s == 1 and hi > UNITS:
                    pool.wait_ge(qk_done, base + B)
                    split_qk(0, pair + 1, pair * 4 + 4)
                if s == 3 and hi > UNITS:
                    pool.wait_ge(vmm_done, pair * B + B)
                    split_v(pair + 1, pair * 4 + 5)
                if s == 9 and hi > UNITS:
                    pool.wait_ge(qk_done, base + 2 * B)
                    split_qk(1, pair + 1, pair * 4 + 6)

            attention(pool, step)

            pool.wait_ge(xw_in, 16 * len(XW))
            pool.tensor_copy(seg[:, :], seg_i[:, :]).then_inc(seg_done, 1)
            phase_one_over(pool)
            pool.tensor_copy(wdqh[:, :, :], wdq[:, :, :]).then_inc(wdqh_done, 1)
            pool.memset(RB[:, :], 0.0)
            pool.memset(BDh[:, :].bitcast(F32), 0.0)
            pool.memset(BDl[:, :].bitcast(F32), 0.0).then_inc(zero_done, 1)
            pool.wait_ge(wdqh_done, 1)
            pool.tensor_tensor(wdql[:, :, :], wdq[:, :, :], wdqh[:, :, :].bitcast(F32), ALU.subtract)\
                .then_inc(wdql_done, 1)
            pool.wait_ge(wqr_in, 16)
            pool.tensor_copy(wqrh[:, :, :, :], wqr[:, :, :, :]).then_inc(wqrh_done, 1)
            pool.wait_ge(wqrh_done, 1)
            pool.tensor_tensor(wqrl[:, :, :, :], wqr[:, :, :, :], wqrh[:, :, :, :].bitcast(F32), ALU.subtract)\
                .then_inc(wqrl_done, 1)
            pool.wait_ge(seg_done, 1)
            every_key = keys[:, :].unsqueeze(1).broadcast_to([P, NT, KT])
            every_seg = seg[:, :].unsqueeze(2).broadcast_to([P, NT, KT])
            pool.tensor_tensor(pen[:, :, :], every_key, every_seg, ALU.subtract).then_inc(pen_step, 1)
            pool.wait_ge(pen_step, 1)
            pool.tensor_scalar(pen2[:, :, :], pen[:, :, :], 0.0, None, ALU.is_gt).then_inc(pen_step, 1)
            pool.tensor_scalar(pen[:, :, :], pen[:, :, :], float(-LOOKBACK), None, ALU.is_lt).then_inc(pen_step, 1)
            pool.wait_ge(pen_step, 3)
            pool.tensor_tensor(pen[:, :, :], pen[:, :, :], pen2[:, :, :], ALU.add).then_inc(pen_step, 1)
            pool.wait_ge(pen_step, 4)
            pool.tensor_scalar(pen[:, :, :], pen[:, :, :], NEG, None, ALU.mult).then_inc(pen_step, 1)
            pool.wait_ge(kr_mul, 2)
            pool.tensor_tensor(krT[:, :, :], krc[:, :, :], krs[:, :, :], ALU.add).then_inc(kr_done, 1)

            def rotary(count):
                for i in range(PAIRS):
                    pool.wait_ge(rq_done, count * PAIRS + (i + 1))
                    pool.tensor_tensor(qrT[:, i, :], rq[:, i % 2, 0, :], rq[:, i % 2, 1, :], ALU.add)\
                        .then_inc(qr_ready, 1)

            def prologue():
                rotary(0)

            def body(b, more):
                if more:
                    pool.wait_ge(c_done, 2 * b + 2)
                    rotary(b + 1)

            cross(pool, prologue, body)

            phase_two_over(pool)
            pool.wait_ge(misc_in, 48)
            pool.tensor_copy(rwh[:, :, :], rwraw[:, :, :]).then_inc(rwh_done, 1)
            pool.wait_ge(rwh_done, 1)
            pool.tensor_tensor(rwl[:, :, :], rwraw[:, :, :], rwh[:, :, :].bitcast(F32), ALU.subtract)\
                .then_inc(rwl_done, 1)
            for c in range(CH):
                r = rows(c)
                pool.wait_ge(raw_in[c % RING], 32 * (c // RING + 1))
                pool.tensor_copy(guh[:, c, :, :, :], guraw[:, c % RING, :, :, :]).then_inc(guh_done, 1)
                pool.tensor_copy(dnh[0:r, c, :], dnraw[0:r, c % RING, :]).then_inc(dnh_done, 1)
                pool.wait_ge(guh_done, c + 1)
                pool.tensor_tensor(gul[:, c, :, :, :], guraw[:, c % RING, :, :, :], guh[:, c, :, :, :].bitcast(F32),
                                   ALU.subtract)
                pool.wait_ge(dnh_done, c + 1)
                pool.tensor_tensor(dnl[0:r, c, :], dnraw[0:r, c % RING, :], dnh[0:r, c, :].bitcast(F32),
                                   ALU.subtract).then_inc(wg_ready, 1)

        @block.scalar
        def _(act):
            act.dma_start(bqk[:, :], t["bqk"]).then_inc(bias_in, 16)
            act.dma_start(bv[:, :], t["bv"]).then_inc(bias_in, 16)
            act.dma_start(maskf[:, :], t["mask"]).then_inc(cst_in, 16)
            act.dma_start(ident[:, :], t["ident"]).then_inc(cst_in, 16)
            act.dma_start(bo[:, :], t["bo"]).then_inc(cst_in, 16)
            for b in range(B):
                act.wait_ge(x_in[b // 2], 16)
                cols = slice(b * T, (b + 1) * T)
                act.activation(xh[:, :, cols], xraw[:, :, cols], ACT.Copy).then_inc(xh_ready, 1)
                if b == 1:
                    act.wait_ge(bias_in, 32)
            act.wait_ge(cst_in, 80)
            act.activation(identb[:, :], ident[:, :], ACT.Copy).then_inc(consts, 1)
            act.activation(maskb[:, :], maskf[:, :], ACT.Copy).then_inc(consts, 1)

            def step(base, pair, s, lo, hi):
                early = isinstance(base, int) and base == 0
                k = s + QK
                if lo <= k < hi:
                    ahead, hh, b = where(k)
                    act.wait_ge(qk_done, base + (k + 1))
                    if not (early and k < 2):
                        act.wait_ge(ropemul_done, base + (k - 1))
                    act.sem_inc(passed_act, 1)
                    for j in range(2):
                        col = (pair + ahead) * 4 + (2 * hh + j)
                        ins = act.activation(qkb[:, k % 2, j, :], bQK[k % 2][:, j * T:(j + 1) * T], ACT.Identity,
                                             bias=bqk[:, bass.ds(col, 1)])
                    ins.then_inc(qkb_done, 1)
                    if hh == 0:
                        act.wait_ge(vmm_done, (pair + ahead) * B + (b + 1))
                        act.wait_ge(pv_done, base + (ahead * UNITS + b + 1))
                        act.activation(V[:, b, :, :], bVO[:, :], ACT.Copy).then_inc(vcopy_done, 1)
                k = s + SC
                if lo <= k < hi:
                    act.wait_ge(max_done, base + (k + 1))
                    if not (early and k < 4):
                        act.wait_ge(t_done, base + (k - 3))
                    act.activation(prob[:, k % 4, 0:P], bS[k % 2][:, 0:P], ACT.Exp, bias=negmax[:, k % 2, 0:1],
                                   accum_out=psums[:, k % 4, 0:1])
                    act.activation(prob[:, k % 4, P:3 * P], bS[k % 2][:, P:3 * P], ACT.Exp,
                                   bias=negmax[:, k % 2, 1:2], accum_out=psums[:, k % 4, 1:2]).then_inc(exp_done, 1)
                k = s + TR
                if lo <= k < hi:
                    act.wait_ge(t_done, base + (k + 1))
                    act.wait_ge(pv_done, base + (k + 7))
                    act.activation(probT[:, k % 2, :], bT[:, 0:3 * P], ACT.Copy).then_inc(ptc_done, 1)
                k = s + PV
                if lo <= k < hi:
                    ahead, hh, b = where(k)
                    act.wait_ge(pv_done, base + (k + 9))
                    act.wait_ge(wo_done, (pair + ahead) * B + (b + 1))
                    act.sem_inc(passed_act, 1)
                    act.activation(zh[:, hh, b, :], bZ[k % 2][:, 0:T], ACT.Identity,
                                   bias=bv[:, bass.ds((pair + ahead) * 2 + hh, 1)]).then_inc(zh_done, 1)

            attention(act, step)

            phase_one_over(act)
            act.wait_ge(pre_mm, 1)
            act.activation(kvc[:, :], bank[2][:, :], ACT.Copy).then_inc(pre_cp, 1)
            for g in range(4):
                act.wait_ge(pre_mm, g + 2)
                act.activation(AT[:, 4 * g:4 * g + 4, :], bank[A_BANKS[g]][0:KVC, 0:4 * QC], ACT.Copy)\
                    .then_inc(pre_cp, 1)
            ln_act_std(act, 0)
            for g in range(4):
                act.wait_ge(pre_mm, g + 6)
                act.activation(Mh[:, 2 * g:2 * g + 2, :], bank[A_BANKS[g]][:, :], ACT.Copy).then_inc(pre_cp, 1)
            for h in range(H):
                act.wait_ge(pre_mm, h + 10)
                act.activation(KP[:, :, h, :], bank[KP_BANKS[h % 4]][0:QC, :].rearrange("p (b k) -> p b k", b=B),
                               ACT.Copy).then_inc(pre_cp, 1)
            ln_act_hi(act, 0)

            def latent(count):
                act.wait_ge(a_done, count + 1)
                act.activation(qc[:, :], bank[4][0:QC, 0:T], ACT.Copy)
                act.activation(qch[:, :], bank[4][0:QC, 0:T], ACT.Copy).then_inc(qch_done, 1)

            def keys_of(b, count):
                act.sem_inc(passed_act, 1)
                for r in (slice(0, 64), slice(64, P)):
                    act.activation(RB[r, r], krT[r, bass.ds(b, 1), :], ACT.Copy)
                    ins = act.activation(BDh[r, r], kvc[r, bass.ds(b * KT, KT)], ACT.Copy)
                ins.then_inc(bdh_done, 1)

            def exp(b, j):
                act.wait_ge(xsub_done, 2 * b + (j + 1))
                act.activation(xs[:, j, :, :], xs[:, j, :, :], ACT.Exp).then_inc(xexp_done, 1)

            def prologue():
                act.wait_ge(pre_cp, 1)
                act.wait_ge(zero_done, 1)
                act.wait_ge(kr_done, 1)
                keys_of(0, 0)
                latent(0)

            def body(b, more):
                for e in range(4):
                    if e == 2:
                        exp(b, 0)
                    act.wait_ge(vo_mm, 4 * b + (e + 1))
                    act.wait_ge(y2_done, 2 * b + 2)
                    act.activation(VO[:, 2 * e:2 * e + 2, :], bank[4 + e % 2][:, :], ACT.Copy).then_inc(vo_cp, 1)
                if more:
                    act.wait_ge(bd_ready, b + 1)
                    keys_of(b + 1, b + 1)
                    latent(b + 1)
                exp(b, 1)
                for j in range(TT):
                    for half in range(2):
                        act.wait_ge(e_done, 4 * b + (2 * j + half + 1))
                        act.activation(xpT[:, j, 4 * half:4 * half + 4, :], bank[6 + half][:, :], ACT.Copy)\
                            .then_inc(pt_cp, 1)

            cross(act, prologue, body)
            ln_act_std(act, 1)
            ln_act_hi(act, 1)

            phase_two_over(act)
            act.wait_ge(misc_in, 48)
            act.activation(sel[:, :], self_[:, :], ACT.Copy).then_inc(sel_done, 1)
            for g in range(GROUPS):
                act.wait_ge(lgT_mm, g + 1)
                act.activation(lgT[:, g * GT:(g + 1) * GT], bank[g][0:GATES, :], ACT.Copy).then_inc(lgT_cp, 1)
            act.wait_ge(lg_mm, 1)
            act.activation(lg[:, :, :], bank[4][:, 0:NT * GATES], ACT.Copy).then_inc(lg_cp, 1)
            act.wait_ge(r_step, 2)
            act.activation(ex[:, :, 0:E], rt[0][:, :, :], ACT.Exp)
            act.activation(ex[:, :, E:GATES], lg[:, :, E:GATES], ACT.Exp, scale=-1.0).then_inc(r_exp, 1)
            for j in range(2):
                act.wait_ge(comb_mm, j + 1)
                act.activation(combT[:, j * 1024:(j + 1) * 1024], bank[5 + j].bitcast(BF16)[0:3 * GATES, :],
                               ACT.Copy).then_inc(comb_cp, 1)

            def step(base, g, s, lo, hi):
                k = s + UP
                if lo <= k < hi:
                    b, r = k % CH % 2, rows(k)
                    act.wait_ge(g_done, base + (k + 1))
                    reuse(act, gut_done, base, k)
                    act.activation(act_g[0:r, b, :], bank[b][0:r, :], ACT.Silu).then_inc(silu_done, 1)
                    act.wait_ge(hf_done, base + (k + 1))
                    reuse(act, d_done, base, k)
                    act.activation(hh_[0:r, b, :], hf[0:r, b, :], ACT.Copy).then_inc(hh_done, 1)
                if s == 4 and not (isinstance(g, int) and g == 0):
                    std(g - 1)

            def std(g):
                act.wait_ge(mv_done, 2 * NT + g * GTT + GTT)
                act.sem_inc(passed_act, 1)
                cols = bass.ds(g * GTT, GTT)
                act.activation(ln_std[:, cols], ln_mv[:, cols, 1], ACT.Sqrt, bias=eps_t[:, 0:1]).then_inc(std_done, 1)

            def end(g):
                if isinstance(g, int) and g == GROUPS - 1:
                    std(g)

            mlp(act, step, end)

        @block.vector
        def _(dve):
            for b in range(B):
                dve.wait_ge(xh_ready, b + 1)
                cols = slice(b * T, (b + 1) * T)
                dve.tensor_tensor(xl[:, :, cols], xraw[:, :, cols], xh[:, :, cols].bitcast(F32),
                                  ALU.subtract).then_inc(xl_ready, 1)
            dve.wait_ge(cst_in, 80)
            dve.sem_inc(yadd_done, 1)

            def step(base, pair, s, lo, hi):
                early = isinstance(base, int) and base == 0
                k = s + NORM
                if lo <= k < hi:
                    dve.wait_ge(exp_done, base + (k + 1))
                    dve.reciprocal(prec[:, k % 4, :], psums[:, k % 4, :]).then_inc(rec_done, 1)
                    dve.wait_ge(rec_done, base + (k + 1))
                    dve.tensor_scalar(prob[:, k % 4, 0:P], prob[:, k % 4, 0:P], prec[:, k % 4, 0:1], None, ALU.mult)
                    dve.tensor_scalar(prob[:, k % 4, P:3 * P], prob[:, k % 4, P:3 * P], prec[:, k % 4, 1:2],
                                      None, ALU.mult).then_inc(norm_done, 1)
                k = s + ROT
                if lo <= k < hi:
                    dve.wait_ge(qkb_done, base + (k + 1))
                    if not (early and k < 2):
                        dve.wait_ge(rope_done, base + (k - 1))
                    dve.tensor_tensor(rcos[:, k % 2, :, :], qkb[:, k % 2, :, :], cosT[:, :, :], ALU.mult)
                    dve.tensor_tensor(rsin[0:64, k % 2, :, :], qkb[64:P, k % 2, :, :], sinT[64:P, :, :], ALU.mult)
                    dve.tensor_tensor(rsin[64:P, k % 2, :, :], qkb[0:64, k % 2, :, :], sinT[0:64, :, :],
                                      ALU.mult).then_inc(ropemul_done, 1)
                k = s + ADD
                if lo <= k < hi and where(k)[1] == 1:
                    b = where(k)[2]
                    dve.wait_ge(wo_done, pair * B + (b + 9))
                    if early and b == 0:
                        dve.wait_ge(y_init, NT)
                    dve.wait_ge(yadd_done, pair * B + (b + 1))
                    dve.tensor_tensor(y[:, 2 * b:2 * b + 2, :], bVO[:, :], y[:, 2 * b:2 * b + 2, :],
                                      ALU.add).then_inc(yadd_done, 1)
                k = s + ZLO
                if lo <= k < hi:
                    ahead, hh, b = where(k)
                    dve.wait_ge(zh_done, base + (k + 1))
                    dve.scalar_tensor_tensor(zl[:, hh, b, :], bZ[k % 2][:, 0:T],
                                             bv[:, bass.ds((pair + ahead) * 2 + hh, 1)],
                                             zh[:, hh, b, :].bitcast(F32), ALU.add, ALU.subtract).then_inc(zl_done, 1)
                k = s + SC
                if lo <= k < hi:
                    dve.wait_ge(s_done, base + (k + 1))
                    if not (early and k < 2):
                        dve.wait_ge(exp_done, base + (k - 1))
                    dve.tensor_reduce(negmax[:, k % 2, 0:1], bS[k % 2][:, 0:P], AX_X, ALU.max, negate=True)
                    dve.tensor_reduce(negmax[:, k % 2, 1:2], bS[k % 2][:, P:3 * P], AX_X, ALU.max,
                                      negate=True).then_inc(max_done, 1)
                if s == -1:
                    dve.wait_ge(y_in, 16)
                    for i in range(NT):
                        dve.tensor_tensor(y[:, i, :], y[:, i, :], bo[:, :], ALU.add).then_inc(y_init, 1)
                    dve.wait_ge(y_init, NT)

            attention(dve, step)
            dve.wait_ge(yadd_done, PAIRS * B + 1)
            for i in range(NT):
                dve.bn_stats(ln_stats[:, i, :], y[:, i, :]).then_inc(stat_done, 1)
            for i in range(NT):
                dve.wait_ge(stat_done, i + 1)
                dve.bn_aggr(ln_mv[:, i, :], ln_stats[:, i, :]).then_inc(mv_done, 1)
            ln_dve_normalise(dve, 0)
            phase_one_over(dve)
            for g in range(4):
                dve.wait_ge(pre_cp, g + 6)
                dve.tensor_tensor(Ml[:, 2 * g:2 * g + 2, :], bank[A_BANKS[g]][:, :], Mh[:, 2 * g:2 * g + 2, :].bitcast(F32),
                                  ALU.subtract).then_inc(ml_done, 1)
            for j, (dst, table) in enumerate(((krc, xcosK), (krs, xsinK))):
                dve.wait_ge(kr_mm, j + 1)
                dve.tensor_tensor(dst[:, :, :], bank[(5, 7)[j]][:, :].rearrange("p (b k) -> p b k", b=B),
                                  table[:, :].unsqueeze(1).broadcast_to([P, B, KT]), ALU.mult).then_inc(kr_mul, 1)
            ln_dve_lo(dve, 0)
            dve.sem_inc(y2_done, 2)

            def latent(count):
                dve.wait_ge(qch_done, count + 1)
                dve.tensor_tensor(qcl[:, :], bank[4][0:QC, 0:T], qch[:, :].bitcast(F32), ALU.subtract).then_inc(qcl_done, 1)

            def rotary(count):
                for i in range(PAIRS):
                    dve.wait_ge(qr_mm, count * PAIRS + (i + 1))
                    if not (isinstance(count, int) and count * PAIRS + i < 2):
                        dve.wait_ge(qr_ready, count * PAIRS + (i - 1))
                    src = bank[4 + (i + 1) % 2]
                    dve.tensor_tensor(rq[:, i % 2, 0, :], src[:, 0:T], xcosQ[:, :], ALU.mult)
                    dve.tensor_tensor(rq[:, i % 2, 1, :], src[:, T:2 * T], xsinQ[:, :], ALU.mult).then_inc(rq_done, 1)

            def keys_of(b, count):
                dve.wait_ge(bdh_done, count + 1)
                for r in (slice(0, 64), slice(64, P)):
                    ins = dve.tensor_tensor(BDl[r, r], kvc[r, bass.ds(b * KT, KT)], BDh[r, r].bitcast(F32), ALU.subtract)
                ins.then_inc(bd_ready, 1)

            def softmax_in(b, j):
                n = 2 * b + (j + 1)
                dve.wait_ge(c_done, n)
                dve.wait_ge(pt_cp, 4 * b + 2)
                for half in range(2):
                    dve.scalar_tensor_tensor(xs[:, j, 8 * half:8 * half + 8, :],
                                             bank[2 * j + half][:, :].rearrange("p (h k) -> p h k", h=8), XSCALE,
                                             pen[:, bass.ds(2 * b + j, 1), :].broadcast_to([P, 8, KT]),
                                             ALU.mult, ALU.add).then_inc(xs_done, 1)
                dve.wait_ge(xs_done, 4 * b + (2 * j + 2))
                dve.tensor_reduce(xmax[:, j, :], xs[:, j, :, :], AX_X, ALU.max).then_inc(xmax_done, 1)
                dve.wait_ge(xmax_done, n)
                dve.tensor_tensor(xs[:, j, :, :], xs[:, j, :, :], xmax[:, j, :].unsqueeze(2).broadcast_to([P, H, KT]),
                                  ALU.subtract).then_inc(xsub_done, 1)

            def softmax_out(b, j):
                n = 2 * b + (j + 1)
                dve.wait_ge(xexp_done, n)
                dve.tensor_reduce(xsum[:, j, :], xs[:, j, :, :], AX_X, ALU.add).then_inc(xsum_done, 1)
                dve.wait_ge(xsum_done, n)
                dve.reciprocal(xrec[:, j, :], xsum[:, j, :]).then_inc(xrec_done, 1)
                dve.wait_ge(xrec_done, n)
                dve.tensor_tensor(xs[:, j, :, :], xs[:, j, :, :], xrec[:, j, :].unsqueeze(2).broadcast_to([P, H, KT]),
                                  ALU.mult).then_inc(xp_ready, 1)

            def add_stats(b, j):
                n = 2 * b + (j + 1)
                dve.wait_ge(f_done, n)
                rows = y[:, bass.ds(2 * b + j, 1), :]
                dve.tensor_tensor(rows, bank[2 * j][:, 0:D], rows, ALU.add).then_inc(y2_done, 1)
                dve.wait_ge(y2_done, n + 2)
                dve.sem_inc(passed_dve, 1)
                dve.bn_stats(ln_stats[:, j, :], rows).then_inc(stat_done, 1)
                dve.wait_ge(stat_done, NT + n)
                dve.sem_inc(passed_dve, 1)
                dve.bn_aggr(mv_tile[:, j, :], ln_stats[:, j, :]).then_inc(aggr_done, 1)
                dve.wait_ge(aggr_done, n)
                dve.tensor_copy(ln_mv[:, bass.ds(2 * b + j, 1), :], mv_tile[:, j:j + 1, :]).then_inc(mv_done, 1)

            def prologue():
                dve.wait_ge(table_in, 32)
                dve.wait_ge(zero_done, 1)
                keys_of(0, 0)
                latent(0)
                rotary(0)
                dve.wait_ge(pen_step, 5)

            def body(b, more):
                softmax_in(b, 0)
                softmax_in(b, 1)
                softmax_out(b, 0)
                if more:
                    keys_of(b + 1, b + 1)
                    latent(b + 1)
                    rotary(b + 1)
                softmax_out(b, 1)
                add_stats(b, 0)
                add_stats(b, 1)

            cross(dve, prologue, body)
            ln_dve_normalise(dve, 1)
            ln_dve_lo(dve, 1)

            count = [0]

            def then(ins):
                count[0] += 1
                ins.then_inc(r_step, 1)
                dve.wait_ge(r_step, count[0])

            wide = [P, NT, E]
            bc = lambda a: a.unsqueeze(2).broadcast_to(wide)
            enum_b = enum[:, :].unsqueeze(1).broadcast_to(wide)
            logit = lg[:, :, 0:E]
            dve.wait_ge(lg_cp, 1)
            dve.wait_ge(misc_in, 48)
            then(dve.tensor_reduce(rcol[0][:, :], logit, AX_X, ALU.max))
            then(dve.tensor_tensor(rt[0][:, :, :], logit, bc(rcol[0][:, :]), ALU.subtract))
            then(dve.tensor_scalar(rt[1][:, :, :], rt[0][:, :, :], 0.0, float(E), ALU.is_lt, ALU.mult))
            then(dve.tensor_tensor(rt[1][:, :, :], rt[1][:, :, :], enum_b, ALU.add))
            then(dve.tensor_reduce(rcol[0][:, :], rt[1][:, :, :], AX_X, ALU.min))
            then(dve.tensor_tensor(rt[1][:, :, :], enum_b, bc(rcol[0][:, :]), ALU.is_equal))
            then(dve.scalar_tensor_tensor(rt[2][:, :, :], rt[1][:, :, :], -BIG, logit, ALU.mult, ALU.add))
            then(dve.tensor_reduce(rcol[0][:, :], rt[2][:, :, :], AX_X, ALU.max))
            then(dve.tensor_tensor(rt[2][:, :, :], rt[2][:, :, :], bc(rcol[0][:, :]), ALU.is_lt))
            then(dve.scalar_tensor_tensor(rt[2][:, :, :], rt[2][:, :, :], float(E), enum_b, ALU.mult, ALU.add))
            then(dve.tensor_reduce(rcol[0][:, :], rt[2][:, :, :], AX_X, ALU.min))
            then(dve.tensor_tensor(rt[2][:, :, :], enum_b, bc(rcol[0][:, :]), ALU.is_equal))
            then(dve.tensor_tensor(rt[2][:, :, :], rt[2][:, :, :], rt[1][:, :, :], ALU.add))
            dve.wait_ge(r_exp, 1)
            then(dve.tensor_tensor(rt[2][:, :, :], rt[2][:, :, :], ex[:, :, 0:E], ALU.mult))
            then(dve.tensor_reduce(rcol[0][:, :], rt[2][:, :, :], AX_X, ALU.add))
            then(dve.reciprocal(rcol[1][:, :], rcol[0][:, :]))
            then(dve.tensor_tensor(comb[:, :, 0:E], rt[2][:, :, :], bc(rcol[1][:, :]), ALU.mult))
            then(dve.tensor_scalar(rcol[0][:, :], ex[:, :, E], 1.0, None, ALU.add))
            then(dve.reciprocal(comb[:, :, E], rcol[0][:, :]))
            then(dve.tensor_copy(cpart[:, :, 0, :], comb[:, :, :]))
            then(dve.tensor_tensor(crest[0][:, :, :], comb[:, :, :], cpart[:, :, 0, :], ALU.subtract))
            then(dve.tensor_copy(cpart[:, :, 1, :], crest[0][:, :, :]))
            then(dve.tensor_tensor(crest[1][:, :, :], crest[0][:, :, :], cpart[:, :, 1, :], ALU.subtract))
            then(dve.tensor_copy(cpart[:, :, 2, :], crest[1][:, :, :]))
            assert count[0] == R_STEPS

            def step(base, g, s, lo, hi):
                k = s + UP
                if lo <= k < hi:
                    b, r = k % CH % 2, rows(k)
                    dve.wait_ge(silu_done, base + (k + 1))
                    dve.wait_ge(u_done, base + (k + 1))
                    dve.tensor_tensor(gu_t[0:r, b, :], bank[2 + b][0:r, :], act_g[0:r, b, :], ALU.mult).then_inc(gut_done, 1)
                    dve.wait_ge(gut_done, base + (k + 1))
                    dve.wait_ge(k_done, base + (k + 1))
                    reuse(dve, hh_done, base, k)
                    dve.tensor_tensor(hf[0:r, b, :], bank[4 + b][0:r, :], gu_t[0:r, b, :], ALU.mult).then_inc(hf_done, 1)
                    dve.wait_ge(hh_done, base + (k + 1))
                    dve.tensor_tensor(hl_[0:r, b, :], hf[0:r, b, :], hh_[0:r, b, :].bitcast(F32),
                                      ALU.subtract).then_inc(hl_done, 1)
                if s == 5 and not (isinstance(g, int) and g == 0):
                    normalise(g - 1)

            def normalise(g):
                dve.wait_ge(std_done, g + 3)
                dve.reciprocal(ln_rstd[:, bass.ds(g * GTT, GTT)], ln_std[:, bass.ds(g * GTT, GTT)]).then_inc(rstd_done, 1)
                dve.wait_ge(rstd_done, g + 3)
                for i in range(GTT):
                    rows_ = y[:, bass.ds(g * GTT + i, 1), :]
                    dve.tensor_scalar(rows_, rows_, ln_mv[:, bass.ds(g * GTT + i, 1), 0],
                                      ln_rstd[:, bass.ds(g * GTT + i, 1)], ALU.subtract, ALU.mult).then_inc(xn_done, 1)

            def end(g):
                dve.wait_ge(d_done, g * CH + CH)
                for j in range(2):
                    part = y[:, bass.ds(g * GTT + 2 * j, 2), :]
                    dve.tensor_tensor(part, bank[6 + j][:, :], part, ALU.add).then_inc(y3_done, 1)
                dve.wait_ge(y3_done, g * 2 + 2)
                dve.sem_inc(passed_dve, 1)
                for i in range(GTT):
                    dve.bn_stats(ln_stats[:, i, :], y[:, bass.ds(g * GTT + i, 1), :]).then_inc(stat_done, 1)
                dve.wait_ge(stat_done, 2 * NT + g * GTT + GTT)
                dve.sem_inc(passed_dve, 1)
                for i in range(GTT):
                    ins = dve.bn_aggr(mv_tile[:, i, :], ln_stats[:, i, :])
                ins.then_inc(aggr_done, 1)
                dve.wait_ge(aggr_done, NT + g + 1)
                dve.tensor_copy(ln_mv[:, bass.ds(g * GTT, GTT), :], mv_tile[:, :, :]).then_inc(mv_done, GTT)
                if isinstance(g, int) and g == GROUPS - 1:
                    normalise(g)

            mlp(dve, step, end)

        @block.tensor
        def _(pe):
            pe.wait_ge(consts, 2)
            pe.sem_inc(pv_done, 8)
            pe.sem_inc(wo_done, 8)

            def three_pass(dst, lh, ll, rh, rl, first, last):
                pe.matmul(dst, lh, rh, start=first, stop=False)
                pe.matmul(dst, ll, rh, start=False, stop=False)
                return pe.matmul(dst, lh, rl, start=False, stop=last)

            def step(base, pair, s, lo, hi):
                early = isinstance(base, int) and base == 0
                k = s + SC
                if lo <= k < hi:
                    pe.wait_ge(rope_done, base + (k + 1))
                    if not (early and k < 2):
                        pe.wait_ge(exp_done, base + (k - 1))
                    dst, r = bS[k % 2], qkr[:, k % 2, :, :]
                    pe.matmul(dst[:, 0:P], r[:, 0, 0:P], r[:, 1, 0:P], start=True, stop=False)
                    pe.matmul(dst[:, 0:P], identb[:, :], maskb[:, :], start=False, stop=True)
                    pe.matmul(dst[:, P:3 * P], r[:, 0, P:T], r[:, 1, :], start=True, stop=False)
                    pe.matmul(dst[:, 2 * P:3 * P], identb[:, :], maskb[:, :], start=False, stop=True).then_inc(s_done, 1)
                k = s + QK
                if lo <= k < hi:
                    ahead, hh, b = where(k)
                    if early and hh == 0 and ahead == 0:
                        pe.wait_ge(xl_ready, b + 1)
                    if b == 0:
                        pe.wait_ge(wqk_ready, pair * 2 + (2 * ahead + hh + 1))
                    if not (early and k < 2):
                        pe.wait_ge(qkb_done, base + (k - 1))
                    cols = slice(b * T, (b + 1) * T)
                    for j in range(2):
                        dst = bQK[k % 2][:, j * T:(j + 1) * T]
                        for c in range(KC):
                            w = slice(j * HD, (j + 1) * HD)
                            ins = three_pass(dst, wqkh[hh][:, c, w], wqkl[hh][:, c, w], xh[:, c, cols], xl[:, c, cols],
                                             c == 0, c == KC - 1)
                    ins.then_inc(qk_done, 1)
                    if hh == 0:
                        if b == 0:
                            pe.wait_ge(wv_ready, pair + (ahead + 1))
                        if not (early and ahead == 0 and b == 0):
                            pe.wait_ge(vcopy_done, (pair + ahead) * B + b)
                        if s > B - 1:
                            pe.wait_ge(yadd_done, pair * B + (s - B + 2))
                        for i in range(TT):
                            rows = slice(b * T + i * P, b * T + (i + 1) * P)
                            for c in range(KC):
                                ins = three_pass(bVO[:, i * 2 * HD:(i + 1) * 2 * HD], xh[:, c, rows], xl[:, c, rows],
                                                 wvh[:, c, :], wvl[:, c, :], c == 0, c == KC - 1)
                        ins.then_inc(vmm_done, 1)
                k = s + TR
                if lo <= k < hi:
                    pe.wait_ge(norm_done, base + (k + 1))
                    if not (early and k < 1):
                        pe.wait_ge(ptc_done, base + k)
                    for i, q in enumerate((0, 1, 2)):
                        ins = pe.transpose(bT[:, i * P:(i + 1) * P], prob[:, k % 4, q * P:(q + 1) * P], ident[:, :])
                    ins.then_inc(t_done, 1)
                k = s + PV
                if lo <= k < hi:
                    ahead, hh, b = where(k)
                    pe.wait_ge(ptc_done, base + (k + 1))
                    if hh == 0:
                        pe.wait_ge(vcopy_done, (pair + ahead) * B + (b + 1))
                    if not (early and k < 2):
                        pe.wait_ge(zl_done, base + (k - 1))
                    dst, w = bZ[k % 2][:, 0:T], slice(hh * HD, (hh + 1) * HD)
                    pe.matmul(dst, V[:, b, 0, w], probT[:, k % 2, 0:2 * P], start=True, stop=False)
                    pe.matmul(dst[:, P:T], V[:, b, 1, w], probT[:, k % 2, 2 * P:3 * P], start=False,
                              stop=True).then_inc(pv_done, 1)
                k = s + WO
                if lo <= k < hi and where(k)[1] == 1:
                    b = where(k)[2]
                    pe.wait_ge(zl_done, base + (k + 1))
                    if b == 0:
                        pe.wait_ge(wo_ready, pair + 1)
                    pe.wait_ge(yadd_done, pair * B + (b + 1))
                    pe.wait_ge(vcopy_done, pair * B + (B + (s - B + 1 if s >= B and hi > UNITS else 0)))
                    for i in range(TT):
                        rows = slice(i * P, (i + 1) * P)
                        for hh in range(2):
                            ins = three_pass(bVO[:, i * D:(i + 1) * D], zh[:, hh, b, rows], zl[:, hh, b, rows],
                                             woh[:, hh, :], wol[:, hh, :], hh == 0, hh == 1)
                    ins.then_inc(wo_done, 1)

            attention(pe, step)

            pe.wait_ge(xw_in, 16 * len(XW))
            phase_one_over(pe)
            pe.wait_ge(zl_done, PAIRS * UNITS)
            pe.wait_ge(exp_done, PAIRS * UNITS)
            for c in range(KC):
                ins = pe.matmul(bank[2][:, :], wkvc[:, c, :], ctxT[:, c, :], start=c == 0, stop=c == KC - 1)
            ins.then_inc(pre_mm, 1)
            for g in range(4):
                for h in range(4 * g, 4 * g + 4):
                    ins = pe.matmul(bank[A_BANKS[g]][0:KVC, h % 4 * QC:(h % 4 + 1) * QC], wukT[:, h, :], wuqT[:, h, :],
                                    start=True, stop=True)
                ins.then_inc(pre_mm, 1)
            pe.wait_ge(pre_cp, 1)
            for j in range(2):
                pe.matmul(bank[(5, 7)[j]][:, :], wkr[:, j, :], kvc[0:KVC, :], start=True, stop=True).then_inc(kr_mm, 1)
            for g in range(4):
                pe.wait_ge(pre_cp, g + 2)
                for h in range(4 * g, 4 * g + 4):
                    ins = pe.matmul(bank[A_BANKS[g]][h % 2 * 64:h % 2 * 64 + 64, h // 2 % 2 * D:(h // 2 % 2 + 1) * D],
                                    wuvT[:, h, :], wox[:, h, :], start=True, stop=True)
                ins.then_inc(pre_mm, 1)
            for h in range(H):
                pe.wait_ge(pre_cp, 9 if h < 4 else h + 6)
                if h < 4:
                    pe.wait_ge(ml_done, 4)
                pe.matmul(bank[KP_BANKS[h % 4]][0:QC, :], AT[:, h, :], kvc[0:KVC, :], start=True, stop=True)\
                    .then_inc(pre_mm, 1)
            pe.wait_ge(kr_mul, 2)
            ln_pe_transpose(pe, 0)
            pe.wait_ge(pre_cp, 9 + H)
            pe.wait_ge(wdql_done, 1)
            pe.wait_ge(wqrl_done, 1)
            pe.wait_ge(xtl_done, B)
            pe.sem_inc(pt_cp, 2)

            def latent(b, count):
                for c in range(KC):
                    ins = three_pass(bank[4][0:QC, 0:T], wdqh[:, c, :], wdql[:, c, :], xh[:, c, bass.ds(b * T, T)],
                                     xl[:, c, bass.ds(b * T, T)], c == 0, c == KC - 1)
                ins.then_inc(a_done, 1)

            def rotary(b, count):
                for i in range(PAIRS):
                    if i == 0:
                        pe.wait_ge(qcl_done, count + 1)
                    if i >= 2:
                        pe.wait_ge(rq_done, count * PAIRS + (i - 1))
                    for j in range(2):
                        ins = three_pass(bank[4 + (i + 1) % 2][:, j * T:(j + 1) * T], wqrh[:, i, j, :], wqrl[:, i, j, :],
                                         qch[:, :], qcl[:, :], True, True)
                    ins.then_inc(qr_mm, 1)

            def prologue():
                latent(0, 0)
                rotary(0, 0)

            def body(b, more):
                pe.wait_ge(qr_ready, (b + 1) * PAIRS)
                pe.wait_ge(bd_ready, b + 1)
                for j in range(TT):
                    pe.wait_ge(y2_done, 2 * b + (j + 1))
                    rows = slice(j * P, (j + 1) * P)
                    for half in range(2):
                        dst = bank[2 * j + half]
                        pe.matmul(dst[:, :], qc[:, rows], KP[:, bass.ds(b, 1), 8 * half:8 * half + 8, :], start=True,
                                  stop=False)
                        for i in range(4):
                            ins = pe.matmul(dst[:, i * P:(i + 1) * P], qrT[:, 4 * half + i, rows], RB[:, :],
                                            start=False, stop=i == 3)
                    ins.then_inc(c_done, 1)
                for e in range(4):
                    if e < 2:
                        pe.wait_ge(rq_done, (b + 1) * PAIRS)
                    else:
                        pe.wait_ge(vo_cp, 4 * b + (e - 1))
                    for i in range(2):
                        ins = three_pass(bank[4 + e % 2][:, i * D:(i + 1) * D], BDh[:, :], BDl[:, :], Mh[:, 2 * e + i, :],
                                         Ml[:, 2 * e + i, :], True, True)
                    ins.then_inc(vo_mm, 1)
                if more:
                    pe.wait_ge(vo_cp, 4 * b + 4)
                    latent(b + 1, b + 1)
                    rotary(b + 1, b + 1)
                for j in range(TT):
                    pe.wait_ge(xp_ready, 2 * b + (j + 1))
                    for half in range(2):
                        pe.wait_ge(pt_cp, 4 * b + (2 * j + half + 1))
                        for i in range(4):
                            src = xs[:, j, 8 * half + 2 * i:8 * half + 2 * i + 2, :].rearrange("p h k -> p (h k)")
                            ins = pe.transpose(bank[6 + half][:, i * P:(i + 1) * P], src, ident[:, :])
                        ins.then_inc(e_done, 1)
                    pe.wait_ge(pt_cp, 4 * b + (2 * j + 4))
                    pe.wait_ge(vo_cp, 4 * b + 4)
                    for i in range(PAIRS):
                        ins = pe.matmul(bank[2 * j][:, 0:D], xpT[:, j, i, :], VO[:, i, :], start=i == 0,
                                        stop=i == PAIRS - 1)
                    ins.then_inc(f_done, 1)

            cross(pe, prologue, body)

            pe.wait_ge(y2_done, NT + 2)
            ln_pe_transpose(pe, 1)
            pe.wait_ge(xtl_done, 2 * B)
            pe.wait_ge(rwl_done, 1)
            for g in range(GROUPS):
                cols = slice(g * GT, (g + 1) * GT)
                for c in range(KC):
                    ins = three_pass(bank[g][:, :], rwh[:, c, :], rwl[:, c, :], xh[:, c, cols], xl[:, c, cols],
                                     c == 0, c == KC - 1)
                ins.then_inc(lgT_mm, 1)
            for i in range(NT):
                pe.wait_ge(lgT_cp, i // GTT + 1)
                ins = pe.transpose(bank[4][:, i * GATES:(i + 1) * GATES], lgT[:, i * P:(i + 1) * P],
                                   ident[0:GATES, 0:GATES])
            ins.then_inc(lg_mm, 1)

            def combined():
                pe.wait_ge(r_step, R_STEPS)
                for i in range(NT):
                    j, n = i // 8, i % 8
                    ins = pe.transpose(bank[5 + j].bitcast(BF16)[0:3 * GATES, n * P:(n + 1) * P],
                                       cpart[:, i, :, :].rearrange("p a e -> p (a e)"), identb[:, :])
                    if n == 7:
                        ins.then_inc(comb_mm, 1)
                pe.wait_ge(comb_cp, 2)
                pe.wait_ge(sel_done, 1)

            def step(base, g, s, lo, hi):
                k = s + UP
                if lo <= k < hi:
                    c, b, r = k % CH, k % CH % 2, rows(k)
                    cols = bass.ds((g + k // CH) * GT, GT)
                    pe.wait_ge(wg_ready, c + 1)
                    for j, used in ((0, silu_done), (1, gut_done)):
                        reuse(pe, used, base, k)
                        for kc in range(KC):
                            ins = three_pass(bank[2 * j + b][0:P, :], guh[:, c, j, kc, 0:P], gul[:, c, j, kc, 0:P],
                                             xh[:, kc, cols], xl[:, kc, cols], kc == 0, kc == KC - 1)
                        ins.then_inc((g_done, u_done)[j], 1)
                    if isinstance(base, int) and base + k == 0:
                        combined()
                    reuse(pe, hf_done, base, k)
                    pe.sem_inc(passed_pe, 1)
                    pe.matmul(bank[4 + b][:, :], sel[:, c * P:(c + 1) * P], combT[:, cols], start=True, stop=True)\
                        .then_inc(k_done, 1)
                k = s
                if lo <= k < hi:
                    b, r = k % 2, rows(k)
                    pe.wait_ge(hl_done, base + (k + 1))
                    if k == 0 and not (isinstance(g, int) and g == 0):
                        pe.wait_ge(y3_done, g * 2)
                    for i in range(GTT):
                        rs = slice(i * P, (i + 1) * P)
                        dst = bank[6 + i // 2][:, i % 2 * D:(i % 2 + 1) * D]
                        for n, (l, w) in enumerate(((hh_, dnh), (hl_, dnh), (hh_, dnl))):
                            ins = pe.matmul(dst, l[0:r, b, rs], w[0:r, k, :], start=k == 0 and n == 0 and i % 2 == 0,
                                            stop=k == CH - 1 and n == 2, skip_group_check=True)
                    ins.then_inc(d_done, 1)

            mlp(pe, step, lambda g: None)


def rope_tables():
    inv = (1.0 / np.float32(10000.0) ** (np.arange(0, HD, 2, dtype=np.float32) / HD)).astype(np.float32)
    ang = np.outer(np.arange(T, dtype=np.float32), inv).T
    scale = np.float32(HD ** -0.5)
    cos, sin = np.cos(ang), np.sin(ang)
    cos = np.concatenate([cos, cos])
    sin = np.concatenate([sin, -sin])
    return [np.ascontiguousarray(np.stack([a * scale, a], axis=1).astype(np.float32)) for a in (cos, sin)]


def layout(inp):
    n = {k: np.asarray(v) for k, v in inp.items()}
    x = n["x"]
    perm = np.concatenate([np.arange(0, HD, 2), np.arange(1, HD, 2)])
    a = {}
    a["xT"] = x.reshape(B * T, KC, P).transpose(2, 1, 0)
    a["x"] = x.reshape(NT, P, D).transpose(1, 0, 2)
    wq = n["L0_attn_W_Q"][:, :, perm].reshape(H, KC, P, HD)
    wk = n["L0_attn_W_K"][:, :, perm].reshape(H, KC, P, HD)
    a["wqk"] = np.concatenate([wq, wk], axis=3).transpose(0, 2, 1, 3)
    wv = n["L0_attn_W_V"].reshape(PAIRS, 2, KC, P, HD)
    a["wv"] = wv.transpose(0, 3, 2, 1, 4).reshape(PAIRS, P, KC, 2 * HD)
    a["wo"] = n["L0_attn_W_O"].reshape(PAIRS, 2, HD, D).transpose(0, 2, 1, 3)
    a["bqk"] = np.stack([n["L0_attn_b_Q"][:, perm], n["L0_attn_b_K"][:, perm]], axis=1).reshape(2 * H, HD).T
    a["bv"] = n["L0_attn_b_V"].T
    a["bo"] = np.broadcast_to(n["L0_attn_b_O"], (P, D))
    a["cos"], a["sin"] = rope_tables()
    gate = np.concatenate([n["L0_ffn_w_gate"].transpose(1, 0, 2).reshape(D, E * I), n["L0_ffn_sw_gate"]], axis=1)
    up = np.concatenate([n["L0_ffn_w_up"].transpose(1, 0, 2).reshape(D, E * I), n["L0_ffn_sw_up"]], axis=1)
    down = np.concatenate([n["L0_ffn_w_down"].reshape(E * I, D), n["L0_ffn_sw_down"]], axis=0)
    pad = CH * P - (E * I + SI)
    gu = np.pad(np.stack([gate, up]), ((0, 0), (0, 0), (0, pad)))
    a["wgu"] = gu.reshape(2, KC, P, CH, P).transpose(3, 2, 0, 1, 4)
    a["wdn"] = np.pad(down, ((0, pad), (0, 0))).reshape(CH, P, D)
    rw = np.concatenate([n["L0_ffn_router_w"].T, n["L0_ffn_shared_gate_w"][:, None]], axis=1)
    a["rw"] = np.pad(rw, ((0, 0), (0, P - GATES))).reshape(KC, P, P).transpose(1, 0, 2)
    expert = np.minimum(np.arange(CH * P) // I, E)
    a["sel"] = np.tile((expert[None, :] == np.arange(GATES)[:, None]).astype(np.float32), (3, 1))
    a["enum"] = np.broadcast_to(np.arange(E, dtype=np.float32), (P, E))
    swap = np.concatenate([np.arange(R // 2, R), np.arange(0, R // 2)])
    twice = lambda w, axis=-1: np.concatenate([w, w], axis=axis)
    a["wukT"] = n["L0_xattn_W_uk"].reshape(KVC, H, HD).transpose(2, 1, 0)
    a["wuqT"] = n["L0_xattn_W_uq"].reshape(QC, H, HD).transpose(2, 1, 0)
    a["wuvT"] = n["L0_xattn_W_uv"].reshape(KVC, H, HD).transpose(2, 1, 0)
    a["wox"] = n["L0_xattn_W_o"].reshape(H, HD, D).transpose(1, 0, 2)
    a["ctxT"] = n["ctx_2048"].reshape(B * KT, KC, P).transpose(2, 1, 0)
    a["wkvc"] = twice(n["L0_xattn_W_kvc"].reshape(KC, P, KVC).transpose(1, 0, 2))
    wkr = n["L0_xattn_W_kr"]
    a["wkr"] = np.stack([twice(wkr), twice(wkr[:, swap])], axis=1)
    a["wdq"] = n["L0_xattn_W_dq"].reshape(KC, P, QC).transpose(1, 0, 2)
    wqr = n["L0_xattn_W_qr"].reshape(QC, PAIRS, 2, R)
    a["wqr"] = np.stack([wqr, wqr[..., swap]], axis=2).reshape(QC, PAIRS, 2, 2 * R)
    a["seg"] = n["itok_BxS_0_1023"].reshape(NT, P).T
    a["keys"] = np.broadcast_to(np.arange(KT, dtype=np.float32), (P, KT))
    for name, count in (("K", KT), ("Q", T)):
        half = R // 2
        inv = (1.0 / np.float32(10000.0) ** (np.arange(half, dtype=np.float32) / half)).astype(np.float32)
        ang = (np.arange(count, dtype=np.float32)[:, None] * inv).T
        a["xcos" + name] = np.tile(np.cos(ang), (4, 1)).astype(np.float32)
        a["xsin" + name] = np.tile(np.concatenate([-np.sin(ang), np.sin(ang)]), (2, 1)).astype(np.float32)
    a["ident"] = np.eye(P, dtype=np.float32)
    q = np.arange(P)
    a["mask"] = np.where(q[None, :] > q[:, None], np.float32(NEG), np.float32(0))
    return {k: np.ascontiguousarray(v) for k, v in a.items()}


def program(nc, arrays):
    t = {k: nc.dram_tensor("in_" + k, v.shape, mybir.dt.from_np(v.dtype), kind="ExternalInput").ap()
         for k, v in arrays.items()}
    out = nc.dram_tensor("out", (B * T, D), F32, kind="ExternalOutput").ap()
    build(nc, t, out.rearrange("(n p) d -> p n d", p=P))


def kernel(**inputs):
    import concourse.bacc as bacc
    from concourse.bass_utils import run_bass_kernel_spmd
    arrays = layout(inputs)
    nc = bacc.Bacc("TRN2", target_bir_lowering=False, num_devices=1)
    program(nc, arrays)
    r = run_bass_kernel_spmd(nc, [{"in_" + k: v for k, v in arrays.items()}], core_ids=[0])
    return r.results[0]["out"].reshape(B, T, D)
```

```python
from contextlib import ExitStack

import numpy as np

import concourse.bass as bass
from concourse import mybir

ALU = mybir.AluOpType
ACT = mybir.ActivationFunctionType
F32 = mybir.dt.float32
F32R = mybir.dt.float32r
BF16 = mybir.dt.bfloat16
I32 = mybir.dt.int32
AX_X = mybir.AxisListType.X

P = 128
B, T, D = 8, 256, 256
KC = D // P
TT = T // P
NT = B * TT
H, HD = 16, 128
PAIRS = H // 2
UNITS = 2 * B
KT, KVC, QC, R = 64, 64, 96, 64
LOOKBACK = 8
E, I, SI = 8, 176, 704
GATES = E + 1
CH = -(-(E * I + SI) // P)
LAST = E * I + SI - (CH - 1) * P
GT = 512
GROUPS = B * T // GT
GTT = GT // P
RING = 4
BIG = 1e30
XSCALE = float(1.0 / np.sqrt(HD + R).astype(np.float32))
EPS = 1e-5
NEG = -1e30


def build(nc, t, out):
    ctx = ExitStack()
    with ctx:
        def sb(name, shape, dt=F32, where=ctx):
            return where.enter_context(nc.sbuf_tensor(name, shape, dt))

        def sem(name):
            return ctx.enter_context(nc.semaphore(name))

        bank = [ctx.enter_context(nc.psum_tensor(f"bank{i}", [P, 512], F32)) for i in range(8)]

        y = sb("y", [P, NT, D])
        xh = sb("xh", [P, KC, B * T], F32R)
        xl = sb("xl", [P, KC, B * T], F32R)
        ident = sb("ident", [P, P])
        ln_stats = sb("ln_stats", [P, NT, 6])
        ln_mv = sb("ln_mv", [P, NT, 2])
        mv_tile = sb("mv_tile", [P, GTT, 2])
        ln_std = sb("ln_std", [P, NT])
        ln_rstd = sb("ln_rstd", [P, NT])
        eps_t = sb("eps_t", [P, 1])
        identb = sb("identb", [P, P], BF16)

        p0 = ExitStack()
        wukT = sb("wukT", [P, H, KVC], where=p0)
        wuqT = sb("wuqT", [P, H, QC], where=p0)
        wuvT = sb("wuvT", [P, H, KVC], where=p0)
        wox = sb("wox", [P, H, D], where=p0)
        ctxT = sb("ctxT", [P, KC, B * KT], where=p0)
        wkvc = sb("wkvc", [P, KC, 2 * KVC], where=p0)
        wkr = sb("wkr", [KVC, 2, 2 * R], where=p0)
        wdq = sb("wdq", [P, KC, QC], where=p0)
        seg_i = sb("seg_i", [P, NT], I32, where=p0)
        seg = sb("seg", [P, NT], where=p0)
        keys = sb("keys", [P, KT], where=p0)
        xcosK = sb("xcosK", [P, KT], where=p0)
        xsinK = sb("xsinK", [P, KT], where=p0)

        p2 = ExitStack()
        wqrh = sb("wqrh", [QC, PAIRS, 2 * R], F32R, where=p2)
        wqrl = sb("wqrl", [QC, PAIRS, 2 * R], F32R, where=p2)
        kvc = sb("kvc", [P, B * KT], where=p2)
        Mh = sb("Mh", [P, PAIRS, D], F32R, where=p2)
        Ml = sb("Ml", [P, PAIRS, D], F32R, where=p2)
        KPh = sb("KPh", [QC, B, H, KT], F32R, where=p2)
        KPl = sb("KPl", [QC, B, H, KT], F32R, where=p2)
        krT = sb("krT", [P, B, KT], where=p2)
        pen = sb("pen", [P, NT, KT], where=p2)
        RB = sb("RB", [P, 2 * KT], where=p2)
        BDh = sb("BDh", [P, 2 * KT], F32R, where=p2)
        BDl = sb("BDl", [P, 2 * KT], F32R, where=p2)
        qch = sb("qch", [QC, T], F32R, where=p2)
        qcl = sb("qcl", [QC, T], F32R, where=p2)
        xmax = sb("xmax", [P, TT, H], where=p2)
        xsum = sb("xsum", [P, TT, H], where=p2)
        xrec = sb("xrec", [P, TT, H], where=p2)
        wdqh = sb("wdqh", [P, KC, QC], F32R, where=p2)
        wdql = sb("wdql", [P, KC, QC], F32R, where=p2)
        p2pre = ExitStack()
        wqr = sb("wqr", [QC, PAIRS, 2 * R], where=p2pre)
        p2pre.close()
        xcosQ = sb("xcosQ", [P, T], where=p2)
        xsinQ = sb("xsinQ", [P, T], where=p2)
        rq = sb("rq", [P, 2, 2, 2, T], where=p2)
        p2key = ExitStack()
        AT = sb("AT", [P, H, QC], F32R, where=p2key)
        kvch = sb("kvch", [P, B * KT], F32R, where=p2key)
        p2key.close()
        qrT = sb("qrT", [P, PAIRS, T], where=p2)
        p2.close()

        p1 = ExitStack()
        xraw = sb("xraw", [P, KC, B * T], where=p1)
        bo = sb("bo", [P, D], where=p1)
        bqk = sb("bqk", [P, H * 2], where=p1)
        bv = sb("bv", [P, H], where=p1)
        cosT = sb("cosT", [P, 2, T], where=p1)
        sinT = sb("sinT", [P, 2, T], where=p1)
        maskb = sb("maskb", [P, P], BF16, where=p1)
        maskf = sb("maskf", [P, P], where=p1)
        qkraw = [sb(f"qkraw{i}", [P, KC, 2 * HD], where=p1) for i in range(2)]
        wqkh = [sb(f"wqkh{i}", [P, KC, 2 * HD], F32R, where=p1) for i in range(2)]
        wqkl = [sb(f"wqkl{i}", [P, KC, 2 * HD], F32R, where=p1) for i in range(2)]
        vraw = sb("vraw", [P, KC, 2 * HD], where=p1)
        wvh = sb("wvh", [P, KC, 2 * HD], F32R, where=p1)
        wvl = sb("wvl", [P, KC, 2 * HD], F32R, where=p1)
        oraw = sb("oraw", [P, 2, D], where=p1)
        woh = sb("woh", [P, 2, D], F32R, where=p1)
        wol = sb("wol", [P, 2, D], F32R, where=p1)
        qkb = sb("qkb", [P, 2, 2, T], where=p1)
        rcos = sb("rcos", [P, 2, 2, T], where=p1)
        rsin = sb("rsin", [P, 2, 2, T], where=p1)
        qkr = sb("qkr", [P, 2, 2, T], where=p1)
        V = sb("V", [P, B, TT, 2 * HD], where=p1)
        prob = sb("prob", [P, 4, 3 * P], where=p1)
        probT = sb("probT", [P, 2, 3 * P], where=p1)
        negmax = sb("negmax", [P, 2, 2], where=p1)
        psums = sb("psums", [P, 4, 2], where=p1)
        prec = sb("prec", [P, 4, 2], where=p1)
        zh = sb("zh", [P, 2, B, T], F32R, where=p1)
        zl = sb("zl", [P, 2, B, T], F32R, where=p1)
        p1.close()
        p0.close()

        p2w = ExitStack()
        kvcl = sb("kvcl", [P, B * KT], F32R, where=p2w)
        krc = sb("krc", [P, B, KT], where=p2w)
        pen2 = sb("pen2", [P, NT, KT], where=p2w)
        p2w.close()

        p3 = ExitStack()
        guraw = sb("guraw", [P, RING, 2, KC, P], where=p3)
        dnraw = sb("dnraw", [P, RING, D], where=p3)
        p3x = ExitStack()
        xs = sb("xs", [P, TT, H, KT], where=p3x)
        xpT = sb("xpT", [P, TT, PAIRS, P], where=p3x)
        VO = sb("VO", [P, PAIRS, D], where=p3x)
        p3x.close()
        guh = sb("guh", [P, CH, 2, KC, P], F32R, where=p3)
        gul = sb("gul", [P, CH, 2, KC, P], F32R, where=p3)
        dnh = sb("dnh", [P, CH, D], F32R, where=p3)
        dnl = sb("dnl", [P, CH, D], F32R, where=p3)
        rwh = sb("rwh", [P, KC, P], F32R, where=p3)
        rwl = sb("rwl", [P, KC, P], F32R, where=p3)
        lg = sb("lg", [P, NT, GATES], where=p3)
        ex = sb("ex", [P, NT, GATES], where=p3)
        rt = [sb(f"rt{i}", [P, NT, E], where=p3) for i in range(3)]
        rcol = [sb(f"rcol{i}", [P, NT], where=p3) for i in range(2)]
        comb = sb("comb", [P, NT, GATES], where=p3)
        crest = [sb(f"crest{i}", [P, NT, GATES], where=p3) for i in range(2)]
        cpart = sb("cpart", [P, NT, 3, GATES], BF16, where=p3)
        combT = sb("combT", [3 * GATES, B * T], BF16, where=p3)
        sel = sb("sel", [3 * GATES, CH * P], BF16, where=p3)
        enum = sb("enum", [P, E], where=p3)
        p3pre = ExitStack()
        self_ = sb("self_", [3 * GATES, CH * P], where=p3pre)
        lgT = sb("lgT", [GATES, B * T], where=p3pre)
        rwraw = sb("rwraw", [P, KC, P], where=p3pre)
        p3pre.close()
        p3loop = ExitStack()
        act_g = sb("act_g", [P, 2, GT], where=p3loop)
        gu_t = sb("gu_t", [P, 2, GT], where=p3loop)
        hf = sb("hf", [P, 2, GT], where=p3loop)
        hh_ = sb("hh_", [P, 2, GT], F32R, where=p3loop)
        hl_ = sb("hl_", [P, 2, GT], F32R, where=p3loop)
        p3loop.close()
        p3.close()

        bQK, bS = (bank[0], bank[1]), (bank[2], bank[3])
        bT, bZ, bVO = bank[4], (bank[5], bank[7]), bank[6]
        ln_bank = (bank[6], bank[7])
        A_BANKS, KP_BANKS = (0, 1, 3, 4), (2, 0, 5)
        VO_BANKS, ROT_BANKS, F_BANKS = (5, 6, 7, 0), (1, 3, 4, 5), (2, 6)
        ROTS = PAIRS // 2

        x_in = [sem(f"x_in{i}") for i in range(4)]
        y_in = sem("y_in")
        cst_in = sem("cst_in")
        bias_in = sem("bias_in")
        qkraw_in = [sem(f"qkraw_in{i}") for i in range(2)]
        vraw_in = sem("vraw_in")
        oraw_in = sem("oraw_in")
        out_done = sem("out_done")
        consts = sem("consts")
        eps_set = sem("eps_set")
        passed_act, passed_pool, passed_pe, passed_dve = (sem("passed_" + e) for e in ("act", "pool", "pe", "dve"))
        xh_ready = sem("xh_ready")
        xl_ready = sem("xl_ready")
        y_init = sem("y_init")
        w_hi = sem("w_hi")
        wqk_ready = sem("wqk_ready")
        wv_ready = sem("wv_ready")
        wo_ready = sem("wo_ready")
        qk_done = sem("qk_done")
        vmm_done = sem("vmm_done")
        s_done = sem("s_done")
        t_done = sem("t_done")
        pv_done = sem("pv_done")
        wo_done = sem("wo_done")
        qkb_done = sem("qkb_done")
        vcopy_done = sem("vcopy_done")
        exp_done = sem("exp_done")
        ptc_done = sem("ptc_done")
        zh_done = sem("zh_done")
        max_done = sem("max_done")
        ropemul_done = sem("ropemul_done")
        rec_done = sem("rec_done")
        zl_done = sem("zl_done")
        yadd_done = sem("yadd_done")
        norm_done = sem("norm_done")
        rope_done = sem("rope_done")
        stat_done = sem("stat_done")
        mv_done = sem("mv_done")
        aggr_done = sem("aggr_done")
        std_done = sem("std_done")
        rstd_done = sem("rstd_done")
        xn_done = sem("xn_done")
        xt_done = sem("xt_done")
        xth_done = sem("xth_done")
        xtl_done = sem("xtl_done")
        xw_in = sem("xw_in")
        wqr_in = sem("wqr_in")
        table_in = sem("table_in")
        wdqh_done = sem("wdqh_done")
        wdql_done = sem("wdql_done")
        wqrh_done = sem("wqrh_done")
        wqrl_done = sem("wqrl_done")
        zero_done = sem("zero_done")
        seg_done = sem("seg_done")
        pen_step = sem("pen_step")
        pre_mm = sem("pre_mm")
        pre_cp = sem("pre_cp")
        ml_done = sem("ml_done")
        kp_lo = sem("kp_lo")
        at_lo = sem("at_lo")
        kr_mm = sem("kr_mm")
        kr_mul = sem("kr_mul")
        kr_done = sem("kr_done")
        raw_in = [sem(f"raw_in{i}") for i in range(RING)]
        misc_in = sem("misc_in")
        rwh_done = sem("rwh_done")
        rwl_done = sem("rwl_done")
        sel_done = sem("sel_done")
        guh_done = sem("guh_done")
        dnh_done = sem("dnh_done")
        wg_ready = sem("wg_ready")
        lgT_mm = sem("lgT_mm")
        lgT_cp = sem("lgT_cp")
        lg_mm = sem("lg_mm")
        lg_cp = sem("lg_cp")
        r_step = sem("r_step")
        r_exp = sem("r_exp")
        comb_mm = sem("comb_mm")
        comb_cp = sem("comb_cp")
        g_done = sem("g_done")
        u_done = sem("u_done")
        k_done = sem("k_done")
        silu_done = sem("silu_done")
        gut_done = sem("gut_done")
        hf_done = sem("hf_done")
        hh_done = sem("hh_done")
        hl_done = sem("hl_done")
        d_done = sem("d_done")
        y3_done = sem("y3_done")
        c_done = sem("c_done")
        vo_mm = sem("vo_mm")
        vo_cp = sem("vo_cp")
        a_done = sem("a_done")
        qch_done = sem("qch_done")
        qcl_done = sem("qcl_done")
        qr_mm = sem("qr_mm")
        rq_done = sem("rq_done")
        swap_cp = sem("swap_cp")
        qr_ready = sem("qr_ready")
        rb_done = sem("rb_done")
        bdh_done = sem("bdh_done")
        bd_ready = sem("bd_ready")
        xs_done = sem("xs_done")
        xmax_done = sem("xmax_done")
        xsub_done = sem("xsub_done")
        xexp_done = sem("xexp_done")
        xsum_done = sem("xsum_done")
        xrec_done = sem("xrec_done")
        xp_ready = sem("xp_ready")
        e_done = sem("e_done")
        pt_cp = sem("pt_cp")
        f_done = sem("f_done")
        y2_done = sem("y2_done")


        QK, ROT, SC, NORM, TR, PV, ZLO, WO, ADD = 8, 7, 6, 5, 4, 3, 2, 1, 0

        def attention(eng, step):
            for s in range(-QK, 0):
                step(0, 0, s, 0, UNITS)
            with eng.Fori(0, PAIRS - 1) as pair:
                base = pair * UNITS
                for s in range(UNITS):
                    step(base, pair, s, 0, 2 * UNITS)
            for s in range(UNITS):
                step((PAIRS - 1) * UNITS, PAIRS - 1, s, 0, UNITS)

        def where(k):
            return k // UNITS, k % UNITS // B, k % B

        LN_GROUP = 512 // D

        def phase_one_over(eng):
            eng.wait_ge(wo_done, PAIRS * B + 8)
            eng.wait_ge(yadd_done, PAIRS * B + 1)
            eng.wait_ge(rope_done, PAIRS * UNITS)
            eng.wait_ge(zh_done, PAIRS * UNITS)

        def ln_act_std(act, n):
            act.wait_ge(mv_done, NT * (n + 1))
            act.activation(ln_std[:, :], ln_mv[:, :, 1], ACT.Sqrt, bias=eps_t[:, 0:1]).then_inc(std_done, 1)

        def ln_act_hi(act, n, lo=0, hi=B):
            for g in range(lo, hi):
                act.wait_ge(xt_done, B * n + g + 1)
                act.activation(xh[:, :, g * T:(g + 1) * T], ln_bank[g % 2][:, :], ACT.Copy).then_inc(xth_done, 1)

        def ln_dve_normalise(dve, n, lo=0, hi=NT):
            if lo == 0:
                dve.wait_ge(std_done, n + 1)
                dve.reciprocal(ln_rstd[:, :], ln_std[:, :]).then_inc(rstd_done, 1)
                dve.wait_ge(rstd_done, n + 1)
            for i in range(lo, hi):
                dve.tensor_scalar(y[:, i, :], y[:, i, :], ln_mv[:, i, 0:1], ln_rstd[:, i:i + 1], ALU.subtract,
                                  ALU.mult).then_inc(xn_done, 1)

        def ln_dve_lo(dve, n, lo=0, hi=B):
            for g in range(lo, hi):
                dve.wait_ge(xth_done, B * n + g + 1)
                cols = slice(g * T, (g + 1) * T)
                dve.tensor_tensor(xl[:, :, cols], ln_bank[g % 2][:, :], xh[:, :, cols].bitcast(F32),
                                  ALU.subtract).then_inc(xtl_done, 1)

        def ln_pe_transpose(pe, n, lo=0, hi=B):
            for g in range(lo, hi):
                if g >= 2:
                    pe.wait_ge(xtl_done, B * n + g - 1)
                for i in range(TT):
                    pe.wait_ge(xn_done, NT * n + g * TT + i + 1)
                    for c in range(KC):
                        ins = pe.transpose(ln_bank[g % 2][:, c * T + i * P:c * T + (i + 1) * P],
                                           y[:, g * TT + i, c * P:(c + 1) * P], ident[:, :])
                ins.then_inc(xt_done, 1)

        XW = [(wukT[:, :, :], "wukT"), (wuqT[:, :, :], "wuqT"), (wuvT[:, :, :], "wuvT"), (wox[:, :, :], "wox"),
              (ctxT[:, :, :], "ctxT"), (wkvc[:, :, :], "wkvc"), (wkr[:, :, :], "wkr"), (wdq[:, :, :], "wdq"),
              (seg_i[:, :], "seg"), (keys[:, :], "keys"), (xcosK[:, :], "xcosK"), (xsinK[:, :], "xsinK")]

        def cross_prologue(norm, latent, key_space, rotary):
            norm(0)
            key_space(0)
            key_space(1)
            latent()
            norm(1)
            for g in range(2, B):
                key_space(2 * g - 2)
                key_space(2 * g - 1)
                norm(g)
                if g in (3, 5):
                    rotary(g // 2 - 1)
            key_space(H - 2)
            key_space(H - 1)
            rotary(2)
            rotary(3)

        def cross(eng, prologue, body):
            prologue()
            with eng.Fori(0, B - 1) as b:
                body(b, True)
            body(B - 1, False)

        R_STEPS = 24

        def phase_two_over(eng):
            eng.wait_ge(f_done, NT)
            eng.wait_ge(y2_done, NT + 2)
            eng.wait_ge(pt_cp, 2 * NT + 2)

        UP = 2

        def mlp(eng, step, end):
            for s in range(-UP, 0):
                step(0, 0, s, 0, CH)
            for s in range(CH):
                step(0, 0, s, 0, 2 * CH)
            end(0)
            with eng.Fori(1, GROUPS - 1) as g:
                for s in range(CH):
                    step(g * CH, g, s, 0, 2 * CH)
                end(g)
            for s in range(CH):
                step((GROUPS - 1) * CH, GROUPS - 1, s, 0, CH)
            end(GROUPS - 1)

        def rows(c):
            return P if c % CH < CH - 1 else LAST

        def reuse(eng, sem_, base, k):
            if isinstance(base, int) and base + k < 2 and k < CH:
                return
            eng.wait_ge(sem_, base + (k if k % CH == 0 else k - 1))

        block = ctx.enter_context(nc.Block())

        @block.sync
        def _(sp):
            for j in range(4):
                cols = slice(j * 2 * T, (j + 1) * 2 * T)
                sp.dma_start(xraw[:, :, cols], t["xT"][:, :, cols]).then_inc(x_in[j], 16)
                if j == 0:
                    sp.dma_start(qkraw[0][:, :, :], t["wqk"][0]).then_inc(qkraw_in[0], 16)
                    sp.dma_start(cosT[:, :, :], t["cos"]).then_inc(cst_in, 16)
                    sp.dma_start(sinT[:, :, :], t["sin"]).then_inc(cst_in, 16)
                    sp.dma_start(vraw[:, :, :], t["wv"][0]).then_inc(vraw_in, 16)
                    sp.dma_start(qkraw[1][:, :, :], t["wqk"][1]).then_inc(qkraw_in[1], 16)
            sp.dma_start(oraw[:, :, :], t["wo"][0]).then_inc(oraw_in, 16)
            sp.dma_start(y[:, :, :], t["x"]).then_inc(y_in, 16)
            for dst, name in XW:
                sp.dma_start(dst, t[name]).then_inc(xw_in, 16)
            with sp.Fori(0, PAIRS - 1) as pair:
                sp.wait_ge(wqk_ready, pair * 2 + 1)
                sp.dma_start(qkraw[0][:, :, :], t["wqk"][pair * 2 + 2]).then_inc(qkraw_in[0], 16)
                sp.wait_ge(wv_ready, pair + 1)
                sp.dma_start(vraw[:, :, :], t["wv"][pair + 1]).then_inc(vraw_in, 16)
                sp.wait_ge(wqk_ready, pair * 2 + 2)
                sp.dma_start(qkraw[1][:, :, :], t["wqk"][pair * 2 + 3]).then_inc(qkraw_in[1], 16)
                sp.wait_ge(wo_ready, pair + 1)
                sp.dma_start(oraw[:, :, :], t["wo"][pair + 1]).then_inc(oraw_in, 16)
            phase_one_over(sp)
            sp.dma_start(wqr[:, :, :], t["wqr"]).then_inc(wqr_in, 16)
            sp.wait_ge(wqrl_done, 1)
            sp.dma_start(xcosQ[:, :], t["xcosQ"]).then_inc(table_in, 16)
            sp.dma_start(xsinQ[:, :], t["xsinQ"]).then_inc(table_in, 16)
            sp.wait_ge(qr_ready, 1)
            sp.wait_ge(a_done, 1)
            sp.wait_ge(pen_step, 5)
            sp.wait_ge(kr_done, 1)
            for c in range(CH):
                if c >= RING:
                    sp.wait_ge(wg_ready, c - RING + 1)
                sp.dma_start(guraw[:, c % RING, :, :, :], t["wgu"][c]).then_inc(raw_in[c % RING], 16)
                sp.dma_start(dnraw[0:rows(c), c % RING, :], t["wdn"][c, 0:rows(c), :]).then_inc(raw_in[c % RING], 16)
                if c == RING - 1:
                    phase_two_over(sp)
                    sp.dma_start(rwraw[:, :, :], t["rw"]).then_inc(misc_in, 16)
                    sp.dma_start(self_[:, :], t["sel"]).then_inc(misc_in, 16)
                    sp.dma_start(enum[:, :], t["enum"]).then_inc(misc_in, 16)
            for g in range(GROUPS):
                sp.wait_ge(xn_done, 2 * NT + (g + 1) * GTT)
                sp.dma_start(out[:, g * GTT:(g + 1) * GTT, :], y[:, g * GTT:(g + 1) * GTT, :]).then_inc(out_done, 16)
            sp.wait_ge(out_done, 16 * GROUPS)

        @block.gpsimd
        def _(pool):
            splits = [0]

            def split(hi, lo, raw, raw_sem, raw_count, number, ready):
                pool.wait_ge(raw_sem, raw_count)
                pool.sem_inc(passed_pool, 1)
                pool.tensor_copy(hi, raw).then_inc(w_hi, 1)
                pool.wait_ge(w_hi, number + 1)
                pool.tensor_tensor(lo, raw, hi.bitcast(F32), ALU.subtract).then_inc(ready, 1)

            def split_qk(hh, pair, number):
                split(wqkh[hh][:, :, :], wqkl[hh][:, :, :], qkraw[hh][:, :, :], qkraw_in[hh],
                      (pair + 1) * 16, number, wqk_ready)

            def split_v(pair, number):
                split(wvh[:, :, :], wvl[:, :, :], vraw[:, :, :], vraw_in, (pair + 1) * 16, number, wv_ready)

            pool.memset(eps_t[:, :], EPS).then_inc(eps_set, 1)
            split_qk(0, 0, 0)
            split_v(0, 1)

            def step(base, pair, s, lo, hi):
                k = s + ROT
                if lo <= k < hi:
                    pool.wait_ge(ropemul_done, base + (k + 1))
                    if not (isinstance(base, int) and base + k < 2):
                        pool.wait_ge(s_done, base + (k - 1))
                    pool.tensor_tensor(qkr[:, k % 2, :, :], rcos[:, k % 2, :, :], rsin[:, k % 2, :, :],
                                       ALU.add).then_inc(rope_done, 1)
                if s == -4:
                    split_qk(1, 0, 2)
                if s == 0:
                    pool.wait_ge(wo_done, pair * B + 8)
                    split(woh[:, :, :], wol[:, :, :], oraw[:, :, :], oraw_in, (pair + 1) * 16, pair * 4 + 3,
                          wo_ready)
                if s == 1 and hi > UNITS:
                    pool.wait_ge(qk_done, base + B)
                    split_qk(0, pair + 1, pair * 4 + 4)
                if s == 3 and hi > UNITS:
                    pool.wait_ge(vmm_done, pair * B + B)
                    split_v(pair + 1, pair * 4 + 5)
                if s == 9 and hi > UNITS:
                    pool.wait_ge(qk_done, base + 2 * B)
                    split_qk(1, pair + 1, pair * 4 + 6)

            attention(pool, step)

            pool.wait_ge(xw_in, 16 * len(XW))
            pool.tensor_copy(seg[:, :], seg_i[:, :]).then_inc(seg_done, 1)
            phase_one_over(pool)
            pool.tensor_copy(wdqh[:, :, :], wdq[:, :, :]).then_inc(wdqh_done, 1)
            pool.memset(RB[:, :], 0.0)
            pool.memset(BDh[:, :].bitcast(F32), 0.0)
            pool.memset(BDl[:, :].bitcast(F32), 0.0).then_inc(zero_done, 1)
            pool.wait_ge(wdqh_done, 1)
            pool.tensor_tensor(wdql[:, :, :], wdq[:, :, :], wdqh[:, :, :].bitcast(F32), ALU.subtract)\
                .then_inc(wdql_done, 1)
            pool.wait_ge(wqr_in, 16)
            pool.tensor_copy(wqrh[:, :, :], wqr[:, :, :]).then_inc(wqrh_done, 1)
            pool.wait_ge(wqrh_done, 1)
            pool.tensor_tensor(wqrl[:, :, :], wqr[:, :, :], wqrh[:, :, :].bitcast(F32), ALU.subtract)\
                .then_inc(wqrl_done, 1)
            pool.wait_ge(seg_done, 1)
            every_key = keys[:, :].unsqueeze(1).broadcast_to([P, NT, KT])
            every_seg = seg[:, :].unsqueeze(2).broadcast_to([P, NT, KT])
            pool.tensor_tensor(pen[:, :, :], every_key, every_seg, ALU.subtract).then_inc(pen_step, 1)
            pool.wait_ge(kr_mul, 2)
            pool.tensor_tensor(krT[:, :, :], krc[:, :, :], krT[:, :, :], ALU.add).then_inc(kr_done, 1)
            pool.wait_ge(pen_step, 1)
            pool.wait_ge(pre_mm, 5)
            pool.tensor_scalar(pen2[:, :, :], pen[:, :, :], 0.0, None, ALU.is_gt).then_inc(pen_step, 1)
            pool.tensor_scalar(pen[:, :, :], pen[:, :, :], float(-LOOKBACK), None, ALU.is_lt).then_inc(pen_step, 1)
            pool.wait_ge(pen_step, 3)
            pool.tensor_tensor(pen[:, :, :], pen[:, :, :], pen2[:, :, :], ALU.add).then_inc(pen_step, 1)
            pool.wait_ge(pen_step, 4)
            pool.tensor_scalar(pen[:, :, :], pen[:, :, :], NEG, None, ALU.mult).then_inc(pen_step, 1)

            def rotary(b):
                for i in range(ROTS):
                    if isinstance(b, int) and b == 0:
                        pool.wait_ge(pre_mm, 9 + H)
                    pool.wait_ge(rq_done, b * ROTS + (i + 1))
                    pool.tensor_tensor(qrT[:, 2 * i:2 * i + 2, :], rq[:, i % 2, 0, :, :], rq[:, i % 2, 1, :, :], ALU.add)\
                        .then_inc(qr_ready, 1)

            def subtract(b, j):
                pool.wait_ge(xmax_done, 2 * b + (j + 1))
                pool.tensor_tensor(xs[:, j, :, :], xs[:, j, :, :], xmax[:, j, :].unsqueeze(2).broadcast_to([P, H, KT]),
                                   ALU.subtract).then_inc(xsub_done, 1)

            def prologue():
                rotary(0)
                subtract(0, 0)

            def body(b, more):
                subtract(b, 1)
                if more:
                    rotary(b + 1)
                    subtract(b + 1, 0)

            cross(pool, prologue, body)

            phase_two_over(pool)
            pool.wait_ge(misc_in, 48)
            pool.tensor_copy(rwh[:, :, :], rwraw[:, :, :]).then_inc(rwh_done, 1)
            pool.wait_ge(rwh_done, 1)
            pool.tensor_tensor(rwl[:, :, :], rwraw[:, :, :], rwh[:, :, :].bitcast(F32), ALU.subtract)\
                .then_inc(rwl_done, 1)
            for c in range(CH):
                r = rows(c)
                pool.wait_ge(raw_in[c % RING], 32 * (c // RING + 1))
                pool.tensor_copy(guh[:, c, :, :, :], guraw[:, c % RING, :, :, :]).then_inc(guh_done, 1)
                pool.tensor_copy(dnh[0:r, c, :], dnraw[0:r, c % RING, :]).then_inc(dnh_done, 1)
                pool.wait_ge(guh_done, c + 1)
                pool.tensor_tensor(gul[:, c, :, :, :], guraw[:, c % RING, :, :, :], guh[:, c, :, :, :].bitcast(F32),
                                   ALU.subtract)
                pool.wait_ge(dnh_done, c + 1)
                pool.tensor_tensor(dnl[0:r, c, :], dnraw[0:r, c % RING, :], dnh[0:r, c, :].bitcast(F32),
                                   ALU.subtract).then_inc(wg_ready, 1)

        @block.scalar
        def _(act):
            act.dma_start(bqk[:, :], t["bqk"]).then_inc(bias_in, 16)
            act.dma_start(bv[:, :], t["bv"]).then_inc(bias_in, 16)
            act.dma_start(maskf[:, :], t["mask"]).then_inc(cst_in, 16)
            act.dma_start(ident[:, :], t["ident"]).then_inc(cst_in, 16)
            act.dma_start(bo[:, :], t["bo"]).then_inc(cst_in, 16)
            for b in range(B):
                act.wait_ge(x_in[b // 2], 16)
                cols = slice(b * T, (b + 1) * T)
                act.activation(xh[:, :, cols], xraw[:, :, cols], ACT.Copy).then_inc(xh_ready, 1)
                if b == 1:
                    act.wait_ge(bias_in, 32)
            act.wait_ge(cst_in, 80)
            act.activation(identb[:, :], ident[:, :], ACT.Copy).then_inc(consts, 1)
            act.activation(maskb[:, :], maskf[:, :], ACT.Copy).then_inc(consts, 1)

            def step(base, pair, s, lo, hi):
                early = isinstance(base, int) and base == 0
                k = s + QK
                if lo <= k < hi:
                    ahead, hh, b = where(k)
                    act.wait_ge(qk_done, base + (k + 1))
                    if not (early and k < 2):
                        act.wait_ge(ropemul_done, base + (k - 1))
                    act.sem_inc(passed_act, 1)
                    for j in range(2):
                        col = (pair + ahead) * 4 + (2 * hh + j)
                        ins = act.activation(qkb[:, k % 2, j, :], bQK[k % 2][:, j * T:(j + 1) * T], ACT.Identity,
                                             bias=bqk[:, bass.ds(col, 1)])
                    ins.then_inc(qkb_done, 1)
                    if hh == 0:
                        act.wait_ge(vmm_done, (pair + ahead) * B + (b + 1))
                        act.wait_ge(pv_done, base + (ahead * UNITS + b + 1))
                        act.activation(V[:, b, :, :], bVO[:, :], ACT.Copy).then_inc(vcopy_done, 1)
                k = s + SC
                if lo <= k < hi:
                    act.wait_ge(max_done, base + (k + 1))
                    if not (early and k < 4):
                        act.wait_ge(t_done, base + (k - 3))
                    act.activation(prob[:, k % 4, 0:P], bS[k % 2][:, 0:P], ACT.Exp, bias=negmax[:, k % 2, 0:1],
                                   accum_out=psums[:, k % 4, 0:1])
                    act.activation(prob[:, k % 4, P:3 * P], bS[k % 2][:, P:3 * P], ACT.Exp,
                                   bias=negmax[:, k % 2, 1:2], accum_out=psums[:, k % 4, 1:2]).then_inc(exp_done, 1)
                k = s + TR
                if lo <= k < hi:
                    act.wait_ge(t_done, base + (k + 1))
                    act.wait_ge(pv_done, base + (k + 7))
                    act.activation(probT[:, k % 2, :], bT[:, 0:3 * P], ACT.Copy).then_inc(ptc_done, 1)
                k = s + PV
                if lo <= k < hi:
                    ahead, hh, b = where(k)
                    act.wait_ge(pv_done, base + (k + 9))
                    act.wait_ge(wo_done, (pair + ahead) * B + (b + 1))
                    act.sem_inc(passed_act, 1)
                    act.activation(zh[:, hh, b, :], bZ[k % 2][:, 0:T], ACT.Identity,
                                   bias=bv[:, bass.ds((pair + ahead) * 2 + hh, 1)]).then_inc(zh_done, 1)

            attention(act, step)

            phase_one_over(act)
            act.wait_ge(pre_mm, 1)
            act.activation(kvch[:, :], bank[2][:, :], ACT.Copy)
            act.activation(kvc[:, :], bank[2][:, :], ACT.Copy).then_inc(pre_cp, 1)
            for g in range(4):
                act.wait_ge(pre_mm, g + 2)
                act.activation(AT[0:KVC, 4 * g:4 * g + 4, :], bank[A_BANKS[g]][0:KVC, 0:4 * QC], ACT.Copy)\
                    .then_inc(pre_cp, 1)
            ln_act_std(act, 0)
            for g in range(4):
                act.wait_ge(pre_mm, g + 6)
                act.activation(Mh[:, 2 * g:2 * g + 2, :], bank[A_BANKS[g]][:, :], ACT.Copy).then_inc(pre_cp, 1)

            def key_space(h):
                act.wait_ge(pre_mm, h + 10)
                act.activation(KPh[:, :, h, :], bank[KP_BANKS[h % 3]][0:QC, :].rearrange("p (b k) -> p b k", b=B),
                               ACT.Copy).then_inc(pre_cp, 1)

            def latent(b):
                act.wait_ge(a_done, b + 1)
                act.activation(qch[:, :], bank[4][0:QC, 0:T], ACT.Copy).then_inc(qch_done, 1)

            def keys_of(b):
                act.sem_inc(passed_act, 1)
                for i in range(4):
                    r = slice(i * R // 2, (i + 1) * R // 2)
                    ins = act.activation(RB[r, i % 2 * KT:(i % 2 + 1) * KT], krT[r, bass.ds(b, 1), :], ACT.Copy)
                ins.then_inc(rb_done, 1)
                for r in (slice(0, KVC), slice(KVC, P)):
                    ins = act.activation(BDh[r, r], kvc[r, bass.ds(b * KT, KT)], ACT.Copy)
                ins.then_inc(bdh_done, 1)

            def rotary(b, lo, hi):
                for i in range(lo, hi):
                    act.wait_ge(qr_mm, b * ROTS + (i + 1))
                    if not (isinstance(b, int) and b * ROTS + i < 2):
                        act.wait_ge(qr_ready, b * ROTS + (i - 1))
                    src = bank[ROT_BANKS[i]][:, :].rearrange("p (i t) -> p i t", i=2)
                    act.activation(rq[0:R, i % 2, 1, :, :], src[R:P], ACT.Copy)
                    act.activation(rq[R:P, i % 2, 1, :, :], src[0:R], ACT.Copy).then_inc(swap_cp, 1)

            def exp(b, j):
                act.wait_ge(xsub_done, 2 * b + (j + 1))
                act.activation(xs[:, j, :, :], xs[:, j, :, :], ACT.Exp).then_inc(xexp_done, 1)

            def prologue():
                cross_prologue(lambda g: ln_act_hi(act, 0, g, g + 1), lambda: latent(0), key_space,
                               lambda i: rotary(0, i, i + 1))
                act.wait_ge(zero_done, 1)
                act.wait_ge(kr_done, 1)
                keys_of(0)
                exp(0, 0)

            def weighted(b, lo, hi):
                for e in range(lo, hi):
                    act.wait_ge(vo_mm, 4 * b + (e + 1))
                    act.activation(VO[:, 2 * e:2 * e + 2, :], bank[VO_BANKS[e]][:, :], ACT.Copy).then_inc(vo_cp, 1)

            def transposed(b, j):
                for half in range(2):
                    act.wait_ge(e_done, 4 * b + (2 * j + half + 1))
                    act.activation(xpT[:, j, 4 * half:4 * half + 4, :], bank[6 + half][:, :], ACT.Copy)\
                        .then_inc(pt_cp, 1)

            def body(b, more):
                if more:
                    latent(b + 1)
                weighted(b, 0, 2)
                if more:
                    rotary(b + 1, 0, 2)
                weighted(b, 2, 4)
                exp(b, 1)
                transposed(b, 0)
                if more:
                    rotary(b + 1, 2, ROTS)
                    act.wait_ge(bd_ready, b + 1)
                    keys_of(b + 1)
                transposed(b, 1)
                if more:
                    exp(b + 1, 0)

            cross(act, prologue, body)
            ln_act_std(act, 1)
            ln_act_hi(act, 1)

            phase_two_over(act)
            act.wait_ge(misc_in, 48)
            act.activation(sel[:, :], self_[:, :], ACT.Copy).then_inc(sel_done, 1)
            for g in range(GROUPS):
                act.wait_ge(lgT_mm, g + 1)
                act.activation(lgT[:, g * GT:(g + 1) * GT], bank[g][0:GATES, :], ACT.Copy).then_inc(lgT_cp, 1)
            act.wait_ge(lg_mm, 1)
            act.activation(lg[:, :, :], bank[4][:, 0:NT * GATES], ACT.Copy).then_inc(lg_cp, 1)
            act.wait_ge(r_step, 2)
            act.activation(ex[:, :, 0:E], rt[0][:, :, :], ACT.Exp)
            act.activation(ex[:, :, E:GATES], lg[:, :, E:GATES], ACT.Exp, scale=-1.0).then_inc(r_exp, 1)
            for j in range(2):
                act.wait_ge(comb_mm, j + 1)
                act.activation(combT[:, j * 1024:(j + 1) * 1024], bank[5 + j].bitcast(BF16)[0:3 * GATES, :],
                               ACT.Copy).then_inc(comb_cp, 1)

            def step(base, g, s, lo, hi):
                k = s + UP
                if lo <= k < hi:
                    b, r = k % CH % 2, rows(k)
                    act.wait_ge(g_done, base + (k + 1))
                    reuse(act, gut_done, base, k)
                    act.activation(act_g[0:r, b, :], bank[b][0:r, :], ACT.Silu).then_inc(silu_done, 1)
                    act.wait_ge(hf_done, base + (k + 1))
                    reuse(act, d_done, base, k)
                    act.activation(hh_[0:r, b, :], hf[0:r, b, :], ACT.Copy).then_inc(hh_done, 1)
                if s == 4 and not (isinstance(g, int) and g == 0):
                    std(g - 1)

            def std(g):
                act.wait_ge(mv_done, 2 * NT + g * GTT + GTT)
                act.sem_inc(passed_act, 1)
                cols = bass.ds(g * GTT, GTT)
                act.activation(ln_std[:, cols], ln_mv[:, cols, 1], ACT.Sqrt, bias=eps_t[:, 0:1]).then_inc(std_done, 1)

            def end(g):
                if isinstance(g, int) and g == GROUPS - 1:
                    std(g)

            mlp(act, step, end)

        @block.vector
        def _(dve):
            for b in range(B):
                dve.wait_ge(xh_ready, b + 1)
                cols = slice(b * T, (b + 1) * T)
                dve.tensor_tensor(xl[:, :, cols], xraw[:, :, cols], xh[:, :, cols].bitcast(F32),
                                  ALU.subtract).then_inc(xl_ready, 1)
            dve.wait_ge(cst_in, 80)
            dve.sem_inc(yadd_done, 1)

            def step(base, pair, s, lo, hi):
                early = isinstance(base, int) and base == 0
                k = s + ROT
                if lo <= k < hi:
                    dve.wait_ge(qkb_done, base + (k + 1))
                    if not (early and k < 2):
                        dve.wait_ge(rope_done, base + (k - 1))
                    dve.tensor_tensor(rcos[:, k % 2, :, :], qkb[:, k % 2, :, :], cosT[:, :, :], ALU.mult)
                    dve.tensor_tensor(rsin[0:64, k % 2, :, :], qkb[64:P, k % 2, :, :], sinT[64:P, :, :], ALU.mult)
                    dve.tensor_tensor(rsin[64:P, k % 2, :, :], qkb[0:64, k % 2, :, :], sinT[0:64, :, :],
                                      ALU.mult).then_inc(ropemul_done, 1)
                k = s + ADD
                if lo <= k < hi and where(k)[1] == 1:
                    b = where(k)[2]
                    dve.wait_ge(wo_done, pair * B + (b + 9))
                    if early and b == 0:
                        dve.wait_ge(y_init, NT)
                    dve.wait_ge(yadd_done, pair * B + (b + 1))
                    dve.tensor_tensor(y[:, 2 * b:2 * b + 2, :], bVO[:, :], y[:, 2 * b:2 * b + 2, :],
                                      ALU.add).then_inc(yadd_done, 1)
                    if not early and hi == UNITS:
                        dve.wait_ge(yadd_done, pair * B + (b + 2))
                        for i in (2 * b, 2 * b + 1):
                            dve.bn_stats(ln_stats[:, i, :], y[:, i, :]).then_inc(stat_done, 1)
                k = s + ZLO
                if lo <= k < hi:
                    ahead, hh, b = where(k)
                    dve.wait_ge(zh_done, base + (k + 1))
                    dve.scalar_tensor_tensor(zl[:, hh, b, :], bZ[k % 2][:, 0:T],
                                             bv[:, bass.ds((pair + ahead) * 2 + hh, 1)],
                                             zh[:, hh, b, :].bitcast(F32), ALU.add, ALU.subtract).then_inc(zl_done, 1)
                k = s + SC
                if lo <= k < hi:
                    dve.wait_ge(s_done, base + (k + 1))
                    if not (early and k < 2):
                        dve.wait_ge(exp_done, base + (k - 1))
                    dve.tensor_reduce(negmax[:, k % 2, 0:1], bS[k % 2][:, 0:P], AX_X, ALU.max, negate=True)
                    dve.tensor_reduce(negmax[:, k % 2, 1:2], bS[k % 2][:, P:3 * P], AX_X, ALU.max,
                                      negate=True).then_inc(max_done, 1)
                k = s + NORM
                if lo <= k < hi:
                    dve.wait_ge(exp_done, base + (k + 1))
                    dve.reciprocal(prec[:, k % 4, :], psums[:, k % 4, :]).then_inc(rec_done, 1)
                    dve.wait_ge(rec_done, base + (k + 1))
                    dve.tensor_scalar(prob[:, k % 4, 0:P], prob[:, k % 4, 0:P], prec[:, k % 4, 0:1], None, ALU.mult)
                    dve.tensor_scalar(prob[:, k % 4, P:3 * P], prob[:, k % 4, P:3 * P], prec[:, k % 4, 1:2],
                                      None, ALU.mult).then_inc(norm_done, 1)
                if s == -1:
                    dve.wait_ge(y_in, 16)
                    for i in range(NT):
                        dve.tensor_tensor(y[:, i, :], y[:, i, :], bo[:, :], ALU.add).then_inc(y_init, 1)
                    dve.wait_ge(y_init, NT)

            attention(dve, step)
            for i in range(NT):
                dve.wait_ge(stat_done, i + 1)
                dve.bn_aggr(ln_mv[:, i, :], ln_stats[:, i, :]).then_inc(mv_done, 1)
            phase_one_over(dve)
            for g in range(4):
                dve.wait_ge(pre_cp, g + 2)
                dve.tensor_tensor(AT[KVC:P, 4 * g:4 * g + 4, :], bank[A_BANKS[g]][0:KVC, 0:4 * QC],
                                  AT[0:KVC, 4 * g:4 * g + 4, :].bitcast(F32), ALU.subtract).then_inc(at_lo, 1)
            dve.wait_ge(pre_mm, 5)
            dve.tensor_tensor(kvcl[:, :], bank[2][:, :], kvch[:, :].bitcast(F32), ALU.subtract).then_inc(at_lo, 1)
            for j, (dst, table) in enumerate(((krc[:, :, :], xcosK), (krT[:, :, :], xsinK))):
                dve.wait_ge(kr_mm, j + 1)
                dve.tensor_tensor(dst, bank[(5, 7)[j]][:, :].rearrange("p (b k) -> p b k", b=B),
                                  table[:, :].unsqueeze(1).broadcast_to([P, B, KT]), ALU.mult).then_inc(kr_mul, 1)
            ln_dve_normalise(dve, 0, 0, 6)
            for g in range(4):
                dve.wait_ge(pre_cp, g + 6)
                dve.tensor_tensor(Ml[:, 2 * g:2 * g + 2, :], bank[A_BANKS[g]][:, :], Mh[:, 2 * g:2 * g + 2, :].bitcast(F32),
                                  ALU.subtract).then_inc(ml_done, 1)
            dve.sem_inc(y2_done, 2)

            def first_norm(g):
                if g < B - 3:
                    ln_dve_normalise(dve, 0, 2 * g + 6, 2 * g + 8)
                ln_dve_lo(dve, 0, g, g + 1)

            def key_space(h):
                dve.wait_ge(pre_cp, h + 10)
                dve.tensor_tensor(KPl[:, :, h, :], bank[KP_BANKS[h % 3]][0:QC, :].rearrange("p (b k) -> p b k", b=B),
                                  KPh[:, :, h, :].bitcast(F32), ALU.subtract).then_inc(kp_lo, 1)

            def latent(b):
                dve.wait_ge(qch_done, b + 1)
                dve.tensor_tensor(qcl[:, :], bank[4][0:QC, 0:T], qch[:, :].bitcast(F32), ALU.subtract).then_inc(qcl_done, 1)

            def rotary(b, lo, hi):
                for i in range(lo, hi):
                    dve.wait_ge(swap_cp, b * ROTS + (i + 1))
                    src = bank[ROT_BANKS[i]][:, :].rearrange("p (i t) -> p i t", i=2)
                    both = lambda table: table[:, :].unsqueeze(1).broadcast_to([P, 2, T])
                    dve.tensor_tensor(rq[:, i % 2, 0, :, :], src, both(xcosQ), ALU.mult)
                    dve.tensor_tensor(rq[:, i % 2, 1, :, :], rq[:, i % 2, 1, :, :], both(xsinQ), ALU.mult)\
                        .then_inc(rq_done, 1)

            def keys_of(b):
                dve.wait_ge(bdh_done, b + 1)
                for r in (slice(0, KVC), slice(KVC, P)):
                    ins = dve.tensor_tensor(BDl[r, r], kvc[r, bass.ds(b * KT, KT)], BDh[r, r].bitcast(F32), ALU.subtract)
                ins.then_inc(bd_ready, 1)

            def softmax_in(b, j):
                n = 2 * b + (j + 1)
                dve.wait_ge(c_done, n)
                for half in range(2):
                    dve.scalar_tensor_tensor(xs[:, j, 8 * half:8 * half + 8, :],
                                             bank[2 * j + half][:, :].rearrange("p (h k) -> p h k", h=8), XSCALE,
                                             pen[:, bass.ds(2 * b + j, 1), :].broadcast_to([P, 8, KT]),
                                             ALU.mult, ALU.add).then_inc(xs_done, 1)

            def maxima(b, j):
                dve.wait_ge(xs_done, 4 * b + (2 * j + 2))
                dve.tensor_reduce(xmax[:, j, :], xs[:, j, :, :], AX_X, ALU.max).then_inc(xmax_done, 1)

            def softmax_out(b, j):
                n = 2 * b + (j + 1)
                dve.wait_ge(xexp_done, n)
                dve.tensor_reduce(xsum[:, j, :], xs[:, j, :, :], AX_X, ALU.add).then_inc(xsum_done, 1)
                dve.wait_ge(xsum_done, n)
                dve.reciprocal(xrec[:, j, :], xsum[:, j, :]).then_inc(xrec_done, 1)
                dve.wait_ge(xrec_done, n)
                dve.tensor_tensor(xs[:, j, :, :], xs[:, j, :, :], xrec[:, j, :].unsqueeze(2).broadcast_to([P, H, KT]),
                                  ALU.mult).then_inc(xp_ready, 1)

            def add(b, j):
                dve.wait_ge(f_done, 2 * b + (j + 1))
                rows = y[:, bass.ds(2 * b + j, 1), :]
                dve.tensor_tensor(rows, bank[F_BANKS[j]][:, 0:D], rows, ALU.add).then_inc(y2_done, 1)

            def stats(b):
                for j in range(TT):
                    dve.wait_ge(y2_done, 2 * b + (j + 3))
                    dve.sem_inc(passed_dve, 1)
                    dve.bn_stats(ln_stats[:, j, :], y[:, bass.ds(2 * b + j, 1), :]).then_inc(stat_done, 1)
                dve.wait_ge(stat_done, NT + 2 * b + 2)
                dve.sem_inc(passed_dve, 1)
                for j in range(TT):
                    ins = dve.bn_aggr(mv_tile[:, j, :], ln_stats[:, j, :])
                ins.then_inc(aggr_done, 1)
                dve.wait_ge(aggr_done, b + 1)
                dve.tensor_copy(ln_mv[:, bass.ds(2 * b, 2), :], mv_tile[:, 0:2, :]).then_inc(mv_done, 2)

            def prologue():
                dve.wait_ge(table_in, 32)
                cross_prologue(first_norm, lambda: latent(0), key_space,
                               lambda i: rotary(0, i, i + 1))
                keys_of(0)
                dve.wait_ge(pen_step, 5)
                softmax_in(0, 0)
                maxima(0, 0)

            def body(b, more):
                softmax_in(b, 1)
                if more:
                    latent(b + 1)
                maxima(b, 1)
                softmax_out(b, 0)
                if more:
                    rotary(b + 1, 0, 2)
                softmax_out(b, 1)
                if more:
                    rotary(b + 1, 2, ROTS)
                    keys_of(b + 1)
                add(b, 0)
                if more:
                    softmax_in(b + 1, 0)
                    maxima(b + 1, 0)
                add(b, 1)
                stats(b)

            cross(dve, prologue, body)
            ln_dve_normalise(dve, 1)
            ln_dve_lo(dve, 1)

            count = [0]

            def then(ins):
                count[0] += 1
                ins.then_inc(r_step, 1)
                dve.wait_ge(r_step, count[0])

            wide = [P, NT, E]
            bc = lambda a: a.unsqueeze(2).broadcast_to(wide)
            enum_b = enum[:, :].unsqueeze(1).broadcast_to(wide)
            logit = lg[:, :, 0:E]
            dve.wait_ge(lg_cp, 1)
            dve.wait_ge(misc_in, 48)
            then(dve.tensor_reduce(rcol[0][:, :], logit, AX_X, ALU.max))
            then(dve.tensor_tensor(rt[0][:, :, :], logit, bc(rcol[0][:, :]), ALU.subtract))
            then(dve.tensor_scalar(rt[1][:, :, :], rt[0][:, :, :], 0.0, float(E), ALU.is_lt, ALU.mult))
            then(dve.tensor_tensor(rt[1][:, :, :], rt[1][:, :, :], enum_b, ALU.add))
            then(dve.tensor_reduce(rcol[0][:, :], rt[1][:, :, :], AX_X, ALU.min))
            then(dve.tensor_tensor(rt[1][:, :, :], enum_b, bc(rcol[0][:, :]), ALU.is_equal))
            then(dve.scalar_tensor_tensor(rt[2][:, :, :], rt[1][:, :, :], -BIG, logit, ALU.mult, ALU.add))
            then(dve.tensor_reduce(rcol[0][:, :], rt[2][:, :, :], AX_X, ALU.max))
            then(dve.tensor_tensor(rt[2][:, :, :], rt[2][:, :, :], bc(rcol[0][:, :]), ALU.is_lt))
            then(dve.scalar_tensor_tensor(rt[2][:, :, :], rt[2][:, :, :], float(E), enum_b, ALU.mult, ALU.add))
            then(dve.tensor_reduce(rcol[0][:, :], rt[2][:, :, :], AX_X, ALU.min))
            then(dve.tensor_tensor(rt[2][:, :, :], enum_b, bc(rcol[0][:, :]), ALU.is_equal))
            then(dve.tensor_tensor(rt[2][:, :, :], rt[2][:, :, :], rt[1][:, :, :], ALU.add))
            dve.wait_ge(r_exp, 1)
            then(dve.tensor_tensor(rt[2][:, :, :], rt[2][:, :, :], ex[:, :, 0:E], ALU.mult))
            then(dve.tensor_reduce(rcol[0][:, :], rt[2][:, :, :], AX_X, ALU.add))
            then(dve.reciprocal(rcol[1][:, :], rcol[0][:, :]))
            then(dve.tensor_tensor(comb[:, :, 0:E], rt[2][:, :, :], bc(rcol[1][:, :]), ALU.mult))
            then(dve.tensor_scalar(rcol[0][:, :], ex[:, :, E], 1.0, None, ALU.add))
            then(dve.reciprocal(comb[:, :, E], rcol[0][:, :]))
            then(dve.tensor_copy(cpart[:, :, 0, :], comb[:, :, :]))
            then(dve.tensor_tensor(crest[0][:, :, :], comb[:, :, :], cpart[:, :, 0, :], ALU.subtract))
            then(dve.tensor_copy(cpart[:, :, 1, :], crest[0][:, :, :]))
            then(dve.tensor_tensor(crest[1][:, :, :], crest[0][:, :, :], cpart[:, :, 1, :], ALU.subtract))
            then(dve.tensor_copy(cpart[:, :, 2, :], crest[1][:, :, :]))
            assert count[0] == R_STEPS

            def step(base, g, s, lo, hi):
                k = s + UP
                if lo <= k < hi:
                    b, r = k % CH % 2, rows(k)
                    dve.wait_ge(silu_done, base + (k + 1))
                    dve.wait_ge(u_done, base + (k + 1))
                    dve.tensor_tensor(gu_t[0:r, b, :], bank[2 + b][0:r, :], act_g[0:r, b, :], ALU.mult).then_inc(gut_done, 1)
                    dve.wait_ge(gut_done, base + (k + 1))
                    dve.wait_ge(k_done, base + (k + 1))
                    reuse(dve, hh_done, base, k)
                    dve.tensor_tensor(hf[0:r, b, :], bank[4 + b][0:r, :], gu_t[0:r, b, :], ALU.mult).then_inc(hf_done, 1)
                    dve.wait_ge(hh_done, base + (k + 1))
                    dve.tensor_tensor(hl_[0:r, b, :], hf[0:r, b, :], hh_[0:r, b, :].bitcast(F32),
                                      ALU.subtract).then_inc(hl_done, 1)
                if s == 5 and not (isinstance(g, int) and g == 0):
                    normalise(g - 1)

            def normalise(g):
                dve.wait_ge(std_done, g + 3)
                dve.reciprocal(ln_rstd[:, bass.ds(g * GTT, GTT)], ln_std[:, bass.ds(g * GTT, GTT)]).then_inc(rstd_done, 1)
                dve.wait_ge(rstd_done, g + 3)
                for i in range(GTT):
                    rows_ = y[:, bass.ds(g * GTT + i, 1), :]
                    dve.tensor_scalar(rows_, rows_, ln_mv[:, bass.ds(g * GTT + i, 1), 0],
                                      ln_rstd[:, bass.ds(g * GTT + i, 1)], ALU.subtract, ALU.mult).then_inc(xn_done, 1)

            def end(g):
                dve.wait_ge(d_done, g * CH + CH)
                for j in range(2):
                    part = y[:, bass.ds(g * GTT + 2 * j, 2), :]
                    dve.tensor_tensor(part, bank[6 + j][:, :], part, ALU.add).then_inc(y3_done, 1)
                dve.wait_ge(y3_done, g * 2 + 2)
                dve.sem_inc(passed_dve, 1)
                for i in range(GTT):
                    dve.bn_stats(ln_stats[:, i, :], y[:, bass.ds(g * GTT + i, 1), :]).then_inc(stat_done, 1)
                dve.wait_ge(stat_done, 2 * NT + g * GTT + GTT)
                dve.sem_inc(passed_dve, 1)
                for i in range(GTT):
                    ins = dve.bn_aggr(mv_tile[:, i, :], ln_stats[:, i, :])
                ins.then_inc(aggr_done, 1)
                dve.wait_ge(aggr_done, B + g + 1)
                dve.tensor_copy(ln_mv[:, bass.ds(g * GTT, GTT), :], mv_tile[:, :, :]).then_inc(mv_done, GTT)
                if isinstance(g, int) and g == GROUPS - 1:
                    normalise(g)

            mlp(dve, step, end)

        @block.tensor
        def _(pe):
            pe.wait_ge(consts, 2)
            pe.sem_inc(pv_done, 8)
            pe.sem_inc(wo_done, 8)

            def three_pass(dst, lh, ll, rh, rl, first, last):
                pe.matmul(dst, lh, rh, start=first, stop=False)
                pe.matmul(dst, ll, rh, start=False, stop=False)
                return pe.matmul(dst, lh, rl, start=False, stop=last)

            def step(base, pair, s, lo, hi):
                early = isinstance(base, int) and base == 0
                k = s + SC
                if lo <= k < hi:
                    pe.wait_ge(rope_done, base + (k + 1))
                    if not (early and k < 2):
                        pe.wait_ge(exp_done, base + (k - 1))
                    dst, r = bS[k % 2], qkr[:, k % 2, :, :]
                    pe.matmul(dst[:, 0:P], r[:, 0, 0:P], r[:, 1, 0:P], start=True, stop=False)
                    pe.matmul(dst[:, 0:P], identb[:, :], maskb[:, :], start=False, stop=True)
                    pe.matmul(dst[:, P:3 * P], r[:, 0, P:T], r[:, 1, :], start=True, stop=False)
                    pe.matmul(dst[:, 2 * P:3 * P], identb[:, :], maskb[:, :], start=False, stop=True).then_inc(s_done, 1)
                k = s + QK
                if lo <= k < hi:
                    ahead, hh, b = where(k)
                    if early and hh == 0 and ahead == 0:
                        pe.wait_ge(xl_ready, b + 1)
                    if b == 0:
                        pe.wait_ge(wqk_ready, pair * 2 + (2 * ahead + hh + 1))
                    if not (early and k < 2):
                        pe.wait_ge(qkb_done, base + (k - 1))
                    cols = slice(b * T, (b + 1) * T)
                    for j in range(2):
                        dst = bQK[k % 2][:, j * T:(j + 1) * T]
                        for c in range(KC):
                            w = slice(j * HD, (j + 1) * HD)
                            ins = three_pass(dst, wqkh[hh][:, c, w], wqkl[hh][:, c, w], xh[:, c, cols], xl[:, c, cols],
                                             c == 0, c == KC - 1)
                    ins.then_inc(qk_done, 1)
                    if hh == 0:
                        if b == 0:
                            pe.wait_ge(wv_ready, pair + (ahead + 1))
                        if not (early and ahead == 0 and b == 0):
                            pe.wait_ge(vcopy_done, (pair + ahead) * B + b)
                        if s > B - 1:
                            pe.wait_ge(yadd_done, pair * B + (s - B + 2))
                        for i in range(TT):
                            rows = slice(b * T + i * P, b * T + (i + 1) * P)
                            for c in range(KC):
                                ins = three_pass(bVO[:, i * 2 * HD:(i + 1) * 2 * HD], xh[:, c, rows], xl[:, c, rows],
                                                 wvh[:, c, :], wvl[:, c, :], c == 0, c == KC - 1)
                        ins.then_inc(vmm_done, 1)
                k = s + TR
                if lo <= k < hi:
                    pe.wait_ge(norm_done, base + (k + 1))
                    if not (early and k < 1):
                        pe.wait_ge(ptc_done, base + k)
                    for i, q in enumerate((0, 1, 2)):
                        ins = pe.transpose(bT[:, i * P:(i + 1) * P], prob[:, k % 4, q * P:(q + 1) * P], ident[:, :])
                    ins.then_inc(t_done, 1)
                k = s + PV
                if lo <= k < hi:
                    ahead, hh, b = where(k)
                    pe.wait_ge(ptc_done, base + (k + 1))
                    if hh == 0:
                        pe.wait_ge(vcopy_done, (pair + ahead) * B + (b + 1))
                    if not (early and k < 2):
                        pe.wait_ge(zl_done, base + (k - 1))
                    dst, w = bZ[k % 2][:, 0:T], slice(hh * HD, (hh + 1) * HD)
                    pe.matmul(dst, V[:, b, 0, w], probT[:, k % 2, 0:2 * P], start=True, stop=False)
                    pe.matmul(dst[:, P:T], V[:, b, 1, w], probT[:, k % 2, 2 * P:3 * P], start=False,
                              stop=True).then_inc(pv_done, 1)
                k = s + WO
                if lo <= k < hi and where(k)[1] == 1:
                    b = where(k)[2]
                    pe.wait_ge(zl_done, base + (k + 1))
                    if b == 0:
                        pe.wait_ge(wo_ready, pair + 1)
                    pe.wait_ge(yadd_done, pair * B + (b + 1))
                    pe.wait_ge(vcopy_done, pair * B + (B + (s - B + 1 if s >= B and hi > UNITS else 0)))
                    for i in range(TT):
                        rows = slice(i * P, (i + 1) * P)
                        for hh in range(2):
                            ins = three_pass(bVO[:, i * D:(i + 1) * D], zh[:, hh, b, rows], zl[:, hh, b, rows],
                                             woh[:, hh, :], wol[:, hh, :], hh == 0, hh == 1)
                    ins.then_inc(wo_done, 1)

            attention(pe, step)

            pe.wait_ge(xw_in, 16 * len(XW))
            phase_one_over(pe)
            pe.wait_ge(zl_done, PAIRS * UNITS)
            pe.wait_ge(exp_done, PAIRS * UNITS)
            for c in range(KC):
                ins = pe.matmul(bank[2][:, :], wkvc[:, c, :], ctxT[:, c, :], start=c == 0, stop=c == KC - 1)
            ins.then_inc(pre_mm, 1)
            for g in range(4):
                for h in range(4 * g, 4 * g + 4):
                    ins = pe.matmul(bank[A_BANKS[g]][0:KVC, h % 4 * QC:(h % 4 + 1) * QC], wukT[:, h, :], wuqT[:, h, :],
                                    start=True, stop=True)
                ins.then_inc(pre_mm, 1)
            pe.wait_ge(pre_cp, 1)
            for j in range(2):
                pe.matmul(bank[(5, 7)[j]][:, :], wkr[:, j, :], kvc[0:KVC, :], start=True, stop=True).then_inc(kr_mm, 1)
            for g in range(4):
                pe.wait_ge(at_lo, g + 1)
                for h in range(4 * g, 4 * g + 4):
                    ins = pe.matmul(bank[A_BANKS[g]][h % 2 * 64:h % 2 * 64 + 64, h // 2 % 2 * D:(h // 2 % 2 + 1) * D],
                                    wuvT[:, h, :], wox[:, h, :], start=True, stop=True)
                ins.then_inc(pre_mm, 1)

            def key_space(h):
                if h == 0:
                    pe.wait_ge(at_lo, 5)
                if h == 1:
                    pe.wait_ge(ml_done, 1)
                if h >= 3:
                    pe.wait_ge(kp_lo, h - 2)
                dst = bank[KP_BANKS[h % 3]][0:QC, :]
                pe.matmul(dst, AT[:, h, :], kvch[:, :], start=True, stop=False)
                pe.matmul(dst, AT[0:KVC, h, :], kvcl[0:KVC, :], start=False, stop=True).then_inc(pre_mm, 1)

            def latent(b):
                for c in range(KC):
                    ins = three_pass(bank[4][0:QC, 0:T], wdqh[:, c, :], wdql[:, c, :], xh[:, c, bass.ds(b * T, T)],
                                     xl[:, c, bass.ds(b * T, T)], c == 0, c == KC - 1)
                ins.then_inc(a_done, 1)

            def rotary(b, lo, hi):
                for i in range(lo, hi):
                    for j in range(2):
                        ins = three_pass(bank[ROT_BANKS[i]][:, j * T:(j + 1) * T], wqrh[:, 2 * i + j, :],
                                         wqrl[:, 2 * i + j, :], qch[:, :], qcl[:, :], True, True)
                    ins.then_inc(qr_mm, 1)

            def scores(b, j):
                rows = slice(j * P, (j + 1) * P)
                for half in range(2):
                    if j == 0:
                        pe.wait_ge(qr_ready, b * ROTS + (2 * half + 2))
                    if half == 0 and j == 1:
                        pe.wait_ge(y2_done, 2 * b + 1)
                    dst = bank[2 * j + half]
                    keys = (slice(None), bass.ds(b, 1), slice(8 * half, 8 * half + 8), slice(None))
                    for n, (q, k) in enumerate(((qch, KPh), (qcl, KPh), (qch, KPl))):
                        pe.matmul(dst[:, :], q[:, rows], k[keys], start=n == 0, stop=False)
                    pe.wait_ge(rb_done, b + 1)
                    for i in range(4):
                        ins = pe.matmul(dst[:, i * P:(i + 1) * P], qrT[:, 4 * half + i, rows], RB[:, :],
                                        start=False, stop=i == 3)
                ins.then_inc(c_done, 1)

            def transpose(b, j):
                pe.wait_ge(xp_ready, 2 * b + (j + 1))
                for half in range(2):
                    if j == 0:
                        pe.wait_ge(vo_cp, 4 * b + (2 + half))
                    else:
                        pe.wait_ge(pt_cp, 4 * b + (half + 3))
                    for i in range(4):
                        src = xs[:, j, 8 * half + 2 * i:8 * half + 2 * i + 2, :].rearrange("p h k -> p (h k)")
                        ins = pe.transpose(bank[6 + half][:, i * P:(i + 1) * P], src, ident[:, :])
                    ins.then_inc(e_done, 1)

            def output(b, j):
                pe.wait_ge(vo_cp, 4 * b + 4)
                pe.wait_ge(pt_cp, 4 * b + (2 * j + 4))
                for i in range(PAIRS):
                    ins = pe.matmul(bank[F_BANKS[j]][:, 0:D], xpT[:, j, i, :], VO[:, i, :], start=i == 0,
                                    stop=i == PAIRS - 1)
                ins.then_inc(f_done, 1)

            def weighted(b, lo, hi):
                for e in range(lo, hi):
                    if e == 1:
                        pe.wait_ge(y2_done, 2 * b + 2)
                    if e == 3:
                        pe.wait_ge(xs_done, 4 * b + 2)
                    for i in range(2):
                        ins = three_pass(bank[VO_BANKS[e]][:, i * D:(i + 1) * D], BDh[:, :], BDl[:, :],
                                         Mh[:, 2 * e + i, :], Ml[:, 2 * e + i, :], True, True)
                    ins.then_inc(vo_mm, 1)

            def first_norm(g):
                if g == 1:
                    pe.wait_ge(kr_mul, 2)
                ln_pe_transpose(pe, 0, g, g + 1)

            def first_latent():
                pe.wait_ge(wdql_done, 1)
                pe.wait_ge(xtl_done, 1)
                pe.wait_ge(ml_done, 4)
                latent(0)

            def first_rotary(i):
                if i == 3:
                    pe.wait_ge(kp_lo, H)
                if i == 0:
                    pe.wait_ge(qcl_done, 1)
                    pe.wait_ge(wqrl_done, 1)
                rotary(0, i, i + 1)

            def prologue():
                cross_prologue(first_norm, first_latent, key_space, first_rotary)
                pe.sem_inc(pt_cp, 2)
                pe.wait_ge(kp_lo, H)
                pe.wait_ge(xtl_done, B)
                scores(0, 0)
                scores(0, 1)

            def body(b, more):
                if more:
                    latent(b + 1)
                pe.wait_ge(bd_ready, b + 1)
                weighted(b, 0, 2)
                if more:
                    pe.wait_ge(qcl_done, b + 2)
                    pe.wait_ge(xs_done, 4 * b + 4)
                    rotary(b + 1, 0, 2)
                weighted(b, 2, 4)
                if more:
                    rotary(b + 1, 2, 3)
                transpose(b, 0)
                if more:
                    rotary(b + 1, 3, ROTS)
                output(b, 0)
                transpose(b, 1)
                if more:
                    scores(b + 1, 0)
                output(b, 1)
                if more:
                    scores(b + 1, 1)

            cross(pe, prologue, body)

            pe.wait_ge(y2_done, NT + 2)
            ln_pe_transpose(pe, 1)
            pe.wait_ge(xtl_done, 2 * B)
            pe.wait_ge(rwl_done, 1)
            for g in range(GROUPS):
                cols = slice(g * GT, (g + 1) * GT)
                for c in range(KC):
                    ins = three_pass(bank[g][:, :], rwh[:, c, :], rwl[:, c, :], xh[:, c, cols], xl[:, c, cols],
                                     c == 0, c == KC - 1)
                ins.then_inc(lgT_mm, 1)
            for i in range(NT):
                pe.wait_ge(lgT_cp, i // GTT + 1)
                ins = pe.transpose(bank[4][:, i * GATES:(i + 1) * GATES], lgT[:, i * P:(i + 1) * P],
                                   ident[0:GATES, 0:GATES])
            ins.then_inc(lg_mm, 1)

            def combined():
                pe.wait_ge(r_step, R_STEPS)
                for i in range(NT):
                    j, n = i // 8, i % 8
                    ins = pe.transpose(bank[5 + j].bitcast(BF16)[0:3 * GATES, n * P:(n + 1) * P],
                                       cpart[:, i, :, :].rearrange("p a e -> p (a e)"), identb[:, :])
                    if n == 7:
                        ins.then_inc(comb_mm, 1)
                pe.wait_ge(comb_cp, 2)
                pe.wait_ge(sel_done, 1)

            def step(base, g, s, lo, hi):
                k = s + UP
                if lo <= k < hi:
                    c, b, r = k % CH, k % CH % 2, rows(k)
                    cols = bass.ds((g + k // CH) * GT, GT)
                    pe.wait_ge(wg_ready, c + 1)
                    for j, used in ((0, silu_done), (1, gut_done)):
                        reuse(pe, used, base, k)
                        for kc in range(KC):
                            ins = three_pass(bank[2 * j + b][0:P, :], guh[:, c, j, kc, 0:P], gul[:, c, j, kc, 0:P],
                                             xh[:, kc, cols], xl[:, kc, cols], kc == 0, kc == KC - 1)
                        ins.then_inc((g_done, u_done)[j], 1)
                    if isinstance(base, int) and base + k == 0:
                        combined()
                    reuse(pe, hf_done, base, k)
                    pe.sem_inc(passed_pe, 1)
                    pe.matmul(bank[4 + b][:, :], sel[:, c * P:(c + 1) * P], combT[:, cols], start=True, stop=True)\
                        .then_inc(k_done, 1)
                k = s
                if lo <= k < hi:
                    b, r = k % 2, rows(k)
                    pe.wait_ge(hl_done, base + (k + 1))
                    if k == 0 and not (isinstance(g, int) and g == 0):
                        pe.wait_ge(y3_done, g * 2)
                    for i in range(GTT):
                        rs = slice(i * P, (i + 1) * P)
                        dst = bank[6 + i // 2][:, i % 2 * D:(i % 2 + 1) * D]
                        for n, (l, w) in enumerate(((hh_, dnh), (hl_, dnh), (hh_, dnl))):
                            ins = pe.matmul(dst, l[0:r, b, rs], w[0:r, k, :], start=k == 0 and n == 0 and i % 2 == 0,
                                            stop=k == CH - 1 and n == 2, skip_group_check=True)
                    ins.then_inc(d_done, 1)

            mlp(pe, step, lambda g: None)


def rope_tables():
    inv = (1.0 / np.float32(10000.0) ** (np.arange(0, HD, 2, dtype=np.float32) / HD)).astype(np.float32)
    ang = np.outer(np.arange(T, dtype=np.float32), inv).T
    scale = np.float32(HD ** -0.5)
    cos, sin = np.cos(ang), np.sin(ang)
    cos = np.concatenate([cos, cos])
    sin = np.concatenate([sin, -sin])
    return [np.ascontiguousarray(np.stack([a * scale, a], axis=1).astype(np.float32)) for a in (cos, sin)]


def layout(inp):
    n = {k: np.asarray(v) for k, v in inp.items()}
    x = n["x"]
    perm = np.concatenate([np.arange(0, HD, 2), np.arange(1, HD, 2)])
    a = {}
    a["xT"] = x.reshape(B * T, KC, P).transpose(2, 1, 0)
    a["x"] = x.reshape(NT, P, D).transpose(1, 0, 2)
    wq = n["L0_attn_W_Q"][:, :, perm].reshape(H, KC, P, HD)
    wk = n["L0_attn_W_K"][:, :, perm].reshape(H, KC, P, HD)
    a["wqk"] = np.concatenate([wq, wk], axis=3).transpose(0, 2, 1, 3)
    wv = n["L0_attn_W_V"].reshape(PAIRS, 2, KC, P, HD)
    a["wv"] = wv.transpose(0, 3, 2, 1, 4).reshape(PAIRS, P, KC, 2 * HD)
    a["wo"] = n["L0_attn_W_O"].reshape(PAIRS, 2, HD, D).transpose(0, 2, 1, 3)
    a["bqk"] = np.stack([n["L0_attn_b_Q"][:, perm], n["L0_attn_b_K"][:, perm]], axis=1).reshape(2 * H, HD).T
    a["bv"] = n["L0_attn_b_V"].T
    a["bo"] = np.broadcast_to(n["L0_attn_b_O"], (P, D))
    a["cos"], a["sin"] = rope_tables()
    gate = np.concatenate([n["L0_ffn_w_gate"].transpose(1, 0, 2).reshape(D, E * I), n["L0_ffn_sw_gate"]], axis=1)
    up = np.concatenate([n["L0_ffn_w_up"].transpose(1, 0, 2).reshape(D, E * I), n["L0_ffn_sw_up"]], axis=1)
    down = np.concatenate([n["L0_ffn_w_down"].reshape(E * I, D), n["L0_ffn_sw_down"]], axis=0)
    pad = CH * P - (E * I + SI)
    gu = np.pad(np.stack([gate, up]), ((0, 0), (0, 0), (0, pad)))
    a["wgu"] = gu.reshape(2, KC, P, CH, P).transpose(3, 2, 0, 1, 4)
    a["wdn"] = np.pad(down, ((0, pad), (0, 0))).reshape(CH, P, D)
    rw = np.concatenate([n["L0_ffn_router_w"].T, n["L0_ffn_shared_gate_w"][:, None]], axis=1)
    a["rw"] = np.pad(rw, ((0, 0), (0, P - GATES))).reshape(KC, P, P).transpose(1, 0, 2)
    expert = np.minimum(np.arange(CH * P) // I, E)
    a["sel"] = np.tile((expert[None, :] == np.arange(GATES)[:, None]).astype(np.float32), (3, 1))
    a["enum"] = np.broadcast_to(np.arange(E, dtype=np.float32), (P, E))
    swap = np.concatenate([np.arange(R // 2, R), np.arange(0, R // 2)])
    twice = lambda w, axis=-1: np.concatenate([w, w], axis=axis)
    a["wukT"] = n["L0_xattn_W_uk"].reshape(KVC, H, HD).transpose(2, 1, 0)
    a["wuqT"] = n["L0_xattn_W_uq"].reshape(QC, H, HD).transpose(2, 1, 0)
    a["wuvT"] = n["L0_xattn_W_uv"].reshape(KVC, H, HD).transpose(2, 1, 0)
    a["wox"] = n["L0_xattn_W_o"].reshape(H, HD, D).transpose(1, 0, 2)
    a["ctxT"] = n["ctx_2048"].reshape(B * KT, KC, P).transpose(2, 1, 0)
    a["wkvc"] = twice(n["L0_xattn_W_kvc"].reshape(KC, P, KVC).transpose(1, 0, 2))
    wkr = n["L0_xattn_W_kr"]
    halves = np.concatenate([np.arange(R // 2), np.arange(R // 2), np.arange(R // 2, R), np.arange(R // 2, R)])
    a["wkr"] = np.stack([wkr[:, halves], wkr[:, swap][:, halves]], axis=1)
    a["wdq"] = n["L0_xattn_W_dq"].reshape(KC, P, QC).transpose(1, 0, 2)
    wqr = n["L0_xattn_W_qr"].reshape(QC, PAIRS, 2, 2, R // 2)
    a["wqr"] = wqr.transpose(0, 1, 3, 2, 4).reshape(QC, PAIRS, 2 * R)
    a["seg"] = n["itok_BxS_0_1023"].reshape(NT, P).T
    a["keys"] = np.broadcast_to(np.arange(KT, dtype=np.float32), (P, KT))
    for name, count in (("K", KT), ("Q", T)):
        half = R // 2
        inv = (1.0 / np.float32(10000.0) ** (np.arange(half, dtype=np.float32) / half)).astype(np.float32)
        ang = (np.arange(count, dtype=np.float32)[:, None] * inv).T
        a["xcos" + name] = np.tile(np.cos(ang), (4, 1)).astype(np.float32)
        sin = np.tile(np.sin(ang), (2, 1)).astype(np.float32)
        a["xsin" + name] = np.concatenate([-sin, sin])
    a["ident"] = np.eye(P, dtype=np.float32)
    q = np.arange(P)
    a["mask"] = np.where(q[None, :] > q[:, None], np.float32(NEG), np.float32(0))
    return {k: np.ascontiguousarray(v) for k, v in a.items()}


def program(nc, arrays):
    t = {k: nc.dram_tensor("in_" + k, v.shape, mybir.dt.from_np(v.dtype), kind="ExternalInput").ap()
         for k, v in arrays.items()}
    out = nc.dram_tensor("out", (B * T, D), F32, kind="ExternalOutput").ap()
    build(nc, t, out.rearrange("(n p) d -> p n d", p=P))


def kernel(**inputs):
    import concourse.bacc as bacc
    from concourse.bass_utils import run_bass_kernel_spmd
    arrays = layout(inputs)
    nc = bacc.Bacc("TRN2", target_bir_lowering=False, num_devices=1)
    program(nc, arrays)
    r = run_bass_kernel_spmd(nc, [{"in_" + k: v for k, v in arrays.items()}], core_ids=[0])
    return r.results[0]["out"].reshape(B, T, D)
```

```python
from contextlib import ExitStack

import numpy as np

import concourse.bass as bass
from concourse import mybir

ALU = mybir.AluOpType
ACT = mybir.ActivationFunctionType
F32 = mybir.dt.float32
F32R = mybir.dt.float32r
BF16 = mybir.dt.bfloat16
I32 = mybir.dt.int32
AX_X = mybir.AxisListType.X

P = 128
B, T, D = 8, 256, 256
KC = D // P
TT = T // P
NT = B * TT
H, HD = 16, 128
PAIRS = H // 2
UNITS = 2 * B
KT, KVC, QC, R = 64, 64, 96, 64
LOOKBACK = 8
E, I, SI = 8, 176, 704
RW = 16
GATES = E + 1
CH = -(-(E * I + SI) // P)
LAST = E * I + SI - (CH - 1) * P
GT = 512
GROUPS = B * T // GT
GTT = GT // P
H_RING = 3
assert (CH - 1) % H_RING != 0
RING = 4
BIG = 1e30
XSCALE = float(1.0 / np.sqrt(HD + R).astype(np.float32))
EPS = 1e-5
NEG = -1e30


def build(nc, t, out):
    ctx = ExitStack()
    with ctx:
        def sb(name, shape, dt=F32, where=ctx):
            return where.enter_context(nc.sbuf_tensor(name, shape, dt))

        def sem(name):
            return ctx.enter_context(nc.semaphore(name))

        bank = [ctx.enter_context(nc.psum_tensor(f"bank{i}", [P, 512], F32)) for i in range(8)]

        y = sb("y", [P, NT, D])
        xh = sb("xh", [P, KC, B * T], F32R)
        xl = sb("xl", [P, KC, B * T], F32R)
        ident = sb("ident", [P, P])
        ln_stats = sb("ln_stats", [P, NT, 6])
        ln_mv = sb("ln_mv", [P, NT, 2])
        mv_tile = sb("mv_tile", [P, GTT, 2])
        ln_std = sb("ln_std", [P, NT])
        ln_rstd = sb("ln_rstd", [P, NT])
        eps_t = sb("eps_t", [P, 1])
        sqrt_load = sb("sqrt_load", [P, 1])
        identb = sb("identb", [P, P], BF16)
        rwraw = sb("rwraw", [P, KC, RW])
        rwh = sb("rwh", [P, KC, RW], F32R)
        rwl = sb("rwl", [P, KC, RW], F32R)
        enum = sb("enum", [P, E])

        p0 = ExitStack()
        wukT = sb("wukT", [P, H, KVC], where=p0)
        wuqT = sb("wuqT", [P, H, QC], where=p0)
        wuvT = sb("wuvT", [P, H, KVC], where=p0)
        wox = sb("wox", [P, H, D], where=p0)
        ctxT = sb("ctxT", [P, KC, B * KT], where=p0)
        wkvc = sb("wkvc", [P, KC, 2 * KVC], where=p0)
        wkr = sb("wkr", [KVC, 2, 2 * R], where=p0)
        wdq = sb("wdq", [P, KC, QC], where=p0)
        seg_i = sb("seg_i", [P, NT], I32, where=p0)
        seg = sb("seg", [P, NT], where=p0)
        keys = sb("keys", [P, KT], where=p0)
        xcosK = sb("xcosK", [P, KT], where=p0)
        xsinK = sb("xsinK", [P, KT], where=p0)

        p2 = ExitStack()
        wqrh = sb("wqrh", [QC, PAIRS, 2 * R], F32R, where=p2)
        wqrl = sb("wqrl", [QC, PAIRS, 2 * R], F32R, where=p2)
        kvc = sb("kvc", [P, B * KT], where=p2)
        Mh = sb("Mh", [P, PAIRS, D], F32R, where=p2)
        Ml = sb("Ml", [P, PAIRS, D], F32R, where=p2)
        KPh = sb("KPh", [QC, B, H, KT], F32R, where=p2)
        KPl = sb("KPl", [QC, B, H, KT], F32R, where=p2)
        krT = sb("krT", [P, B, KT], where=p2)
        pen = sb("pen", [P, NT, KT], where=p2)
        RB = sb("RB", [P, 2 * KT], where=p2)
        BDh = sb("BDh", [P, 2 * KT], F32R, where=p2)
        BDl = sb("BDl", [P, 2 * KT], F32R, where=p2)
        qch = sb("qch", [QC, T], F32R, where=p2)
        qcl = sb("qcl", [QC, T], F32R, where=p2)
        xmax = sb("xmax", [P, TT, H], where=p2)
        xsum = sb("xsum", [P, TT, H], where=p2)
        xrec = sb("xrec", [P, TT, H], where=p2)
        wdqh = sb("wdqh", [P, KC, QC], F32R, where=p2)
        wdql = sb("wdql", [P, KC, QC], F32R, where=p2)
        p2pre = ExitStack()
        wqr = sb("wqr", [QC, PAIRS, 2 * R], where=p2pre)
        p2pre.close()
        xcosQ = sb("xcosQ", [P, T], where=p2)
        xsinQ = sb("xsinQ", [P, T], where=p2)
        rq = sb("rq", [P, 2, 2, 2, T], where=p2)
        p2key = ExitStack()
        AT = sb("AT", [P, H, QC], F32R, where=p2key)
        kvch = sb("kvch", [P, B * KT], F32R, where=p2key)
        p2key.close()
        qrT = sb("qrT", [P, PAIRS, T], where=p2)
        p2.close()

        p1 = ExitStack()
        xraw = sb("xraw", [P, KC, B * T], where=p1)
        bo = sb("bo", [P, D], where=p1)
        bqk = sb("bqk", [P, H * 2], where=p1)
        bv = sb("bv", [P, H], where=p1)
        cosT = sb("cosT", [P, 2, T], where=p1)
        sinT = sb("sinT", [P, 2, T], where=p1)
        maskb = sb("maskb", [P, P], BF16, where=p1)
        maskf = sb("maskf", [P, P], where=p1)
        qkraw = [sb(f"qkraw{i}", [P, KC, 2 * HD], where=p1) for i in range(2)]
        wqkh = [sb(f"wqkh{i}", [P, KC, 2 * HD], F32R, where=p1) for i in range(2)]
        wqkl = [sb(f"wqkl{i}", [P, KC, 2 * HD], F32R, where=p1) for i in range(2)]
        vraw = sb("vraw", [P, KC, 2 * HD], where=p1)
        wvh = sb("wvh", [P, KC, 2 * HD], F32R, where=p1)
        wvl = sb("wvl", [P, KC, 2 * HD], F32R, where=p1)
        oraw = sb("oraw", [P, 2, D], where=p1)
        woh = sb("woh", [P, 2, D], F32R, where=p1)
        wol = sb("wol", [P, 2, D], F32R, where=p1)
        qkb = sb("qkb", [P, 2, 2, T], where=p1)
        rcos = sb("rcos", [P, 2, 2, T], where=p1)
        rsin = sb("rsin", [P, 2, 2, T], where=p1)
        qkr = sb("qkr", [P, 2, 2, T], where=p1)
        V = sb("V", [P, B, TT, 2 * HD], where=p1)
        prob = sb("prob", [P, 4, 3 * P], where=p1)
        probT = sb("probT", [P, 2, 3 * P], where=p1)
        negmax = sb("negmax", [P, 2, 2], where=p1)
        psums = sb("psums", [P, 4, 2], where=p1)
        prec = sb("prec", [P, 4, 2], where=p1)
        zh = sb("zh", [P, 2, B, T], F32R, where=p1)
        zl = sb("zl", [P, 2, B, T], F32R, where=p1)
        p1.close()
        p0.close()

        p2w = ExitStack()
        kvcl = sb("kvcl", [P, B * KT], F32R, where=p2w)
        krc = sb("krc", [P, B, KT], where=p2w)
        pen2 = sb("pen2", [P, NT, KT], where=p2w)
        p2w.close()

        p3 = ExitStack()
        guraw = sb("guraw", [P, RING, 2, KC, P], where=p3)
        dnraw = sb("dnraw", [P, RING, D], where=p3)
        p3x = ExitStack()
        xs = sb("xs", [P, TT, H, KT], where=p3x)
        xpT = sb("xpT", [P, TT, PAIRS, P], where=p3x)
        VO = sb("VO", [P, PAIRS, D], where=p3x)
        p3x.close()
        guh = sb("guh", [P, CH, 2, KC, P], F32R, where=p3)
        gul = sb("gul", [P, CH, 2, KC, P], F32R, where=p3)
        dnh = sb("dnh", [P, CH, D], F32R, where=p3)
        dnl = sb("dnl", [P, CH, D], F32R, where=p3)
        lg = sb("lg", [P, NT, GATES], where=p3)
        ex = sb("ex", [P, NT, GATES], where=p3)
        rt = [sb(f"rt{i}", [P, NT, E], where=p3) for i in range(3)]
        rcol = [sb(f"rcol{i}", [P, NT], where=p3) for i in range(2)]
        comb = sb("comb", [P, NT, GATES], where=p3)
        crest = [sb(f"crest{i}", [P, NT, GATES], where=p3) for i in range(2)]
        cpart = sb("cpart", [P, NT, 3, GATES], BF16, where=p3)
        combT = sb("combT", [3 * GATES, B * T], BF16, where=p3)
        sel = sb("sel", [3 * GATES, CH * P], BF16, where=p3)
        p3pre = ExitStack()
        lgT = sb("lgT", [RW, B * T], where=p3pre)
        p3pre.close()
        act_g = sb("act_g", [P, 2, GT], where=p3)
        gu_t = sb("gu_t", [P, 2, GT], where=p3)
        hf = sb("hf", [P, 2, GT], where=p3)
        p3sel = ExitStack()
        self_ = sb("self_", [3 * GATES, CH * P], where=p3sel)
        p3sel.close()
        hh_ = sb("hh_", [P, H_RING, GT], F32R, where=p3)
        hl_ = sb("hl_", [P, H_RING, GT], F32R, where=p3)
        p3.close()

        bQK, bS = (bank[0], bank[1]), (bank[2], bank[3])
        bT, bZ, bVO = bank[4], (bank[5], bank[7]), bank[6]
        ln_bank = ((bank[6], bank[7]), (bank[1], bank[3]))
        A_BANKS, M_BANKS, KP_BANKS = (0, 1, 3, 4), (0, 1, 3, 5), (2, 0, 5)
        VO_BANKS, ROT_BANKS, F_BANKS = (5, 6, 7, 0), (1, 3, 4, 5), (2, 6)
        ROTS = PAIRS // 2

        x_in = [sem(f"x_in{i}") for i in range(4)]
        y_in = sem("y_in")
        cst_in = sem("cst_in")
        bias_in = sem("bias_in")
        qkraw_in = [sem(f"qkraw_in{i}") for i in range(2)]
        vraw_in = sem("vraw_in")
        oraw_in = sem("oraw_in")
        out_done = sem("out_done")
        consts = sem("consts")
        eps_set = sem("eps_set")
        passed_act, passed_pool, passed_pe, passed_dve = (sem("passed_" + e) for e in ("act", "pool", "pe", "dve"))
        xh_ready = sem("xh_ready")
        xl_ready = sem("xl_ready")
        y_init = sem("y_init")
        w_hi = sem("w_hi")
        wqk_ready = sem("wqk_ready")
        wv_ready = sem("wv_ready")
        wo_ready = sem("wo_ready")
        qk_done = sem("qk_done")
        vmm_done = sem("vmm_done")
        s_done = sem("s_done")
        t_done = sem("t_done")
        pv_done = sem("pv_done")
        wo_done = sem("wo_done")
        qkb_done = sem("qkb_done")
        vcopy_done = sem("vcopy_done")
        exp_done = sem("exp_done")
        ptc_done = sem("ptc_done")
        zh_done = sem("zh_done")
        max_done = sem("max_done")
        ropemul_done = sem("ropemul_done")
        rec_done = sem("rec_done")
        zl_done = sem("zl_done")
        yadd_done = sem("yadd_done")
        norm_done = sem("norm_done")
        rope_done = sem("rope_done")
        stat_done = sem("stat_done")
        mv_done = sem("mv_done")
        aggr_done = sem("aggr_done")
        std_done = sem("std_done")
        rstd_done = sem("rstd_done")
        xn_done = sem("xn_done")
        xt_done = sem("xt_done")
        xth_done = sem("xth_done")
        xtl_done = sem("xtl_done")
        xw_in = sem("xw_in")
        wqr_in = sem("wqr_in")
        table_in = sem("table_in")
        wdqh_done = sem("wdqh_done")
        wdql_done = sem("wdql_done")
        wqrh_done = sem("wqrh_done")
        wqrl_done = sem("wqrl_done")
        zero_done = sem("zero_done")
        seg_done = sem("seg_done")
        pen_step = sem("pen_step")
        pre_mm = sem("pre_mm")
        pre_cp = sem("pre_cp")
        ml_done = sem("ml_done")
        kp_lo = sem("kp_lo")
        at_lo = sem("at_lo")
        kr_mm = sem("kr_mm")
        kr_mul = sem("kr_mul")
        kr_done = sem("kr_done")
        raw_in = [sem(f"raw_in{i}") for i in range(RING)]
        router_in = sem("router_in")
        sel_in = sem("sel_in")
        rwh_done = sem("rwh_done")
        rwl_done = sem("rwl_done")
        sel_done = sem("sel_done")
        guh_done = sem("guh_done")
        dnh_done = sem("dnh_done")
        wg_ready = sem("wg_ready")
        lgT_mm = sem("lgT_mm")
        lgT_cp = sem("lgT_cp")
        lg_mm = sem("lg_mm")
        lg_cp = sem("lg_cp")
        r_step = sem("r_step")
        r_exp = sem("r_exp")
        comb_mm = sem("comb_mm")
        comb_cp = sem("comb_cp")
        g_done = sem("g_done")
        u_done = sem("u_done")
        k_done = sem("k_done")
        silu_done = sem("silu_done")
        gut_done = sem("gut_done")
        hf_done = sem("hf_done")
        hh_done = sem("hh_done")
        hl_done = sem("hl_done")
        d_done = sem("d_done")
        y3_done = sem("y3_done")
        c_done = sem("c_done")
        vo_mm = sem("vo_mm")
        vo_cp = sem("vo_cp")
        a_done = sem("a_done")
        qch_done = sem("qch_done")
        qcl_done = sem("qcl_done")
        qr_mm = sem("qr_mm")
        rq_done = sem("rq_done")
        swap_cp = sem("swap_cp")
        qr_ready = sem("qr_ready")
        rb_done = sem("rb_done")
        bdh_done = sem("bdh_done")
        bd_ready = sem("bd_ready")
        xs_done = sem("xs_done")
        xmax_done = sem("xmax_done")
        xsub_done = sem("xsub_done")
        xexp_done = sem("xexp_done")
        xsum_done = sem("xsum_done")
        xrec_done = sem("xrec_done")
        xp_ready = sem("xp_ready")
        e_done = sem("e_done")
        pt_cp = sem("pt_cp")
        f_done = sem("f_done")
        y2_done = sem("y2_done")


        QK, ROT, SC, NORM, TR, PV, ZLO, WO, ADD = 8, 7, 6, 5, 4, 3, 2, 1, 0

        BO_STEPS = 6

        def attention(eng, step):
            for s in range(-QK, 0):
                step(0, 0, s, 0, UNITS)
            with eng.Fori(0, PAIRS - 1) as pair:
                base = pair * UNITS
                for s in range(UNITS):
                    step(base, pair, s, 0, 2 * UNITS)
            for s in range(UNITS):
                step((PAIRS - 1) * UNITS, PAIRS - 1, s, 0, UNITS)

        def where(k):
            return k // UNITS, k % UNITS // B, k % B

        LN_GROUP = 512 // D

        def phase_one_over(eng):
            eng.wait_ge(wo_done, PAIRS * B + 8)
            eng.wait_ge(yadd_done, PAIRS * B + 1)
            eng.wait_ge(rope_done, PAIRS * UNITS)
            eng.wait_ge(zh_done, PAIRS * UNITS)

        EARLY = NT - TT

        def ln_act_std(act, n, lo=0, hi=NT):
            act.wait_ge(mv_done, NT * n + hi)
            act.wait_ge(eps_set, 1)
            act.activation(ln_std[:, lo:hi], ln_mv[:, lo:hi, 1], ACT.Sqrt, bias=eps_t[:, 0:1]).then_inc(std_done, 1)

        def ln_act_hi(act, n, lo=0, hi=B):
            for g in range(lo, hi):
                act.wait_ge(xt_done, B * n + g + 1)
                act.activation(xh[:, :, g * T:(g + 1) * T], ln_bank[n][g % 2][:, :], ACT.Copy).then_inc(xth_done, 1)

        def ln_dve_rstd(dve, number, lo=0, hi=NT):
            dve.wait_ge(std_done, number)
            dve.reciprocal(ln_rstd[:, lo:hi], ln_std[:, lo:hi]).then_inc(rstd_done, 1)
            dve.wait_ge(rstd_done, number)

        def ln_dve_normalise(dve, n, lo=0, hi=NT):
            for i in range(lo, hi):
                dve.tensor_scalar(y[:, i, :], y[:, i, :], ln_mv[:, i, 0:1], ln_rstd[:, i:i + 1], ALU.subtract,
                                  ALU.mult).then_inc(xn_done, 1)

        def ln_dve_lo(dve, n, lo=0, hi=B):
            for g in range(lo, hi):
                dve.wait_ge(xth_done, B * n + g + 1)
                cols = slice(g * T, (g + 1) * T)
                dve.tensor_tensor(xl[:, :, cols], ln_bank[n][g % 2][:, :], xh[:, :, cols].bitcast(F32),
                                  ALU.subtract).then_inc(xtl_done, 1)

        def ln_pe_transpose(pe, n, lo=0, hi=B):
            for g in range(lo, hi):
                if g >= 2:
                    pe.wait_ge(xtl_done, B * n + g - 1)
                for i in range(TT):
                    pe.wait_ge(xn_done, NT * n + g * TT + i + 1)
                    for c in range(KC):
                        ins = pe.transpose(ln_bank[n][g % 2][:, c * T + i * P:c * T + (i + 1) * P],
                                           y[:, g * TT + i, c * P:(c + 1) * P], ident[:, :])
                ins.then_inc(xt_done, 1)

        XW = [(wukT[:, :, :], "wukT"), (wuqT[:, :, :], "wuqT"), (wuvT[:, :, :], "wuvT"), (wox[:, :, :], "wox"),
              (ctxT[:, :, :], "ctxT"), (wkvc[:, :, :], "wkvc"), (wkr[:, :, :], "wkr"), (wdq[:, :, :], "wdq"),
              (seg_i[:, :], "seg"), (keys[:, :], "keys"), (xcosK[:, :], "xcosK"), (xsinK[:, :], "xsinK")]

        def cross_prologue(norm, latent, key_space, keys, rotary):
            norm(0)
            key_space(0)
            key_space(1)
            latent()
            norm(1)
            for g in range(2, B):
                key_space(2 * g - 2)
                key_space(2 * g - 1)
                norm(g)
                if g in (2, 4):
                    rotary(g // 2 - 1)
            key_space(H - 2)
            key_space(H - 1)
            keys()
            rotary(2)
            rotary(3)

        def cross(eng, prologue, body):
            prologue()
            with eng.Fori(0, B - 1) as b:
                body(b, True)
            body(B - 1, False)

        R_STEPS = 24
        HT = NT // 2
        LG_BANKS, LGT_BANKS = (5, 4), (0, 2)

        def second_norm(norm, logits, turn, gather):
            norm(2)
            logits(0)
            norm(3)
            norm(4)
            logits(1)
            turn(0)
            norm(5)
            turn(1)
            gather(0)
            norm(6)
            logits(2)
            norm(7)
            turn(2)
            logits(3)
            turn(3)
            gather(1)
        COMBINE = 10

        def phase_two_over(eng):
            eng.wait_ge(f_done, NT)
            eng.wait_ge(y2_done, NT + 2)
            eng.wait_ge(pt_cp, 2 * NT + 2)

        UP = 2
        STD_STEP = GTT + 2

        def mlp(eng, step, end):
            for s in range(-UP, 0):
                step(0, 0, s, 0, CH)
            for s in range(CH):
                step(0, 0, s, 0, 2 * CH)
            end(0)
            with eng.Fori(1, GROUPS - 1) as g:
                for s in range(CH):
                    step(g * CH, g, s, 0, 2 * CH)
                end(g)
            for s in range(CH):
                step((GROUPS - 1) * CH, GROUPS - 1, s, 0, CH)
            end(GROUPS - 1)

        def rows(c):
            return P if c % CH < CH - 1 else LAST

        def reuse(eng, sem_, base, k):
            if isinstance(base, int) and base + k < 2 and k < CH:
                return
            eng.wait_ge(sem_, base + (k if k % CH == 0 else k - 1))

        def reuse_hidden(eng, base, k):
            c = k % CH
            if c >= H_RING:
                before = k - H_RING
            else:
                before = k - c - 1 - (CH - 1 - c) % H_RING
            if isinstance(base, int) and base + before < 0:
                return
            eng.wait_ge(d_done, base + (before + 1))

        block = ctx.enter_context(nc.Block())

        @block.sync
        def _(sp):
            for j in range(4):
                cols = slice(j * 2 * T, (j + 1) * 2 * T)
                sp.dma_start(xraw[:, :, cols], t["xT"][:, :, cols]).then_inc(x_in[j], 16)
                if j == 0:
                    sp.dma_start(qkraw[0][:, :, :], t["wqk"][0]).then_inc(qkraw_in[0], 16)
                    sp.dma_start(cosT[:, :, :], t["cos"]).then_inc(cst_in, 16)
                    sp.dma_start(sinT[:, :, :], t["sin"]).then_inc(cst_in, 16)
                    sp.dma_start(vraw[:, :, :], t["wv"][0]).then_inc(vraw_in, 16)
                    sp.dma_start(qkraw[1][:, :, :], t["wqk"][1]).then_inc(qkraw_in[1], 16)
            sp.dma_start(oraw[:, :, :], t["wo"][0]).then_inc(oraw_in, 16)
            sp.dma_start(y[:, :, :], t["x"]).then_inc(y_in, 16)
            sp.dma_start(rwraw[:, :, :], t["rw"]).then_inc(router_in, 16)
            sp.dma_start(enum[:, :], t["enum"]).then_inc(router_in, 16)
            for dst, name in XW:
                sp.dma_start(dst, t[name]).then_inc(xw_in, 16)
            with sp.Fori(0, PAIRS - 1) as pair:
                sp.wait_ge(wqk_ready, pair * 2 + 1)
                sp.dma_start(qkraw[0][:, :, :], t["wqk"][pair * 2 + 2]).then_inc(qkraw_in[0], 16)
                sp.wait_ge(wv_ready, pair + 1)
                sp.dma_start(vraw[:, :, :], t["wv"][pair + 1]).then_inc(vraw_in, 16)
                sp.wait_ge(wqk_ready, pair * 2 + 2)
                sp.dma_start(qkraw[1][:, :, :], t["wqk"][pair * 2 + 3]).then_inc(qkraw_in[1], 16)
                sp.wait_ge(wo_ready, pair + 1)
                sp.dma_start(oraw[:, :, :], t["wo"][pair + 1]).then_inc(oraw_in, 16)
            phase_one_over(sp)
            sp.dma_start(wqr[:, :, :], t["wqr"]).then_inc(wqr_in, 16)
            sp.wait_ge(wqrl_done, 1)
            sp.dma_start(xcosQ[:, :], t["xcosQ"]).then_inc(table_in, 16)
            sp.dma_start(xsinQ[:, :], t["xsinQ"]).then_inc(table_in, 16)
            sp.wait_ge(qr_ready, 1)
            sp.wait_ge(a_done, 1)
            sp.wait_ge(pen_step, 5)
            sp.wait_ge(kr_done, 1)
            for c in range(CH):
                if c >= RING:
                    sp.wait_ge(wg_ready, c - RING + 1)
                sp.dma_start(guraw[:, c % RING, :, :, :], t["wgu"][c]).then_inc(raw_in[c % RING], 16)
                sp.dma_start(dnraw[0:rows(c), c % RING, :], t["wdn"][c, 0:rows(c), :]).then_inc(raw_in[c % RING], 16)
                if c == RING - 1:
                    phase_two_over(sp)
                    sp.dma_start(self_[:, :], t["sel"]).then_inc(sel_in, 16)
            for g in range(2 * GROUPS):
                rows_ = slice(g * GTT // 2, (g + 1) * GTT // 2)
                sp.wait_ge(xn_done, 2 * NT + rows_.stop)
                sp.dma_start(out[:, rows_, :], y[:, rows_, :]).then_inc(out_done, 16)
            sp.wait_ge(out_done, 16 * 2 * GROUPS)

        @block.gpsimd
        def _(pool):
            def split_lo(hi, lo, raw, number, ready):
                pool.wait_ge(w_hi, number + 1)
                pool.tensor_tensor(lo, raw, hi.bitcast(F32), ALU.subtract).then_inc(ready, 1)

            def split_lo_qk(hh, number):
                split_lo(wqkh[hh][:, :, :], wqkl[hh][:, :, :], qkraw[hh][:, :, :], number, wqk_ready)

            def split_lo_v(number):
                split_lo(wvh[:, :, :], wvl[:, :, :], vraw[:, :, :], number, wv_ready)

            pool.memset(eps_t[:, :], EPS).then_inc(eps_set, 1)
            pool.wait_ge(qkraw_in[0], 16)
            pool.tensor_copy(wqkh[0][:, :, :], qkraw[0][:, :, :]).then_inc(w_hi, 1)
            split_lo_qk(0, 0)
            pool.wait_ge(vraw_in, 16)
            pool.tensor_copy(wvh[:, :, :], vraw[:, :, :]).then_inc(w_hi, 1)
            split_lo_v(1)

            def step(base, pair, s, lo, hi):
                k = s + ROT
                if lo <= k < hi:
                    pool.wait_ge(ropemul_done, base + (k + 1))
                    if not (isinstance(base, int) and base + k < 2):
                        pool.wait_ge(s_done, base + (k - 1))
                    pool.tensor_tensor(qkr[:, k % 2, :, :], rcos[:, k % 2, :, :], rsin[:, k % 2, :, :],
                                       ALU.add).then_inc(rope_done, 1)
                if s == -3:
                    split_lo_qk(1, 2)
                if s == 1:
                    split_lo(woh[:, :, :], wol[:, :, :], oraw[:, :, :], pair * 4 + 3, wo_ready)
                if s == 2 and hi > UNITS:
                    split_lo_qk(0, pair * 4 + 4)
                if s == 4 and hi > UNITS:
                    split_lo_v(pair * 4 + 5)
                if s == 10 and hi > UNITS:
                    split_lo_qk(1, pair * 4 + 6)

            attention(pool, step)

            pool.wait_ge(router_in, 32)
            pool.tensor_copy(rwh[:, :, :], rwraw[:, :, :]).then_inc(rwh_done, 1)
            pool.wait_ge(rwh_done, 1)
            pool.tensor_tensor(rwl[:, :, :], rwraw[:, :, :], rwh[:, :, :].bitcast(F32), ALU.subtract)\
                .then_inc(rwl_done, 1)
            pool.wait_ge(xw_in, 16 * len(XW))
            pool.tensor_copy(seg[:, :], seg_i[:, :]).then_inc(seg_done, 1)
            phase_one_over(pool)
            pool.tensor_copy(wdqh[:, :, :], wdq[:, :, :]).then_inc(wdqh_done, 1)
            pool.memset(RB[:, :], 0.0)
            pool.memset(BDh[:, :].bitcast(F32), 0.0)
            pool.memset(BDl[:, :].bitcast(F32), 0.0).then_inc(zero_done, 1)
            pool.wait_ge(wdqh_done, 1)
            pool.tensor_tensor(wdql[:, :, :], wdq[:, :, :], wdqh[:, :, :].bitcast(F32), ALU.subtract)\
                .then_inc(wdql_done, 1)
            pool.wait_ge(wqr_in, 16)
            pool.tensor_copy(wqrh[:, :, :], wqr[:, :, :]).then_inc(wqrh_done, 1)
            pool.wait_ge(wqrh_done, 1)
            pool.tensor_tensor(wqrl[:, :, :], wqr[:, :, :], wqrh[:, :, :].bitcast(F32), ALU.subtract)\
                .then_inc(wqrl_done, 1)
            pool.wait_ge(seg_done, 1)
            every_key = keys[:, :].unsqueeze(1).broadcast_to([P, NT, KT])
            every_seg = seg[:, :].unsqueeze(2).broadcast_to([P, NT, KT])
            pool.tensor_tensor(pen[:, :, :], every_key, every_seg, ALU.subtract).then_inc(pen_step, 1)
            pool.wait_ge(kr_mul, 2)
            pool.tensor_tensor(krT[:, :, :], krc[:, :, :], krT[:, :, :], ALU.add).then_inc(kr_done, 1)
            pool.wait_ge(pen_step, 1)
            pool.wait_ge(pre_mm, 5)
            pool.tensor_scalar(pen2[:, :, :], pen[:, :, :], 0.0, None, ALU.is_gt).then_inc(pen_step, 1)
            pool.tensor_scalar(pen[:, :, :], pen[:, :, :], float(-LOOKBACK), None, ALU.is_lt).then_inc(pen_step, 1)
            pool.wait_ge(pen_step, 3)
            pool.tensor_tensor(pen[:, :, :], pen[:, :, :], pen2[:, :, :], ALU.add).then_inc(pen_step, 1)
            pool.wait_ge(pen_step, 4)
            pool.tensor_scalar(pen[:, :, :], pen[:, :, :], NEG, None, ALU.mult).then_inc(pen_step, 1)

            def rotary(b):
                for i in range(ROTS - 1):
                    if isinstance(b, int) and b == 0:
                        pool.wait_ge(pre_mm, 9 + H)
                    pool.wait_ge(rq_done, b * ROTS + (i + 1))
                    pool.tensor_tensor(qrT[:, 2 * i:2 * i + 2, :], rq[:, i % 2, 0, :, :], rq[:, i % 2, 1, :, :], ALU.add)\
                        .then_inc(qr_ready, 1)

            def subtract(b, j):
                pool.wait_ge(xmax_done, 2 * b + (j + 1))
                pool.tensor_tensor(xs[:, j, :, :], xs[:, j, :, :], xmax[:, j, :].unsqueeze(2).broadcast_to([P, H, KT]),
                                   ALU.subtract).then_inc(xsub_done, 1)

            def prologue():
                rotary(0)
                subtract(0, 0)

            def body(b, more):
                subtract(b, 1)
                if more:
                    rotary(b + 1)
                    subtract(b + 1, 0)

            cross(pool, prologue, body)

            phase_two_over(pool)
            for c in range(CH):
                r = rows(c)
                pool.wait_ge(guh_done, c + 1)
                pool.tensor_tensor(gul[:, c, :, :, :], guraw[:, c % RING, :, :, :], guh[:, c, :, :, :].bitcast(F32),
                                   ALU.subtract)
                pool.wait_ge(dnh_done, c + 1)
                pool.tensor_tensor(dnl[0:r, c, :], dnraw[0:r, c % RING, :], dnh[0:r, c, :].bitcast(F32),
                                   ALU.subtract).then_inc(wg_ready, 1)

        @block.scalar
        def _(act):
            act.dma_start(bqk[:, :], t["bqk"]).then_inc(bias_in, 16)
            act.dma_start(bv[:, :], t["bv"]).then_inc(bias_in, 16)
            act.dma_start(maskf[:, :], t["mask"]).then_inc(cst_in, 16)
            act.dma_start(ident[:, :], t["ident"]).then_inc(cst_in, 16)
            act.dma_start(bo[:, :], t["bo"]).then_inc(cst_in, 16)
            for b in range(B):
                act.wait_ge(x_in[b // 2], 16)
                cols = slice(b * T, (b + 1) * T)
                act.activation(xh[:, :, cols], xraw[:, :, cols], ACT.Copy).then_inc(xh_ready, 1)
                if b == 1:
                    act.wait_ge(bias_in, 32)
            act.wait_ge(cst_in, 80)
            act.activation(identb[:, :], ident[:, :], ACT.Copy).then_inc(consts, 1)
            act.activation(maskb[:, :], maskf[:, :], ACT.Copy).then_inc(consts, 1)

            def split_w(hi, raw, raw_sem, count):
                act.wait_ge(raw_sem, count)
                act.sem_inc(passed_act, 1)
                act.activation(hi, raw, ACT.Copy).then_inc(w_hi, 1)

            def step(base, pair, s, lo, hi):
                early = isinstance(base, int) and base == 0
                k = s + QK
                if lo <= k < hi:
                    ahead, hh, b = where(k)
                    act.wait_ge(qk_done, base + (k + 1))
                    if not (early and k < 2):
                        act.wait_ge(ropemul_done, base + (k - 1))
                    act.sem_inc(passed_act, 1)
                    for j in range(2):
                        col = (pair + ahead) * 4 + (2 * hh + j)
                        ins = act.activation(qkb[:, k % 2, j, :], bQK[k % 2][:, j * T:(j + 1) * T], ACT.Identity,
                                             bias=bqk[:, bass.ds(col, 1)])
                    ins.then_inc(qkb_done, 1)
                    if hh == 0:
                        act.wait_ge(vmm_done, (pair + ahead) * B + (b + 1))
                        act.wait_ge(pv_done, base + (ahead * UNITS + b + 1))
                        act.activation(V[:, b, :, :], bVO[:, :], ACT.Copy).then_inc(vcopy_done, 1)
                k = s + SC
                if lo <= k < hi:
                    act.wait_ge(max_done, base + (k + 1))
                    if not (early and k < 4):
                        act.wait_ge(t_done, base + (k - 3))
                    act.activation(prob[:, k % 4, 0:P], bS[k % 2][:, 0:P], ACT.Exp, bias=negmax[:, k % 2, 0:1],
                                   accum_out=psums[:, k % 4, 0:1])
                    act.activation(prob[:, k % 4, P:3 * P], bS[k % 2][:, P:3 * P], ACT.Exp,
                                   bias=negmax[:, k % 2, 1:2], accum_out=psums[:, k % 4, 1:2]).then_inc(exp_done, 1)
                k = s + TR
                if lo <= k < hi:
                    act.wait_ge(t_done, base + (k + 1))
                    act.wait_ge(pv_done, base + (k + 7))
                    act.activation(probT[:, k % 2, :], bT[:, 0:3 * P], ACT.Copy).then_inc(ptc_done, 1)
                k = s + PV
                if lo <= k < hi:
                    ahead, hh, b = where(k)
                    act.wait_ge(pv_done, base + (k + 9))
                    act.wait_ge(wo_done, (pair + ahead) * B + (b + 1))
                    act.sem_inc(passed_act, 1)
                    act.activation(zh[:, hh, b, :], bZ[k % 2][:, 0:T], ACT.Identity,
                                   bias=bv[:, bass.ds((pair + ahead) * 2 + hh, 1)]).then_inc(zh_done, 1)
                if s == -4:
                    split_w(wqkh[1][:, :, :], qkraw[1][:, :, :], qkraw_in[1], 16)
                if s == 0:
                    act.wait_ge(wo_done, pair * B + 8)
                    split_w(woh[:, :, :], oraw[:, :, :], oraw_in, (pair + 1) * 16)
                if s == 1 and hi > UNITS:
                    act.wait_ge(qk_done, base + B)
                    split_w(wqkh[0][:, :, :], qkraw[0][:, :, :], qkraw_in[0], (pair + 2) * 16)
                if s == 3 and hi > UNITS:
                    act.wait_ge(vmm_done, pair * B + B)
                    split_w(wvh[:, :, :], vraw[:, :, :], vraw_in, (pair + 2) * 16)
                if s == 9 and hi > UNITS:
                    act.wait_ge(qk_done, base + 2 * B)
                    split_w(wqkh[1][:, :, :], qkraw[1][:, :, :], qkraw_in[1], (pair + 2) * 16)

            attention(act, step)

            phase_one_over(act)
            act.wait_ge(pre_mm, 1)
            act.activation(kvch[:, :], bank[2][:, :], ACT.Copy)
            act.activation(kvc[:, :], bank[2][:, :], ACT.Copy).then_inc(pre_cp, 1)
            for g in range(4):
                act.wait_ge(pre_mm, g + 2)
                act.activation(AT[0:KVC, 4 * g:4 * g + 4, :], bank[A_BANKS[g]][0:KVC, 0:4 * QC], ACT.Copy)\
                    .then_inc(pre_cp, 1)
            ln_act_std(act, 0)
            for g in range(4):
                act.wait_ge(pre_mm, g + 6)
                act.activation(Mh[:, 2 * g:2 * g + 2, :], bank[M_BANKS[g]][:, :], ACT.Copy).then_inc(pre_cp, 1)

            def key_space(h):
                act.wait_ge(pre_mm, h + 10)
                act.activation(KPh[:, :, h, :], bank[KP_BANKS[h % 3]][0:QC, :].rearrange("p (b k) -> p b k", b=B),
                               ACT.Copy).then_inc(pre_cp, 1)

            def latent(b):
                act.wait_ge(a_done, b + 1)
                act.activation(qch[:, :], bank[4][0:QC, 0:T], ACT.Copy).then_inc(qch_done, 1)

            def keys_of(b):
                if isinstance(b, int) and b == 0:
                    act.wait_ge(zero_done, 1)
                    act.wait_ge(kr_done, 1)
                act.sem_inc(passed_act, 1)
                for i in range(4):
                    r = slice(i * R // 2, (i + 1) * R // 2)
                    ins = act.activation(RB[r, i % 2 * KT:(i % 2 + 1) * KT], krT[r, bass.ds(b, 1), :], ACT.Copy)
                ins.then_inc(rb_done, 1)
                for r in (slice(0, KVC), slice(KVC, P)):
                    ins = act.activation(BDh[r, r], kvc[r, bass.ds(b * KT, KT)], ACT.Copy)
                ins.then_inc(bdh_done, 1)

            def rotary(b, lo, hi):
                for i in range(lo, hi):
                    act.wait_ge(qr_mm, b * ROTS + (i + 1))
                    if not (isinstance(b, int) and b * ROTS + i < 2):
                        act.wait_ge(qr_ready, b * ROTS + (i - 1))
                    src = bank[ROT_BANKS[i]][:, :].rearrange("p (i t) -> p i t", i=2)
                    act.activation(rq[0:R, i % 2, 1, :, :], src[R:P], ACT.Copy)
                    act.activation(rq[R:P, i % 2, 1, :, :], src[0:R], ACT.Copy).then_inc(swap_cp, 1)

            def exp(b, j):
                act.wait_ge(xsub_done, 2 * b + (j + 1))
                act.activation(xs[:, j, :, :], xs[:, j, :, :], ACT.Exp).then_inc(xexp_done, 1)

            def prologue():
                cross_prologue(lambda g: ln_act_hi(act, 0, g, g + 1), lambda: latent(0), key_space,
                               lambda: keys_of(0), lambda i: rotary(0, i, i + 1))
                exp(0, 0)

            def weighted(b, lo, hi):
                for e in range(lo, hi):
                    act.wait_ge(vo_mm, 4 * b + (e + 1))
                    act.activation(VO[:, 2 * e:2 * e + 2, :], bank[VO_BANKS[e]][:, :], ACT.Copy).then_inc(vo_cp, 1)

            def transposed(b, j):
                for half in range(2):
                    act.wait_ge(e_done, 4 * b + (2 * j + half + 1))
                    act.activation(xpT[:, j, 4 * half:4 * half + 4, :], bank[6 + half][:, :], ACT.Copy)\
                        .then_inc(pt_cp, 1)

            def body(b, more):
                if more:
                    latent(b + 1)
                weighted(b, 0, 2)
                if more:
                    rotary(b + 1, 0, 2)
                weighted(b, 2, 4)
                exp(b, 1)
                transposed(b, 0)
                if more:
                    rotary(b + 1, 2, ROTS)
                    act.wait_ge(bd_ready, b + 1)
                    keys_of(b + 1)
                else:
                    ln_act_std(act, 1, 0, EARLY)
                transposed(b, 1)
                if more:
                    exp(b + 1, 0)
                else:
                    ln_act_hi(act, 1, 0, 2)

            cross(act, prologue, body)
            ln_act_std(act, 1, EARLY, NT)
            phase_two_over(act)

            def logits(g):
                act.wait_ge(lgT_mm, g + 1)
                act.activation(lgT[:, g * GT:(g + 1) * GT], bank[LGT_BANKS[g % 2]][0:RW, :], ACT.Copy).then_inc(lgT_cp, 1)

            def gather(part):
                act.wait_ge(lg_mm, 2 * part + 2)
                rows_ = slice(part * HT, (part + 1) * HT)
                act.activation(lg[:, rows_, :], bank[LG_BANKS[part]][:, 0:HT * RW]
                               .rearrange("p (n e) -> p n e", e=RW)[:, :, 0:GATES], ACT.Copy).then_inc(lg_cp, 1)
                if part == 0:
                    exps(0)

            def exps(part):
                rows_ = slice(part * HT, (part + 1) * HT)
                act.wait_ge(r_step, part * R_STEPS + 2)
                act.activation(ex[:, rows_, 0:E], rt[0][:, rows_, :], ACT.Exp)
                act.activation(ex[:, rows_, E:GATES], lg[:, rows_, E:GATES], ACT.Exp, scale=-1.0).then_inc(r_exp, 1)

            def combined(part, src):
                act.wait_ge(comb_mm, part + 1)
                act.activation(combT[:, part * HT * P:(part + 1) * HT * P], src.bitcast(BF16)[0:3 * GATES, :],
                               ACT.Copy).then_inc(comb_cp, 1)

            def split_hi(c):
                r = rows(c)
                act.wait_ge(raw_in[c % RING], 32 * (c // RING + 1))
                act.activation(guh[:, c, :, :, :], guraw[:, c % RING, :, :, :], ACT.Copy).then_inc(guh_done, 1)
                act.activation(dnh[0:r, c, :], dnraw[0:r, c % RING, :], ACT.Copy).then_inc(dnh_done, 1)

            AHEAD = RING - 1

            def norm(g):
                ln_act_hi(act, 1, g, g + 1)
                if 2 <= g <= 3:
                    split_hi(g - 2)

            second_norm(norm, logits, lambda g: None, gather)
            act.wait_ge(sel_in, 16)
            act.activation(sel[:, :], self_[:, :], ACT.Copy).then_inc(sel_done, 1)
            split_hi(2)
            combined(0, bank[LG_BANKS[0]])
            exps(1)

            def step(base, g, s, lo, hi):
                k = s + UP
                if lo <= k < hi:
                    b, r = k % CH % 2, rows(k)
                    if isinstance(base, int) and base + k == COMBINE:
                        combined(1, bank[4 + b])
                    act.wait_ge(g_done, base + (k + 1))
                    reuse(act, gut_done, base, k)
                    act.activation(act_g[0:r, b, :], bank[b][0:r, :], ACT.Silu).then_inc(silu_done, 1)
                    act.wait_ge(hf_done, base + (k + 1))
                    reuse_hidden(act, base, k)
                    act.activation(hh_[0:r, k % CH % H_RING, :], hf[0:r, b, :], ACT.Copy).then_inc(hh_done, 1)
                    if isinstance(base, int) and base + k + AHEAD < CH:
                        split_hi(k + AHEAD)
                if s == STD_STEP and not (isinstance(g, int) and g == 0):
                    std(g - 1)

            def std(g):
                act.wait_ge(mv_done, 2 * NT + g * GTT + GTT)
                act.sem_inc(passed_act, 1)
                cols = bass.ds(g * GTT, GTT)
                act.activation(ln_std[:, cols], ln_mv[:, cols, 1], ACT.Sqrt, bias=eps_t[:, 0:1]).then_inc(std_done, 1)

            def end(g):
                if isinstance(g, int) and g == GROUPS - 1:
                    act.activation(sqrt_load[:, :], eps_t[:, :], ACT.Sqrt)
                    std(g)

            mlp(act, step, end)

        @block.vector
        def _(dve):
            for b in range(B):
                dve.wait_ge(xh_ready, b + 1)
                cols = slice(b * T, (b + 1) * T)
                dve.tensor_tensor(xl[:, :, cols], xraw[:, :, cols], xh[:, :, cols].bitcast(F32),
                                  ALU.subtract).then_inc(xl_ready, 1)
            dve.wait_ge(cst_in, 80)
            dve.sem_inc(yadd_done, 1)

            def step(base, pair, s, lo, hi):
                early = isinstance(base, int) and base == 0
                k = s + ROT
                if lo <= k < hi:
                    dve.wait_ge(qkb_done, base + (k + 1))
                    if not (early and k < 2):
                        dve.wait_ge(rope_done, base + (k - 1))
                    dve.tensor_tensor(rcos[:, k % 2, :, :], qkb[:, k % 2, :, :], cosT[:, :, :], ALU.mult)
                    dve.tensor_tensor(rsin[0:64, k % 2, :, :], qkb[64:P, k % 2, :, :], sinT[64:P, :, :], ALU.mult)
                    dve.tensor_tensor(rsin[64:P, k % 2, :, :], qkb[0:64, k % 2, :, :], sinT[0:64, :, :],
                                      ALU.mult).then_inc(ropemul_done, 1)
                k = s + ADD
                if lo <= k < hi and where(k)[1] == 1:
                    b = where(k)[2]
                    dve.wait_ge(wo_done, pair * B + (b + 9))
                    dve.wait_ge(yadd_done, pair * B + (b + 1))
                    dve.tensor_tensor(y[:, 2 * b:2 * b + 2, :], bVO[:, :], y[:, 2 * b:2 * b + 2, :],
                                      ALU.add).then_inc(yadd_done, 1)
                    if not early and hi == UNITS:
                        dve.wait_ge(yadd_done, pair * B + (b + 2))
                        for i in (2 * b, 2 * b + 1):
                            dve.bn_stats(ln_stats[:, i, :], y[:, i, :]).then_inc(stat_done, 1)
                k = s + ZLO
                if lo <= k < hi:
                    ahead, hh, b = where(k)
                    dve.wait_ge(zh_done, base + (k + 1))
                    dve.scalar_tensor_tensor(zl[:, hh, b, :], bZ[k % 2][:, 0:T],
                                             bv[:, bass.ds((pair + ahead) * 2 + hh, 1)],
                                             zh[:, hh, b, :].bitcast(F32), ALU.add, ALU.subtract).then_inc(zl_done, 1)
                k = s + SC
                if lo <= k < hi:
                    dve.wait_ge(s_done, base + (k + 1))
                    if not (early and k < 2):
                        dve.wait_ge(exp_done, base + (k - 1))
                    dve.tensor_reduce(negmax[:, k % 2, 0:1], bS[k % 2][:, 0:P], AX_X, ALU.max, negate=True)
                    dve.tensor_reduce(negmax[:, k % 2, 1:2], bS[k % 2][:, P:3 * P], AX_X, ALU.max,
                                      negate=True).then_inc(max_done, 1)
                k = s + NORM
                if lo <= k < hi:
                    dve.wait_ge(exp_done, base + (k + 1))
                    dve.reciprocal(prec[:, k % 4, :], psums[:, k % 4, :]).then_inc(rec_done, 1)
                    dve.wait_ge(rec_done, base + (k + 1))
                    dve.tensor_scalar(prob[:, k % 4, 0:P], prob[:, k % 4, 0:P], prec[:, k % 4, 0:1], None, ALU.mult)
                    dve.tensor_scalar(prob[:, k % 4, P:3 * P], prob[:, k % 4, P:3 * P], prec[:, k % 4, 1:2],
                                      None, ALU.mult).then_inc(norm_done, 1)
                if -BO_STEPS <= s < 0:
                    dve.wait_ge(y_in, 16)
                    each = -(-NT // BO_STEPS)
                    for i in range((s + BO_STEPS) * each, min(NT, (s + BO_STEPS + 1) * each)):
                        dve.tensor_tensor(y[:, i, :], y[:, i, :], bo[:, :], ALU.add).then_inc(y_init, 1)
                if s == -1:
                    dve.wait_ge(y_init, NT)

            attention(dve, step)
            for i in range(NT):
                dve.wait_ge(stat_done, i + 1)
                dve.bn_aggr(ln_mv[:, i, :], ln_stats[:, i, :]).then_inc(mv_done, 1)
            phase_one_over(dve)
            for g in range(4):
                dve.wait_ge(pre_cp, g + 2)
                dve.tensor_tensor(AT[KVC:P, 4 * g:4 * g + 4, :], bank[A_BANKS[g]][0:KVC, 0:4 * QC],
                                  AT[0:KVC, 4 * g:4 * g + 4, :].bitcast(F32), ALU.subtract).then_inc(at_lo, 1)
            dve.wait_ge(pre_mm, 5)
            dve.tensor_tensor(kvcl[:, :], bank[2][:, :], kvch[:, :].bitcast(F32), ALU.subtract).then_inc(at_lo, 1)
            for j, (dst, table) in enumerate(((krc[:, :, :], xcosK), (krT[:, :, :], xsinK))):
                dve.wait_ge(kr_mm, j + 1)
                dve.tensor_tensor(dst, bank[(5, 7)[j]][:, :].rearrange("p (b k) -> p b k", b=B),
                                  table[:, :].unsqueeze(1).broadcast_to([P, B, KT]), ALU.mult).then_inc(kr_mul, 1)
            ln_dve_rstd(dve, 1)
            ln_dve_normalise(dve, 0, 0, 4)
            for g in range(4):
                dve.wait_ge(pre_cp, g + 6)
                dve.tensor_tensor(Ml[:, 2 * g:2 * g + 2, :], bank[M_BANKS[g]][:, :], Mh[:, 2 * g:2 * g + 2, :].bitcast(F32),
                                  ALU.subtract).then_inc(ml_done, 1)
            dve.sem_inc(y2_done, 2)

            def norm(n, g):
                if g < B - 2:
                    ln_dve_normalise(dve, n, 2 * g + 4, 2 * g + 6)
                ln_dve_lo(dve, n, g, g + 1)

            def key_space(h):
                dve.wait_ge(pre_cp, h + 10)
                dve.tensor_tensor(KPl[:, :, h, :], bank[KP_BANKS[h % 3]][0:QC, :].rearrange("p (b k) -> p b k", b=B),
                                  KPh[:, :, h, :].bitcast(F32), ALU.subtract).then_inc(kp_lo, 1)

            def latent(b):
                dve.wait_ge(qch_done, b + 1)
                dve.tensor_tensor(qcl[:, :], bank[4][0:QC, 0:T], qch[:, :].bitcast(F32), ALU.subtract).then_inc(qcl_done, 1)

            def rotary(b, lo, hi):
                if isinstance(b, int) and b == 0 and lo == 0:
                    dve.wait_ge(table_in, 32)
                for i in range(lo, hi):
                    dve.wait_ge(swap_cp, b * ROTS + (i + 1))
                    src = bank[ROT_BANKS[i]][:, :].rearrange("p (i t) -> p i t", i=2)
                    both = lambda table: table[:, :].unsqueeze(1).broadcast_to([P, 2, T])
                    dve.tensor_tensor(rq[:, i % 2, 0, :, :], src, both(xcosQ), ALU.mult)
                    dve.tensor_tensor(rq[:, i % 2, 1, :, :], rq[:, i % 2, 1, :, :], both(xsinQ), ALU.mult)\
                        .then_inc(rq_done, 1)
                if hi == ROTS:
                    dve.wait_ge(rq_done, (b + 1) * ROTS)
                    dve.tensor_tensor(qrT[:, 2 * i:2 * i + 2, :], rq[:, i % 2, 0, :, :], rq[:, i % 2, 1, :, :], ALU.add)\
                        .then_inc(qr_ready, 1)

            def keys_of(b):
                dve.wait_ge(bdh_done, b + 1)
                for r in (slice(0, KVC), slice(KVC, P)):
                    ins = dve.tensor_tensor(BDl[r, r], kvc[r, bass.ds(b * KT, KT)], BDh[r, r].bitcast(F32), ALU.subtract)
                ins.then_inc(bd_ready, 1)

            def softmax_in(b, j):
                n = 2 * b + (j + 1)
                dve.wait_ge(c_done, n)
                for half in range(2):
                    dve.scalar_tensor_tensor(xs[:, j, 8 * half:8 * half + 8, :],
                                             bank[2 * j + half][:, :].rearrange("p (h k) -> p h k", h=8), XSCALE,
                                             pen[:, bass.ds(2 * b + j, 1), :].broadcast_to([P, 8, KT]),
                                             ALU.mult, ALU.add).then_inc(xs_done, 1)

            def maxima(b, j):
                dve.wait_ge(xs_done, 4 * b + (2 * j + 2))
                dve.tensor_reduce(xmax[:, j, :], xs[:, j, :, :], AX_X, ALU.max).then_inc(xmax_done, 1)

            def softmax_out(b, j):
                n = 2 * b + (j + 1)
                dve.wait_ge(xexp_done, n)
                dve.tensor_reduce(xsum[:, j, :], xs[:, j, :, :], AX_X, ALU.add).then_inc(xsum_done, 1)
                dve.wait_ge(xsum_done, n)
                dve.reciprocal(xrec[:, j, :], xsum[:, j, :]).then_inc(xrec_done, 1)
                dve.wait_ge(xrec_done, n)
                dve.tensor_tensor(xs[:, j, :, :], xs[:, j, :, :], xrec[:, j, :].unsqueeze(2).broadcast_to([P, H, KT]),
                                  ALU.mult).then_inc(xp_ready, 1)

            def add(b, j):
                dve.wait_ge(f_done, 2 * b + (j + 1))
                rows = y[:, bass.ds(2 * b + j, 1), :]
                dve.tensor_tensor(rows, bank[F_BANKS[j]][:, 0:D], rows, ALU.add).then_inc(y2_done, 1)

            def stats(b):
                for j in range(TT):
                    dve.wait_ge(y2_done, 2 * b + (j + 3))
                    dve.sem_inc(passed_dve, 1)
                    dve.bn_stats(ln_stats[:, j, :], y[:, bass.ds(2 * b + j, 1), :]).then_inc(stat_done, 1)
                dve.wait_ge(stat_done, NT + 2 * b + 2)
                dve.sem_inc(passed_dve, 1)
                for j in range(TT):
                    ins = dve.bn_aggr(mv_tile[:, j, :], ln_stats[:, j, :])
                ins.then_inc(aggr_done, 1)
                dve.wait_ge(aggr_done, b + 1)
                dve.tensor_copy(ln_mv[:, bass.ds(2 * b, 2), :], mv_tile[:, 0:2, :]).then_inc(mv_done, 2)

            def prologue():
                cross_prologue(lambda g: norm(0, g), lambda: latent(0), key_space,
                               lambda: keys_of(0), lambda i: rotary(0, i, i + 1))
                dve.wait_ge(pen_step, 5)
                softmax_in(0, 0)
                maxima(0, 0)

            def body(b, more):
                softmax_in(b, 1)
                if more:
                    latent(b + 1)
                maxima(b, 1)
                softmax_out(b, 0)
                if more:
                    rotary(b + 1, 0, 2)
                softmax_out(b, 1)
                if more:
                    rotary(b + 1, 2, ROTS)
                    keys_of(b + 1)
                else:
                    ln_dve_rstd(dve, 2, 0, EARLY)
                    ln_dve_normalise(dve, 1, 0, 8)
                add(b, 0)
                if more:
                    softmax_in(b + 1, 0)
                    maxima(b + 1, 0)
                else:
                    ln_dve_lo(dve, 1, 0, 2)
                    ln_dve_normalise(dve, 1, 8, 12)
                add(b, 1)
                stats(b)

            cross(dve, prologue, body)

            count = [0]

            def then(ins):
                count[0] += 1
                ins.then_inc(r_step, 1)
                dve.wait_ge(r_step, count[0])

            wide = [P, HT, E]
            bc = lambda a: a.unsqueeze(2).broadcast_to(wide)
            enum_b = enum[:, :].unsqueeze(1).broadcast_to(wide)

            def half(part, *arrays):
                return [a[:, part * HT:(part + 1) * HT] for a in arrays]

            def route_maxima(part):
                l, r0, col = half(part, lg, rt[0], rcol[0])
                dve.wait_ge(lg_cp, part + 1)
                then(dve.tensor_reduce(col, l[:, :, 0:E], AX_X, ALU.max))
                then(dve.tensor_tensor(r0, l[:, :, 0:E], bc(col), ALU.subtract))

            def route_first(part):
                r0, r1, col = half(part, rt[0], rt[1], rcol[0])
                then(dve.tensor_scalar(r1, r0, 0.0, float(E), ALU.is_lt, ALU.mult))
                then(dve.tensor_tensor(r1, r1, enum_b, ALU.add))
                then(dve.tensor_reduce(col, r1, AX_X, ALU.min))
                then(dve.tensor_tensor(r1, enum_b, bc(col), ALU.is_equal))

            def route_second(part):
                l, r1, r2, col = half(part, lg, rt[1], rt[2], rcol[0])
                then(dve.scalar_tensor_tensor(r2, r1, -BIG, l[:, :, 0:E], ALU.mult, ALU.add))
                then(dve.tensor_reduce(col, r2, AX_X, ALU.max))
                then(dve.tensor_tensor(r2, r2, bc(col), ALU.is_lt))
                then(dve.scalar_tensor_tensor(r2, r2, float(E), enum_b, ALU.mult, ALU.add))
                then(dve.tensor_reduce(col, r2, AX_X, ALU.min))
                then(dve.tensor_tensor(r2, enum_b, bc(col), ALU.is_equal))
                then(dve.tensor_tensor(r2, r2, r1, ALU.add))

            def route_weights(part):
                r2, x, w, col, inv = half(part, rt[2], ex, comb, rcol[0], rcol[1])
                dve.wait_ge(r_exp, part + 1)
                then(dve.tensor_tensor(r2, r2, x[:, :, 0:E], ALU.mult))
                then(dve.tensor_reduce(col, r2, AX_X, ALU.add))
                then(dve.reciprocal(inv, col))
                then(dve.tensor_tensor(w[:, :, 0:E], r2, bc(inv), ALU.mult))
                then(dve.tensor_scalar(col, x[:, :, E], 1.0, None, ALU.add))
                then(dve.reciprocal(w[:, :, E], col))

            def route_parts(part):
                w, c0, c1, parts = half(part, comb, crest[0], crest[1], cpart)
                then(dve.tensor_copy(parts[:, :, 0, :], w))
                then(dve.tensor_tensor(c0, w, parts[:, :, 0, :], ALU.subtract))
                then(dve.tensor_copy(parts[:, :, 1, :], c0))
                then(dve.tensor_tensor(c1, c0, parts[:, :, 1, :], ALU.subtract))
                then(dve.tensor_copy(parts[:, :, 2, :], c1))

            def gather(part):
                if part == 0:
                    dve.wait_ge(router_in, 32)
                    route_maxima(0)

            def logits(g):
                if g == 2:
                    route_first(0)

            def turn(g):
                if g == 2:
                    route_second(0)

            def second(g):
                if g == 3:
                    ln_dve_normalise(dve, 1, 12, EARLY)
                    ln_dve_rstd(dve, 3, EARLY, NT)
                    ln_dve_normalise(dve, 1, EARLY, NT)
                ln_dve_lo(dve, 1, g, g + 1)

            second_norm(second, logits, turn, gather)
            route_weights(0)
            route_parts(0)
            assert count[0] == R_STEPS
            route_maxima(1)

            def step(base, g, s, lo, hi):
                if s == CH - 1:
                    add_group(g)
                k = s + UP
                if lo <= k < hi:
                    b, r = k % CH % 2, rows(k)
                    dve.wait_ge(silu_done, base + (k + 1))
                    dve.wait_ge(u_done, base + (k + 1))
                    dve.tensor_tensor(gu_t[0:r, b, :], bank[2 + b][0:r, :], act_g[0:r, b, :], ALU.mult).then_inc(gut_done, 1)
                    dve.wait_ge(gut_done, base + (k + 1))
                    dve.wait_ge(k_done, base + (k + 1))
                    reuse(dve, hh_done, base, k)
                    dve.tensor_tensor(hf[0:r, b, :], bank[4 + b][0:r, :], gu_t[0:r, b, :], ALU.mult).then_inc(hf_done, 1)
                    dve.wait_ge(hh_done, base + (k + 1))
                    h = k % CH % H_RING
                    dve.tensor_tensor(hl_[0:r, h, :], hf[0:r, b, :], hh_[0:r, h, :].bitcast(F32),
                                      ALU.subtract).then_inc(hl_done, 1)
                if s >= 1 and not (isinstance(g, int) and g == 0):
                    if s <= GTT:
                        stats(g - 1, s - 1)
                    elif s == GTT + 1:
                        moments(g - 1)
                    elif STD_STEP < s <= STD_STEP + GTT:
                        normalise(g - 1, s - STD_STEP - 1)
                if isinstance(g, int) and g == 0:
                    if s == 0:
                        route_first(1)
                    if s == 2:
                        route_second(1)
                    if s == 4:
                        route_weights(1)
                    if s == 6:
                        route_parts(1)

            def stats(g, i):
                dve.wait_ge(y3_done, g * 2 + 2)
                dve.sem_inc(passed_dve, 1)
                dve.bn_stats(ln_stats[:, i, :], y[:, bass.ds(g * GTT + i, 1), :]).then_inc(stat_done, 1)

            def moments(g):
                dve.wait_ge(stat_done, 2 * NT + g * GTT + GTT)
                dve.sem_inc(passed_dve, 1)
                for i in range(GTT):
                    ins = dve.bn_aggr(mv_tile[:, i, :], ln_stats[:, i, :])
                ins.then_inc(aggr_done, 1)
                dve.wait_ge(aggr_done, B + g + 1)
                dve.tensor_copy(ln_mv[:, bass.ds(g * GTT, GTT), :], mv_tile[:, :, :]).then_inc(mv_done, GTT)

            def normalise(g, i):
                if i == 0:
                    dve.wait_ge(std_done, g + 4)
                    dve.reciprocal(ln_rstd[:, bass.ds(g * GTT, GTT)], ln_std[:, bass.ds(g * GTT, GTT)])\
                        .then_inc(rstd_done, 1)
                    dve.wait_ge(rstd_done, g + 4)
                rows_ = y[:, bass.ds(g * GTT + i, 1), :]
                dve.tensor_scalar(rows_, rows_, ln_mv[:, bass.ds(g * GTT + i, 1), 0],
                                  ln_rstd[:, bass.ds(g * GTT + i, 1)], ALU.subtract, ALU.mult).then_inc(xn_done, 1)

            def add_group(g):
                dve.wait_ge(d_done, g * CH + CH)
                for j in range(2):
                    part = y[:, bass.ds(g * GTT + 2 * j, 2), :]
                    dve.tensor_tensor(part, bank[6 + j][:, :], part, ALU.add).then_inc(y3_done, 1)

            def end(g):
                if isinstance(g, int) and g == GROUPS - 1:
                    for i in range(GTT):
                        stats(g, i)
                    moments(g)
                    for i in range(GTT):
                        normalise(g, i)

            mlp(dve, step, end)

        @block.tensor
        def _(pe):
            pe.sem_inc(pv_done, 8)
            pe.sem_inc(wo_done, 8)

            def three_pass(dst, lh, ll, rh, rl, first, last):
                pe.matmul(dst, lh, rh, start=first, stop=False)
                pe.matmul(dst, ll, rh, start=False, stop=False)
                return pe.matmul(dst, lh, rl, start=False, stop=last)

            def latent_keys():
                for c in range(KC):
                    ins = pe.matmul(bank[2][:, :], wkvc[:, c, :], ctxT[:, c, :], start=c == 0, stop=c == KC - 1)
                ins.then_inc(pre_mm, 1)

            def latent_products(g):
                for h in range(4 * g, 4 * g + 4):
                    ins = pe.matmul(bank[A_BANKS[g]][0:KVC, h % 4 * QC:(h % 4 + 1) * QC], wukT[:, h, :], wuqT[:, h, :],
                                    start=True, stop=True)
                ins.then_inc(pre_mm, 1)

            def step(base, pair, s, lo, hi):
                early = isinstance(base, int) and base == 0
                if early and s == -SC:
                    pe.wait_ge(consts, 2)
                k = s + SC
                if lo <= k < hi:
                    pe.wait_ge(rope_done, base + (k + 1))
                    if not (early and k < 2):
                        pe.wait_ge(exp_done, base + (k - 1))
                    dst, r = bS[k % 2], qkr[:, k % 2, :, :]
                    pe.matmul(dst[:, 0:P], r[:, 0, 0:P], r[:, 1, 0:P], start=True, stop=False)
                    pe.matmul(dst[:, 0:P], identb[:, :], maskb[:, :], start=False, stop=True)
                    pe.matmul(dst[:, P:3 * P], r[:, 0, P:T], r[:, 1, :], start=True, stop=False)
                    pe.matmul(dst[:, 2 * P:3 * P], identb[:, :], maskb[:, :], start=False, stop=True).then_inc(s_done, 1)
                k = s + QK
                if lo <= k < hi:
                    ahead, hh, b = where(k)
                    if early and hh == 0 and ahead == 0:
                        pe.wait_ge(xl_ready, b + 1)
                    if b == 0:
                        pe.wait_ge(wqk_ready, pair * 2 + (2 * ahead + hh + 1))
                    if not (early and k < 2):
                        pe.wait_ge(qkb_done, base + (k - 1))
                    cols = slice(b * T, (b + 1) * T)
                    for j in range(2):
                        dst = bQK[k % 2][:, j * T:(j + 1) * T]
                        for c in range(KC):
                            w = slice(j * HD, (j + 1) * HD)
                            ins = three_pass(dst, wqkh[hh][:, c, w], wqkl[hh][:, c, w], xh[:, c, cols], xl[:, c, cols],
                                             c == 0, c == KC - 1)
                    ins.then_inc(qk_done, 1)
                    if hh == 0:
                        if b == 0:
                            pe.wait_ge(wv_ready, pair + (ahead + 1))
                        if not (early and ahead == 0 and b == 0):
                            pe.wait_ge(vcopy_done, (pair + ahead) * B + b)
                        if s > B - 1:
                            pe.wait_ge(yadd_done, pair * B + (s - B + 2))
                        for i in range(TT):
                            rows = slice(b * T + i * P, b * T + (i + 1) * P)
                            for c in range(KC):
                                ins = three_pass(bVO[:, i * 2 * HD:(i + 1) * 2 * HD], xh[:, c, rows], xl[:, c, rows],
                                                 wvh[:, c, :], wvl[:, c, :], c == 0, c == KC - 1)
                        ins.then_inc(vmm_done, 1)
                k = s + TR
                if lo <= k < hi:
                    pe.wait_ge(norm_done, base + (k + 1))
                    if not (early and k < 1):
                        pe.wait_ge(ptc_done, base + k)
                    for i, q in enumerate((0, 1, 2)):
                        ins = pe.transpose(bT[:, i * P:(i + 1) * P], prob[:, k % 4, q * P:(q + 1) * P], ident[:, :])
                    ins.then_inc(t_done, 1)
                k = s + PV
                if lo <= k < hi:
                    ahead, hh, b = where(k)
                    pe.wait_ge(ptc_done, base + (k + 1))
                    if hh == 0:
                        pe.wait_ge(vcopy_done, (pair + ahead) * B + (b + 1))
                    if not (early and k < 2):
                        pe.wait_ge(zl_done, base + (k - 1))
                    dst, w = bZ[k % 2][:, 0:T], slice(hh * HD, (hh + 1) * HD)
                    pe.matmul(dst, V[:, b, 0, w], probT[:, k % 2, 0:2 * P], start=True, stop=False)
                    pe.matmul(dst[:, P:T], V[:, b, 1, w], probT[:, k % 2, 2 * P:3 * P], start=False,
                              stop=True).then_inc(pv_done, 1)
                k = s + WO
                if lo <= k < hi and where(k)[1] == 1:
                    b = where(k)[2]
                    pe.wait_ge(zl_done, base + (k + 1))
                    if b == 0:
                        pe.wait_ge(wo_ready, pair + 1)
                    pe.wait_ge(yadd_done, pair * B + (b + 1))
                    pe.wait_ge(vcopy_done, pair * B + (B + (s - B + 1 if s >= B and hi > UNITS else 0)))
                    for i in range(TT):
                        rows = slice(i * P, (i + 1) * P)
                        for hh in range(2):
                            ins = three_pass(bVO[:, i * D:(i + 1) * D], zh[:, hh, b, rows], zl[:, hh, b, rows],
                                             woh[:, hh, :], wol[:, hh, :], hh == 0, hh == 1)
                    ins.then_inc(wo_done, 1)
                if not early and hi == UNITS and s >= UNITS - 4:
                    if s == UNITS - 4:
                        pe.wait_ge(xw_in, 16 * len(XW))
                        pe.wait_ge(exp_done, PAIRS * UNITS)
                        latent_keys()
                    else:
                        latent_products(s - (UNITS - 3))

            attention(pe, step)

            phase_one_over(pe)
            pe.wait_ge(zl_done, PAIRS * UNITS)
            latent_products(3)
            pe.wait_ge(pre_cp, 1)
            for j in range(2):
                pe.matmul(bank[(5, 7)[j]][:, :], wkr[:, j, :], kvc[0:KVC, :], start=True, stop=True).then_inc(kr_mm, 1)
            for g in range(4):
                pe.wait_ge(at_lo, g + 1)
                if g == 3:
                    pe.wait_ge(kr_mul, 1)
                for h in range(4 * g, 4 * g + 4):
                    ins = pe.matmul(bank[M_BANKS[g]][h % 2 * 64:h % 2 * 64 + 64, h // 2 % 2 * D:(h // 2 % 2 + 1) * D],
                                    wuvT[:, h, :], wox[:, h, :], start=True, stop=True)
                ins.then_inc(pre_mm, 1)

            def key_space(h):
                if h == 0:
                    pe.wait_ge(at_lo, 5)
                if h == 1:
                    pe.wait_ge(ml_done, 1)
                if h == 2:
                    pe.wait_ge(ml_done, 4)
                if h >= 3:
                    pe.wait_ge(kp_lo, h - 2)
                dst = bank[KP_BANKS[h % 3]][0:QC, :]
                pe.matmul(dst, AT[:, h, :], kvch[:, :], start=True, stop=False)
                pe.matmul(dst, AT[0:KVC, h, :], kvcl[0:KVC, :], start=False, stop=True).then_inc(pre_mm, 1)

            def latent(b):
                for c in range(KC):
                    ins = three_pass(bank[4][0:QC, 0:T], wdqh[:, c, :], wdql[:, c, :], xh[:, c, bass.ds(b * T, T)],
                                     xl[:, c, bass.ds(b * T, T)], c == 0, c == KC - 1)
                ins.then_inc(a_done, 1)

            def rotary(b, lo, hi):
                for i in range(lo, hi):
                    for j in range(2):
                        ins = three_pass(bank[ROT_BANKS[i]][:, j * T:(j + 1) * T], wqrh[:, 2 * i + j, :],
                                         wqrl[:, 2 * i + j, :], qch[:, :], qcl[:, :], True, True)
                    ins.then_inc(qr_mm, 1)

            def scores(b, j):
                rows = slice(j * P, (j + 1) * P)
                for half in range(2):
                    if j == 0:
                        pe.wait_ge(qr_ready, b * ROTS + (2 * half + 2))
                    if half == 0 and j == 1:
                        pe.wait_ge(y2_done, 2 * b + 1)
                    dst = bank[2 * j + half]
                    keys = (slice(None), bass.ds(b, 1), slice(8 * half, 8 * half + 8), slice(None))
                    for n, (q, k) in enumerate(((qch, KPh), (qcl, KPh), (qch, KPl))):
                        pe.matmul(dst[:, :], q[:, rows], k[keys], start=n == 0, stop=False)
                    pe.wait_ge(rb_done, b + 1)
                    for i in range(4):
                        ins = pe.matmul(dst[:, i * P:(i + 1) * P], qrT[:, 4 * half + i, rows], RB[:, :],
                                        start=False, stop=i == 3)
                ins.then_inc(c_done, 1)

            def transpose(b, j):
                pe.wait_ge(xp_ready, 2 * b + (j + 1))
                for half in range(2):
                    if j == 0:
                        pe.wait_ge(vo_cp, 4 * b + (2 + half))
                    else:
                        pe.wait_ge(pt_cp, 4 * b + (half + 3))
                    for i in range(4):
                        src = xs[:, j, 8 * half + 2 * i:8 * half + 2 * i + 2, :].rearrange("p h k -> p (h k)")
                        ins = pe.transpose(bank[6 + half][:, i * P:(i + 1) * P], src, ident[:, :])
                    ins.then_inc(e_done, 1)

            def output(b, j):
                pe.wait_ge(vo_cp, 4 * b + 4)
                for i in range(PAIRS):
                    if i % 4 == 0:
                        pe.wait_ge(pt_cp, 4 * b + (2 * j + 3 + i // 4))
                    ins = pe.matmul(bank[F_BANKS[j]][:, 0:D], xpT[:, j, i, :], VO[:, i, :], start=i == 0,
                                    stop=i == PAIRS - 1)
                ins.then_inc(f_done, 1)

            def weighted(b, lo, hi):
                for e in range(lo, hi):
                    if e == 1:
                        pe.wait_ge(y2_done, 2 * b + 2)
                    if e == 3:
                        pe.wait_ge(xs_done, 4 * b + 2)
                    for i in range(2):
                        ins = three_pass(bank[VO_BANKS[e]][:, i * D:(i + 1) * D], BDh[:, :], BDl[:, :],
                                         Mh[:, 2 * e + i, :], Ml[:, 2 * e + i, :], True, True)
                    ins.then_inc(vo_mm, 1)

            def first_norm(g):
                if g == 1:
                    pe.wait_ge(kr_mul, 2)
                ln_pe_transpose(pe, 0, g, g + 1)

            def first_latent():
                pe.wait_ge(wdql_done, 1)
                pe.wait_ge(xtl_done, 1)
                latent(0)

            def first_rotary(i):
                if i == 3:
                    pe.wait_ge(kp_lo, H)
                if i == 0:
                    pe.wait_ge(qcl_done, 1)
                    pe.wait_ge(wqrl_done, 1)
                rotary(0, i, i + 1)

            def prologue():
                cross_prologue(first_norm, first_latent, key_space, lambda: None, first_rotary)
                pe.sem_inc(pt_cp, 2)
                pe.wait_ge(kp_lo, H)
                pe.wait_ge(xtl_done, B)
                scores(0, 0)
                scores(0, 1)

            def body(b, more):
                if more:
                    latent(b + 1)
                pe.wait_ge(bd_ready, b + 1)
                weighted(b, 0, 2)
                if more:
                    pe.wait_ge(qcl_done, b + 2)
                    pe.wait_ge(xs_done, 4 * b + 4)
                    rotary(b + 1, 0, 2)
                weighted(b, 2, 4)
                if more:
                    rotary(b + 1, 2, 3)
                transpose(b, 0)
                if more:
                    rotary(b + 1, 3, ROTS)
                output(b, 0)
                transpose(b, 1)
                if more:
                    scores(b + 1, 0)
                else:
                    ln_pe_transpose(pe, 1, 0, 2)
                output(b, 1)
                if more:
                    scores(b + 1, 1)

            cross(pe, prologue, body)

            pe.wait_ge(y2_done, NT + 2)
            def logits(g):
                pe.wait_ge(xtl_done, B + 2 * g + 2)
                if g >= 2:
                    pe.wait_ge(lgT_cp, g - 1)
                cols = slice(g * GT, (g + 1) * GT)
                for c in range(KC):
                    ins = three_pass(bank[LGT_BANKS[g % 2]][0:RW, :], rwh[:, c, :], rwl[:, c, :], xh[:, c, cols],
                                     xl[:, c, cols], c == 0, c == KC - 1)
                ins.then_inc(lgT_mm, 1)

            def turn(g):
                pe.wait_ge(lgT_cp, g + 1)
                for i in range(GTT * g, GTT * g + GTT):
                    ins = pe.transpose(bank[LG_BANKS[i // HT]][:, i % HT * RW:(i % HT + 1) * RW],
                                       lgT[:, i * P:(i + 1) * P], ident[0:RW, 0:RW])
                ins.then_inc(lg_mm, 1)

            pe.wait_ge(rwl_done, 1)
            second_norm(lambda g: ln_pe_transpose(pe, 1, g, g + 1), logits, turn, lambda part: None)

            def combined(part, dst):
                pe.wait_ge(r_step, (part + 1) * R_STEPS)
                for n in range(HT):
                    ins = pe.transpose(dst.bitcast(BF16)[0:3 * GATES, n * P:(n + 1) * P],
                                       cpart[:, part * HT + n, :, :].rearrange("p a e -> p (a e)"), identb[:, :])
                ins.then_inc(comb_mm, 1)

            def step(base, g, s, lo, hi):
                k = s + UP
                if lo <= k < hi:
                    c, b, r = k % CH, k % CH % 2, rows(k)
                    cols = bass.ds((g + k // CH) * GT, GT)
                    first = isinstance(base, int) and base + k == 0
                    second = isinstance(base, int) and base + k == COMBINE
                    if second:
                        reuse(pe, hf_done, base, k)
                        combined(1, bank[4 + b])
                    pe.wait_ge(wg_ready, c + 1)
                    for j, used in ((0, silu_done), (1, gut_done)):
                        reuse(pe, used, base, k)
                        for kc in range(KC):
                            ins = three_pass(bank[2 * j + b][0:P, :], guh[:, c, j, kc, 0:P], gul[:, c, j, kc, 0:P],
                                             xh[:, kc, cols], xl[:, kc, cols], kc == 0, kc == KC - 1)
                        ins.then_inc((g_done, u_done)[j], 1)
                    if first:
                        combined(0, bank[LG_BANKS[0]])
                        pe.wait_ge(lg_cp, 2)
                        pe.wait_ge(sel_done, 1)
                    if first or second:
                        pe.wait_ge(comb_cp, 1 if first else 2)
                    reuse(pe, hf_done, base, k)
                    pe.sem_inc(passed_pe, 1)
                    pe.matmul(bank[4 + b][:, :], sel[:, c * P:(c + 1) * P], combT[:, cols], start=True, stop=True)\
                        .then_inc(k_done, 1)
                k = s
                if lo <= k < hi:
                    h, r = k % H_RING, rows(k)
                    pe.wait_ge(hl_done, base + (k + 1))
                    if k == 0 and not (isinstance(g, int) and g == 0):
                        pe.wait_ge(y3_done, g * 2)
                    for i in range(GTT):
                        rs = slice(i * P, (i + 1) * P)
                        dst = bank[6 + i // 2][:, i % 2 * D:(i % 2 + 1) * D]
                        for n, (l, w) in enumerate(((hh_, dnh), (hl_, dnh), (hh_, dnl))):
                            ins = pe.matmul(dst, l[0:r, h, rs], w[0:r, k, :], start=k == 0 and n == 0 and i % 2 == 0,
                                            stop=k == CH - 1 and n == 2, skip_group_check=True)
                    ins.then_inc(d_done, 1)

            mlp(pe, step, lambda g: None)


def rope_tables():
    inv = (1.0 / np.float32(10000.0) ** (np.arange(0, HD, 2, dtype=np.float32) / HD)).astype(np.float32)
    ang = np.outer(np.arange(T, dtype=np.float32), inv).T
    scale = np.float32(HD ** -0.5)
    cos, sin = np.cos(ang), np.sin(ang)
    cos = np.concatenate([cos, cos])
    sin = np.concatenate([sin, -sin])
    return [np.ascontiguousarray(np.stack([a * scale, a], axis=1).astype(np.float32)) for a in (cos, sin)]


def layout(inp):
    n = {k: np.asarray(v) for k, v in inp.items()}
    x = n["x"]
    perm = np.concatenate([np.arange(0, HD, 2), np.arange(1, HD, 2)])
    a = {}
    a["xT"] = x.reshape(B * T, KC, P).transpose(2, 1, 0)
    a["x"] = x.reshape(NT, P, D).transpose(1, 0, 2)
    wq = n["L0_attn_W_Q"][:, :, perm].reshape(H, KC, P, HD)
    wk = n["L0_attn_W_K"][:, :, perm].reshape(H, KC, P, HD)
    a["wqk"] = np.concatenate([wq, wk], axis=3).transpose(0, 2, 1, 3)
    wv = n["L0_attn_W_V"].reshape(PAIRS, 2, KC, P, HD)
    a["wv"] = wv.transpose(0, 3, 2, 1, 4).reshape(PAIRS, P, KC, 2 * HD)
    a["wo"] = n["L0_attn_W_O"].reshape(PAIRS, 2, HD, D).transpose(0, 2, 1, 3)
    a["bqk"] = np.stack([n["L0_attn_b_Q"][:, perm], n["L0_attn_b_K"][:, perm]], axis=1).reshape(2 * H, HD).T
    a["bv"] = n["L0_attn_b_V"].T
    a["bo"] = np.broadcast_to(n["L0_attn_b_O"], (P, D))
    a["cos"], a["sin"] = rope_tables()
    gate = np.concatenate([n["L0_ffn_w_gate"].transpose(1, 0, 2).reshape(D, E * I), n["L0_ffn_sw_gate"]], axis=1)
    up = np.concatenate([n["L0_ffn_w_up"].transpose(1, 0, 2).reshape(D, E * I), n["L0_ffn_sw_up"]], axis=1)
    down = np.concatenate([n["L0_ffn_w_down"].reshape(E * I, D), n["L0_ffn_sw_down"]], axis=0)
    pad = CH * P - (E * I + SI)
    gu = np.pad(np.stack([gate, up]), ((0, 0), (0, 0), (0, pad)))
    a["wgu"] = gu.reshape(2, KC, P, CH, P).transpose(3, 2, 0, 1, 4)
    a["wdn"] = np.pad(down, ((0, pad), (0, 0))).reshape(CH, P, D)
    rw = np.concatenate([n["L0_ffn_router_w"].T, n["L0_ffn_shared_gate_w"][:, None]], axis=1)
    a["rw"] = np.pad(rw, ((0, 0), (0, RW - GATES))).reshape(KC, P, RW).transpose(1, 0, 2)
    expert = np.minimum(np.arange(CH * P) // I, E)
    a["sel"] = np.tile((expert[None, :] == np.arange(GATES)[:, None]).astype(np.float32), (3, 1))
    a["enum"] = np.broadcast_to(np.arange(E, dtype=np.float32), (P, E))
    swap = np.concatenate([np.arange(R // 2, R), np.arange(0, R // 2)])
    twice = lambda w, axis=-1: np.concatenate([w, w], axis=axis)
    a["wukT"] = n["L0_xattn_W_uk"].reshape(KVC, H, HD).transpose(2, 1, 0)
    a["wuqT"] = n["L0_xattn_W_uq"].reshape(QC, H, HD).transpose(2, 1, 0)
    a["wuvT"] = n["L0_xattn_W_uv"].reshape(KVC, H, HD).transpose(2, 1, 0)
    a["wox"] = n["L0_xattn_W_o"].reshape(H, HD, D).transpose(1, 0, 2)
    a["ctxT"] = n["ctx_2048"].reshape(B * KT, KC, P).transpose(2, 1, 0)
    a["wkvc"] = twice(n["L0_xattn_W_kvc"].reshape(KC, P, KVC).transpose(1, 0, 2))
    wkr = n["L0_xattn_W_kr"]
    halves = np.concatenate([np.arange(R // 2), np.arange(R // 2), np.arange(R // 2, R), np.arange(R // 2, R)])
    a["wkr"] = np.stack([wkr[:, halves], wkr[:, swap][:, halves]], axis=1)
    a["wdq"] = n["L0_xattn_W_dq"].reshape(KC, P, QC).transpose(1, 0, 2)
    wqr = n["L0_xattn_W_qr"].reshape(QC, PAIRS, 2, 2, R // 2)
    a["wqr"] = wqr.transpose(0, 1, 3, 2, 4).reshape(QC, PAIRS, 2 * R)
    a["seg"] = n["itok_BxS_0_1023"].reshape(NT, P).T
    a["keys"] = np.broadcast_to(np.arange(KT, dtype=np.float32), (P, KT))
    for name, count in (("K", KT), ("Q", T)):
        half = R // 2
        inv = (1.0 / np.float32(10000.0) ** (np.arange(half, dtype=np.float32) / half)).astype(np.float32)
        ang = (np.arange(count, dtype=np.float32)[:, None] * inv).T
        a["xcos" + name] = np.tile(np.cos(ang), (4, 1)).astype(np.float32)
        sin = np.tile(np.sin(ang), (2, 1)).astype(np.float32)
        a["xsin" + name] = np.concatenate([-sin, sin])
    a["ident"] = np.eye(P, dtype=np.float32)
    q = np.arange(P)
    a["mask"] = np.where(q[None, :] > q[:, None], np.float32(NEG), np.float32(0))
    return {k: np.ascontiguousarray(v) for k, v in a.items()}


def program(nc, arrays):
    t = {k: nc.dram_tensor("in_" + k, v.shape, mybir.dt.from_np(v.dtype), kind="ExternalInput").ap()
         for k, v in arrays.items()}
    out = nc.dram_tensor("out", (B * T, D), F32, kind="ExternalOutput").ap()
    build(nc, t, out.rearrange("(n p) d -> p n d", p=P))


def kernel(**inputs):
    import concourse.bacc as bacc
    from concourse.bass_utils import run_bass_kernel_spmd
    arrays = layout(inputs)
    nc = bacc.Bacc("TRN2", target_bir_lowering=False, num_devices=1)
    program(nc, arrays)
    r = run_bass_kernel_spmd(nc, [{"in_" + k: v for k, v in arrays.items()}], core_ids=[0])
    return r.results[0]["out"].reshape(B, T, D)
```
